# Optimizing a Trainium2 kernel written in Bass

```python
import numpy as np
import jax
import jax.numpy as jnp

def _softmax(x, axis=-1):
    return jax.nn.softmax(x, axis=axis)

def _gelu(x):
    return jax.nn.gelu(x, approximate=True)

def _silu(x):
    return jax.nn.silu(x)

def _sigmoid(x):
    return jax.nn.sigmoid(x)

def _layernorm(x, axis=-1, eps=1e-05):
    m = jnp.mean(x, axis=axis, keepdims=True)
    v = jnp.var(x, axis=axis, keepdims=True)
    return (x - m) / jnp.sqrt(v + eps)

def _scatter_add(tgt, idx, src, axis=0):
    return tgt.at[idx].add(src)

def _segment_sum(src, seg, n):
    return jax.ops.segment_sum(src, seg, n)
kernel_name = 'mk_macaron_d1_jaxref_r4_48480c'

def setup_inputs(seed: int=0):
    np.random.seed(seed)
    _w = jnp.asarray

    def _L0_attn_setup():
        import jax, jax.numpy as jnp
        import numpy as np
        D_IN = 512
        D_OUT = 512
        DL = 128
        NUM_HEAD = 16
        CTX = 512
        HEAD_DIM = D_OUT // NUM_HEAD
        key = jax.random.key(seed)
        ks = jax.random.split(key, 20)
        s = 0.02

        def lin(k, din, dout):
            k1, k2 = jax.random.split(k)
            return (jax.random.normal(k1, (din, dout), jnp.float32) * s, jax.random.normal(k2, (dout,), jnp.float32) * s)
        w_kv, b_kv = lin(ks[0], D_IN, DL)
        w_ku, b_ku = lin(ks[1], DL, D_OUT // 2)
        w_kr, b_kr = lin(ks[2], D_IN, D_OUT // 2)
        w_vu, b_vu = lin(ks[3], DL, D_OUT)
        w_q, b_q = lin(ks[4], D_IN, DL)
        w_qu, b_qu = lin(ks[5], DL, D_OUT // 2)
        w_qr, b_qr = lin(ks[6], DL, D_OUT // 2)
        w_o, b_o = lin(ks[7], D_OUT, D_OUT)
        x = jax.random.normal(ks[8], (2, 512, D_IN), jnp.float32)
        return dict(x=x, w_kv=w_kv, b_kv=b_kv, w_ku=w_ku, b_ku=b_ku, w_kr=w_kr, b_kr=b_kr, w_vu=w_vu, b_vu=b_vu, w_q=w_q, b_q=b_q, w_qu=w_qu, b_qu=b_qu, w_qr=w_qr, b_qr=b_qr, w_o=w_o, b_o=b_o)
    _L0_attn_in = _L0_attn_setup()

    def _L0_ffn_setup():
        import jax, jax.numpy as jnp
        import numpy as np
        TARGET_SPARSITY = 0.9
        LN_EPS = 1e-05

        def ternary_quant(W):
            scale = jnp.mean(jnp.abs(W))
            q = jnp.clip(jnp.round(W / (scale + 1e-08)), -1.0, 1.0) * scale
            return W + jax.lax.stop_gradient(q - W)

        def layernorm(x, gamma, beta):
            mu = jnp.mean(x, axis=-1, keepdims=True)
            var = jnp.var(x, axis=-1, keepdims=True)
            return (x - mu) * jax.lax.rsqrt(var + LN_EPS) * gamma + beta
        key = jax.random.key(seed)
        ks = jax.random.split(key, 3)
        B, S, D, N = (4, 512, 512, 2048)
        x = jax.random.normal(ks[0], (B, S, D), dtype=jnp.float32)
        W_syn = jax.random.normal(ks[1], (N, D), dtype=jnp.float32) * (1.0 / np.sqrt(D))
        b_syn = jnp.zeros((N,), dtype=jnp.float32)
        W_out = jax.random.normal(ks[2], (D, N), dtype=jnp.float32) * (1.0 / np.sqrt(N))
        b_out = jnp.zeros((D,), dtype=jnp.float32)
        gamma = jnp.ones((D,), dtype=jnp.float32)
        beta = jnp.zeros((D,), dtype=jnp.float32)
        return {'x': x, 'W_syn': W_syn, 'b_syn': b_syn, 'W_out': W_out, 'b_out': b_out, 'gamma': gamma, 'beta': beta}
    _L0_ffn_in = _L0_ffn_setup()
    _d = {'L0_attn_x': _L0_attn_in['x'], 'L0_attn_w_kv': _L0_attn_in['w_kv'], 'L0_attn_b_kv': _L0_attn_in['b_kv'], 'L0_attn_w_ku': _L0_attn_in['w_ku'], 'L0_attn_b_ku': _L0_attn_in['b_ku'], 'L0_attn_w_kr': _L0_attn_in['w_kr'], 'L0_attn_b_kr': _L0_attn_in['b_kr'], 'L0_attn_w_vu': _L0_attn_in['w_vu'], 'L0_attn_b_vu': _L0_attn_in['b_vu'], 'L0_attn_w_q': _L0_attn_in['w_q'], 'L0_attn_b_q': _L0_attn_in['b_q'], 'L0_attn_w_qu': _L0_attn_in['w_qu'], 'L0_attn_b_qu': _L0_attn_in['b_qu'], 'L0_attn_w_qr': _L0_attn_in['w_qr'], 'L0_attn_b_qr': _L0_attn_in['b_qr'], 'L0_attn_w_o': _L0_attn_in['w_o'], 'L0_attn_b_o': _L0_attn_in['b_o'], 'L0_ffn_W_syn': _L0_ffn_in['W_syn'], 'L0_ffn_b_syn': _L0_ffn_in['b_syn'], 'L0_ffn_W_out': _L0_ffn_in['W_out'], 'L0_ffn_b_out': _L0_ffn_in['b_out'], 'L0_ffn_gamma': _L0_ffn_in['gamma'], 'L0_ffn_beta': _L0_ffn_in['beta']}
    _x0 = _d['L0_attn_x']
    _d['L0_attn_x'] = jax.random.normal(jax.random.fold_in(jax.random.key(seed), 1), (2, 1024, 512), dtype=_x0.dtype)
    del _x0
    return _d

def reference(L0_attn_x, L0_attn_w_kv, L0_attn_b_kv, L0_attn_w_ku, L0_attn_b_ku, L0_attn_w_kr, L0_attn_b_kr, L0_attn_w_vu, L0_attn_b_vu, L0_attn_w_q, L0_attn_b_q, L0_attn_w_qu, L0_attn_b_qu, L0_attn_w_qr, L0_attn_b_qr, L0_attn_w_o, L0_attn_b_o, L0_ffn_W_syn, L0_ffn_b_syn, L0_ffn_W_out, L0_ffn_b_out, L0_ffn_gamma, L0_ffn_beta):

    def _L0_attn_ref(x, w_kv, b_kv, w_ku, b_ku, w_kr, b_kr, w_vu, b_vu, w_q, b_q, w_qu, b_qu, w_qr, b_qr, w_o, b_o):
        import jax, jax.numpy as jnp
        import numpy as np
        D_IN = 512
        D_OUT = 512
        DL = 128
        NUM_HEAD = 16
        CTX = 512
        HEAD_DIM = D_OUT // NUM_HEAD
        b, s, _ = x.shape
        ckv = x @ w_kv + b_kv
        key = jnp.concatenate([ckv @ w_ku + b_ku, x @ w_kr + b_kr], axis=-1)
        q_lat = x @ w_q + b_q
        query = jnp.concatenate([q_lat @ w_qu + b_qu, q_lat @ w_qr + b_qr], axis=-1)
        value = ckv @ w_vu + b_vu

        def heads(t):
            return t.reshape(b, s, NUM_HEAD, HEAD_DIM).transpose(0, 2, 1, 3)
        q, k, v = (heads(query), heads(key), heads(value))
        scores = jnp.einsum('bhqd,bhkd->bhqk', q, k)
        causal = jnp.tril(jnp.ones((s, s), dtype=bool))
        scores = jnp.where(causal, scores, -jnp.inf)
        at = jax.nn.softmax(scores / jnp.sqrt(jnp.float32(HEAD_DIM)), axis=-1)
        out = jnp.einsum('bhqk,bhkd->bhqd', at, v).transpose(0, 2, 1, 3).reshape(b, s, D_OUT)
        return out @ w_o + b_o

    def _L0_ffn_ref(x, W_syn, b_syn, W_out, b_out, gamma, beta):
        import jax, jax.numpy as jnp
        import numpy as np
        TARGET_SPARSITY = 0.9
        LN_EPS = 1e-05

        def ternary_quant(W):
            scale = jnp.mean(jnp.abs(W))
            q = jnp.clip(jnp.round(W / (scale + 1e-08)), -1.0, 1.0) * scale
            return W + jax.lax.stop_gradient(q - W)

        def layernorm(x, gamma, beta):
            mu = jnp.mean(x, axis=-1, keepdims=True)
            var = jnp.var(x, axis=-1, keepdims=True)
            return (x - mu) * jax.lax.rsqrt(var + LN_EPS) * gamma + beta
        B, S, D = x.shape
        N = W_syn.shape[0]
        x_flat = x.reshape(-1, D)
        z = x_flat @ ternary_quant(W_syn).T + b_syn
        k = max(1, int(N * (1.0 - TARGET_SPARSITY)))
        topv, _ = jax.lax.top_k(z, k)
        thresh = topv[:, -1:]
        hidden = jnp.where(z >= thresh, jax.nn.relu(z), 0.0)
        out = hidden @ ternary_quant(W_out).T + b_out
        out = out.reshape(B, S, D)
        return layernorm(x + out, gamma, beta)
    x = L0_attn_x
    x = x + 0.5 * _L0_ffn_ref(_layernorm(x, axis=-1), L0_ffn_W_syn, L0_ffn_b_syn, L0_ffn_W_out, L0_ffn_b_out, L0_ffn_gamma, L0_ffn_beta)
    x = x + _L0_attn_ref(_layernorm(x, axis=-1), L0_attn_w_kv, L0_attn_b_kv, L0_attn_w_ku, L0_attn_b_ku, L0_attn_w_kr, L0_attn_b_kr, L0_attn_w_vu, L0_attn_b_vu, L0_attn_w_q, L0_attn_b_q, L0_attn_w_qu, L0_attn_b_qu, L0_attn_w_qr, L0_attn_b_qr, L0_attn_w_o, L0_attn_b_o)
    x = x + 0.5 * _L0_ffn_ref(_layernorm(x, axis=-1), L0_ffn_W_syn, L0_ffn_b_syn, L0_ffn_W_out, L0_ffn_b_out, L0_ffn_gamma, L0_ffn_beta)
    return x

_drawn_inputs = setup_inputs


def setup_inputs(seed=0):
    import zlib

    import numpy as np

    out = dict(_drawn_inputs(seed))
    spreads = {'L0_ffn_b_syn': (0.0, 0.1),
     'L0_ffn_b_out': (0.0, 0.1),
     'L0_ffn_gamma': (1.0, 0.2),
     'L0_ffn_beta': (0.0, 0.1)}
    factors = {'L0_attn_w_kv': 8.0,
     'L0_attn_b_kv': 8.0,
     'L0_attn_w_ku': 8.0,
     'L0_attn_b_ku': 64.0,
     'L0_attn_w_kr': 8.0,
     'L0_attn_b_kr': 64.0,
     'L0_attn_w_vu': 8.0,
     'L0_attn_b_vu': 8.0,
     'L0_attn_w_q': 8.0,
     'L0_attn_b_q': 8.0,
     'L0_attn_w_qu': 8.0,
     'L0_attn_b_qu': 8.0,
     'L0_attn_w_qr': 8.0,
     'L0_attn_b_qr': 8.0,
     'L0_attn_w_o': 7.225,
     'L0_attn_b_o': 31.056}
    for name, (base, spread) in spreads.items():
        noise = np.random.default_rng([zlib.crc32(name.encode()), seed]).standard_normal(out[name].shape)
        drawn = base * np.exp(spread * noise) if base else spread * noise
        out[name] = jnp.asarray(drawn.astype(out[name].dtype))
    for name, factor in factors.items():
        out[name] = (out[name] * factor).astype(out[name].dtype)
    return out
```

```python
import concourse.bass as bass
from concourse import mybir
from contextlib import ExitStack

F32 = mybir.dt.float32
F16 = mybir.dt.float16
BF16 = mybir.dt.bfloat16
I32 = mybir.dt.int32
I8 = mybir.dt.int8
ALU = mybir.AluOpType
ACT = mybir.ActivationFunctionType
AX = mybir.AxisListType

P = 128
TOKENS, D, N = 2048, 512, 2048
NT = TOKENS // P
KD = D // P
KN = N // P
CH = 4
CW = N // CH
TOPK = int(N * (1.0 - 0.9))
EPS = 1e-5

NC = 5
TARGET = TOPK - 4.5
SSTAR = 2 * TARGET - N
BIG = 1e30
S_SEL, S_OUT, S_FIN = 2 + NC, 3 + NC, 4 + NC
ZR = 8
XR = 11
XSCALE = 256.0
HTOP = 16384.0
NF = 2

HEADS, HD = 16, 32
SEQ = 1024
BT = SEQ // P
HG = 4
GROUPS = HEADS // HG
MUNIT = 64.0
MASK = 32768.0
ATT_SCALE = 1.0 / HD ** 0.5


def group_order(first, second):
    rows = []
    if first is not None:
        rows = [("row", first, h, t, c) for t in range(BT) for h in range(HG) for c in range(t // 4 + 1)]
    cols = []
    if second is not None:
        for qc in range(2):
            last = None
            for kb in range(4 * qc + 4):
                cols.append([("col", second, qc, kb, h) for h in range(HG)])
                if last is not None:
                    cols[-1].append(("mix", second, qc, last))
                last = kb
            cols[-1].append(("mix", second, qc, last))
            cols[-1].append(("norm", second, qc))
    order = []
    parts = max(1, int(0.75 * len(cols)))
    done = 0
    if not cols:
        order = rows
        done = len(rows)
    for n, col in enumerate(cols):
        upto = min(len(rows), -(-len(rows) * (n + 1) // parts))
        new = rows[done:upto]
        done = upto
        for j in range(max(len(new), len(col))):
            order += new[j:j + 1] + col[j:j + 1]
        if rows and done == len(rows) and new:
            order.append(("max", first))
    if rows and not cols:
        order.append(("max", first))
    return order


def core_order():
    order = group_order(0, None)
    for g in range(GROUPS):
        order += group_order(g + 1 if g + 1 < GROUPS else None, g)
    return order


def program(nc, x, w_synT, b_syn, w_outT, b_out, gamma, beta, w_kv, w_q, w_kr, w_ku, w_qu, w_qr, w_vu, w_o, b_cols,
            b_o, out):
    ctx = ExitStack()
    with ctx:
        def sb(name, shape, dt):
            return ctx.enter_context(nc.sbuf_tensor(name, shape, dt))

        def pb(name, shape, dt):
            return ctx.enter_context(nc.psum_tensor(name, shape, dt))

        def sem(name):
            return ctx.enter_context(nc.semaphore(name))

        x_sb = sb("x_sb", [P, NT, D], F32)
        T1 = sb("T1", [P, KD, N], F16)
        T2 = sb("T2", [P, KN, D], F16)
        bsyn = sb("bsyn", [P, N], F32)
        bout = sb("bout", [P, D], F32)
        gam = sb("gam", [P, D], F32)
        bet = sb("bet", [P, D], F32)
        identf = sb("identf", [P, P], F32)
        onesf = sb("onesf", [P, P], F32)
        iota8 = sb("iota8", [P, 8], F32)
        nhalf = sb("nhalf", [P, 1], F32)
        half = sb("half", [P, 1], F32)
        ARENA = (4 * ZR * N + 4 * N + 2 * 2 * N + 2 * 2 * KN * P + 2 * 2 * 2 * KD * P + 4 * 2 * D + 4 * XR * D
                 + 2 * 4 * 2 * D) // 4
        arena = sb("arena", [P, ARENA], F32)
        taken = [0]

        def carve(words, dt=F32):
            a = arena[:, taken[0]:taken[0] + words]
            taken[0] += words
            assert taken[0] <= ARENA
            return a if dt == F32 else a.bitcast(dt)

        Z = carve(ZR * N).rearrange("p (z n) -> p z n", z=ZR)
        M = carve(N)
        junk = carve(N // 2, I8).rearrange("p (b n) -> p b n", b=2)
        hThi = carve(KN * P // 2, F16).rearrange("p (k t) -> p k t", k=KN)
        hTlo = carve(KN * P // 2, F16).rearrange("p (k t) -> p k t", k=KN)
        xThi = carve(KD * P, F16).rearrange("p (b k t) -> p b k t", b=2, k=KD)
        xTlo = carve(KD * P, F16).rearrange("p (b k t) -> p b k t", b=2, k=KD)
        xn = carve(2 * D).rearrange("p (b d) -> p b d", b=2)
        xb = carve(XR * D).rearrange("p (b d) -> p b d", b=XR)
        y = carve(2 * D).rearrange("p (b d) -> p b d", b=2)
        yt = carve(2 * D).rearrange("p (b d) -> p b d", b=2)

        G = carve(4 * NC).rearrange("p (g k) -> p g k", g=4)
        Y4 = carve(4 * NC).rearrange("p (g k) -> p g k", g=4)
        W2 = carve(2 * NC).rearrange("p (g k) -> p g k", g=2)
        E2 = carve(3 * NC).rearrange("p (g k) -> p g k", g=3)
        flags, flagsT = carve(32), carve(32)

        taken[0] = 0
        xnT = carve(KD * SEQ).rearrange("p (k t) -> p k t", k=KD)
        attT = xnT
        w_in = carve(KD * D).rearrange("p (k n) -> p k n", k=KD)
        wo_sb = w_in
        PT = carve(2 * HG * 512).rearrange("p (b h q) -> p b h q", b=2, h=HG)
        lat = PT.rearrange("p b h q -> p (b h q)")[:, 0:2 * SEQ].rearrange("p (l t) -> p l t", l=2)
        qk_at = taken[0]
        qk = carve(2 * KD * SEQ).rearrange("p (w k t) -> p w k t", w=2, k=KD)
        taken[0] = qk_at
        stack = carve(2 * 2 * HG * SEQ // 2, F16).rearrange("p (b w h t) -> p b w h t", b=2, w=2, h=HG)
        taken[0] = qk_at + 2 * KD * SEQ
        parts = carve(2 * 2 * KD * SEQ // 2, F16).rearrange("p (w l k t) -> p w l k t", w=2, l=2, k=KD)
        V = carve(BT * D).rearrange("p (t n) -> p t n", t=BT)
        axn = arena[:, qk_at + 2 * KD * SEQ:qk_at + 2 * KD * SEQ + 2 * D].rearrange(
            "p (b d) -> p b d", b=2)
        tail = taken[0]
        w_lat = carve(5 * 256).rearrange("p (k n) -> p k n", k=5)
        taken[0] = tail
        rec = carve(512)
        mrows = carve(SEQ // 2, F16)[0:2 * HG, :]
        bo = carve(D)
        flagi = sb("flagi", [P, 1], I32)
        bcols = sb("bcols", [P, 14], F32)
        ident16 = sb("ident16", [P, P], F16)
        identm = sb("identm", [P, P], F16)
        maskq = sb("maskq", [P, P], F16)
        maskk = sb("maskk", [P, P], F16)
        mx = sb("mx", [P, HG, BT, 2], F32)
        mm_ = sb("mm_", [P, HG * BT], F32)
        mrow = sb("mrow", [P, BT, HG, 2], F16)
        aln = sb("aln", [P, 2, 4], F32)
        mxq = sb("mxq", [P, 2, 8], F32)
        asc = sb("asc", [P, 16], F32)
        st6 = sb("st6", [P, 24], F32)
        ln1 = sb("ln1", [P, 2, 4], F32)
        ln2 = sb("ln2", [P, 2, 4], F32)
        wsum = sb("wsum", [P, 16], F32)
        sc = sb("sc", [P, 32], F32)
        X = sb("X", [P, 4, NC], F32)
        Bk = sb("Bk", [P, 2, 4, NC], F32)
        S = sb("S", [P, NC], F32)
        FIN = sb("FIN", [P, 8], F32)
        m8 = sb("m8", [P, 8], F32)
        e8 = sb("e8", [P, 8], F32)
        sel = sb("sel", [P, 16], F32)
        okf = sb("okf", [P, 2], F32)
        oki = sb("oki", [P, 1], I32)

        zP = pb("zP", [P, N], F32)
        hP = pb("hP", [P, 2, CW], F32)
        oP = pb("oP", [P, D], F32)
        xP = pb("xP", [P, KD * P], F32)
        ones32 = onesf[:, 0:HD]
        rowP = hP
        colP = [zP[:, j * 512:(j + 1) * 512] for j in range(3)]
        mT = zP[:, 3 * 512:4 * 512].bitcast(F16)
        mixP, sumP = oP, xP

        SC1, THR, NTHR, S1, S2, SH, SC2, SIG, T0 = (sc[:, i:i + 1] for i in range(9))

        names = ("vec_in x_in0 x_in1 x_in2 x_in3 w1_in0 w1_in1 w1_in2 w1_in3 w2_in0 w2_in1 w2_in2 w2_in3 "
                 "ones_set ident_set consts_set abs_done sum_ps sum_read tern_done sq_done scales_set search_set "
                 "stats1 xn_done rstd1 xT_ps xT_hi xT_lo z_ps z_evac z_bias upd cnt ok_set ok_sum "
                 "h_set hT_ps hT_hi hT_lo mm2 out_ps y_set stats2 rstd2 yn_set x_new xb_set out_done "
                 "consts2 ch_dve ch_act ch_pool phase "
                 "aw_in ab_in a_stats a_rstd a_xn a_turn a_xT p_ps p_out p_max q_max q_scale split_hi split_lo wo_in bo_in "
                 "stk0 stk1 mrow_in row_ps row_max m_set mT_ps m_rows col_ps exp_done mix_done norm_set "
                 "o_ps x_att masks bo_added attn_set")
        sm = {n: sem(n) for n in names.split()}

        block = ctx.enter_context(nc.Block())
        slots = range(-1, NT + S_FIN)

        ORDER = core_order()

        def seen(kind, upto, g=None):
            return sum(1 for e in ORDER[:upto] if e[0] == kind)

        ITEMS = [(kind, j, tc) for tc in range(2) for kind, js in (("in", range(4)), ("up", range(6))) for j in js]
        ITEMS += [("val", i, 0) for i in range(BT)]

        TOTAL = {k: seen(k, len(ORDER)) for k in ("row", "max", "col", "mix", "norm")}

        def barrier(eng, k):
            eng.drain().then_inc(sm["phase"], 1)
            eng.wait_ge(sm["phase"], 5 * k)

        def at(s, off):
            i = s - off
            return i if 0 <= i < NT else None

        FIRST_UPD, LAST_UPD = 3, NT + S_SEL - 1

        def updates(f, s):
            return f * (LAST_UPD - FIRST_UPD + 1) + s - FIRST_UPD + 1

        @block.sync
        def _(eng):
            xv = x.rearrange("(t p) d -> p t d", p=P)
            for c in range(4):
                eng.dma_start(Z[:, c, :], w_synT[c * P:(c + 1) * P, :]).then_inc(sm[f"w1_in{c}"], 16)
                if c == 0:
                    eng.dma_start(x_sb[:, 0:4, :], xv[:, 0:4, :]).then_inc(sm["x_in0"], 16)
            for v, d in ((b_syn, bsyn), (b_out, bout), (gamma, gam), (beta, bet)):
                eng.dma_start(d[:, :], v.partition_broadcast(P)).then_inc(sm["vec_in"], 16)
            w2v = w_outT.rearrange("(k p) o -> p k o", p=P)
            for c in range(4):
                eng.dma_start(Z[:, 4 + c, :].rearrange("p (k o) -> p k o", o=D),
                              w2v[:, 4 * c:4 * c + 4, :]).then_inc(sm[f"w2_in{c}"], 16)
            for c in range(1, 4):
                eng.dma_start(x_sb[:, 4 * c:4 * c + 4, :], xv[:, 4 * c:4 * c + 4, :]).then_inc(sm[f"x_in{c}"], 16)
            barrier(eng, 1)
            for b in range(2):
                for k in range(KD):
                    for w, lo in ((w_kv, 0), (w_q, 128), (w_kr, 256)):
                        eng.dma_start(w_in[:, k, lo:lo + w.shape[1]], w[k * P:(k + 1) * P, :]).then_inc(sm["aw_in"], 16)
                for k, w in ((0, w_ku), (1, w_qu), (2, w_qr), (3, w_vu)):
                    eng.dma_start(w_lat[:, k:k + w.shape[1] // 256, :].rearrange("p k n -> p (k n)"), w)\
                        .then_inc(sm["aw_in"], 16)
                if b == 0:
                    eng.dma_start(bcols[:, :], b_cols).then_inc(sm["ab_in"], 16)
                barrier(eng, 2 + 2 * b)

                def stacks(g):
                    if g >= 2:
                        eng.wait_ge(sm["mix_done"], b * TOTAL["mix"] + (g - 1) * TOTAL["mix"] // GROUPS)
                    for h in range(HG):
                        for w, order in enumerate(((0, 0, 1), (0, 1, 0))):
                            for j, part in enumerate(order):
                                eng.dma_start(stack[HD * j:HD * (j + 1), g % 2, w, h, :],
                                              parts[HD * h:HD * (h + 1), w, part, g, :])\
                                    .then_inc(sm[f"stk{g % 2}"], 16)

                def max_rows(g):
                    eng.wait_ge(sm["m_rows"], b * GROUPS + g + 1)
                    for h in range(HG):
                        eng.dma_start(stack[3 * HD:3 * HD + 2, g % 2, 0, h, :], mrows[2 * h:2 * h + 2, :])\
                            .then_inc(sm["mrow_in"], 16)

                stacks(0)
                stacks(1)
                eng.dma_start(wo_sb, w_o.rearrange("(k p) n -> p k n", p=P)).then_inc(sm["wo_in"], 16)
                eng.dma_start(bo, b_o.partition_broadcast(P)).then_inc(sm["bo_in"], 16)
                for g in range(GROUPS):
                    max_rows(g)
                    if g and g + 1 < GROUPS:
                        stacks(g + 1)
                barrier(eng, 3 + 2 * b)
            ov = out.rearrange("(t p) d -> p t d", p=P)
            for i in range(NT):
                eng.wait_ge(sm["x_new"], (NF - 1) * NT + i + 1)
                eng.dma_start(ov[:, i, :], x_sb[:, i, :]).then_inc(sm["out_done"], 16)
            eng.wait_ge(sm["out_done"], 16 * NT)

        @block.tensor
        def _(pe):
            def partition_sum(out_, in_, ready, value):
                pe.wait_ge(sm[ready], value)
                pe.matmul(out_, onesf[:, :], in_, start=True, stop=True).then_inc(sm["sum_ps"], 1)

            pe.wait_ge(sm["ones_set"], 1)
            pe.wait_ge(sm["ident_set"], 2)
            partition_sum(xP[:, 0:4], wsum[:, 0:4], "abs_done", 4)
            pe.wait_ge(sm["sum_read"], 1)

            def x_turn(f, i):
                g = f * NT + i
                pe.wait_ge(sm["xn_done"], g + 1)
                if g:
                    pe.wait_ge(sm["xT_lo"], g)
                for k in range(KD):
                    mm = pe.transpose(xP[:, k * P:(k + 1) * P], xn[:, g % 2, k * P:(k + 1) * P], identf[:, :])
                mm.then_inc(sm["xT_ps"], 1)

            def mm1(f, i, c):
                g = f * NT + i
                if c == 0:
                    pe.wait_ge(sm["xT_lo"], g + 1)
                    pe.wait_ge(sm["tern_done"], 4)
                if g:
                    pe.wait_ge(sm["z_evac"], 4 * (g - 1) + c + 1)
                for n, part in enumerate((xThi, xTlo)):
                    for k in range(KD):
                        mm = pe.matmul(zP[:, c * CW:(c + 1) * CW], part[:, g % 2, k, :], T1[:, k, c * CW:(c + 1) * CW],
                                       start=(n == 0 and k == 0), stop=(n == 1 and k == KD - 1))
                mm.then_inc(sm["z_ps"], 1)

            def h_turn(f, i, c):
                g = f * NT + i
                if c == 0:
                    pe.wait_ge(sm["h_set"], g + 1)
                q = 4 * g + c
                if q >= 2:
                    pe.wait_ge(sm["hT_lo"], q - 1)
                for k in range(4):
                    n0 = c * CW + k * P
                    mm = pe.transpose(hP[:, c % 2, k * P:(k + 1) * P], Z[:, g % ZR, n0:n0 + P], identf[:, :])
                mm.then_inc(sm["hT_ps"], 1)

            def mm2(f, i, c):
                g = f * NT + i
                pe.wait_ge(sm["hT_lo"], 4 * g + c + 1)
                if c == 0:
                    pe.wait_ge(sm["tern_done"], 8)
                    pe.wait_ge(sm["sum_read"], 3)
                    if g:
                        pe.wait_ge(sm["y_set"], g)
                for n, part in enumerate((hThi, hTlo)):
                    for k in range(4 * c, 4 * c + 4):
                        mm = pe.matmul(oP[:, :], part[:, k, :], T2[:, k, :],
                                       start=(c == 0 and n == 0 and k == 0), stop=(c == 3 and n == 1 and k == KN - 1))
                mm.then_inc(sm["mm2"], 1)

            def project(b):
                for i in range(BT):
                    g = b * BT + i
                    pe.wait_ge(sm["a_xn"], g + 1)
                    if g >= 2:
                        pe.wait_ge(sm["a_xT"], g - 1)
                    for k in range(KD):
                        mm = pe.transpose(hP[:, i % 2, k * P:(k + 1) * P], axn[:, g % 2, k * P:(k + 1) * P], identf[:, :])
                    mm.then_inc(sm["a_turn"], 1)
                pe.wait_ge(sm["aw_in"], 16 * 16 * (b + 1))
                for n, (kind, j, tc) in enumerate(ITEMS):
                    g = b * len(ITEMS) + n
                    if g >= 4:
                        pe.wait_ge(sm["p_out"], g - 3)
                    o = zP[:, n % 4 * 512:(n % 4 + 1) * 512]
                    tok = slice(tc * 512, (tc + 1) * 512)
                    if kind == "in":
                        pe.wait_ge(sm["a_xT"], b * BT + 4 * (tc + 1))
                        for k in range(KD):
                            mm = pe.matmul(o, w_in[:, k, j * P:(j + 1) * P], xnT[:, k, tok],
                                           start=(k == 0), stop=(k == KD - 1))
                    elif kind == "up":
                        src = 0 if j < 2 else 1
                        pe.wait_ge(sm["p_out"], b * len(ITEMS) + ITEMS.index(("in", src, tc)) + 1)
                        mm = pe.matmul(o, w_lat[:, j // 2, (j % 2) * P:(j % 2 + 1) * P], lat[:, src, tok],
                                       start=True, stop=True)
                    else:
                        mm = pe.matmul(o, lat[:, 0, j * P:(j + 1) * P],
                                       w_lat[:, 3:5, :].rearrange("p k n -> p (k n)"), start=True, stop=True)
                    mm.then_inc(sm["p_ps"], 1)

            def core(b):
                n = {k: b * v for k, v in TOTAL.items()}
                for e in ORDER:
                    kind, g = e[:2]
                    buf = g % 2
                    m = n[kind]
                    n[kind] += 1
                    if kind == "row":
                        h, t, c = e[2:]
                        if (h, t, c) == (0, 0, 0):
                            pe.wait_ge(sm[f"stk{buf}"], 16 * 6 * HG * (2 * b + g // 2 + 1))
                            pe.wait_ge(sm["masks"], 2)
                        if m >= 2:
                            pe.wait_ge(sm["row_max"], m - 1)
                        w = min(512, (t + 1) * P - 512 * c)
                        own = c == t // 4
                        mm = pe.matmul(rowP[:, m % 2, 0:w], stack[0:3 * HD, buf, 0, h, t * P:(t + 1) * P],
                                       stack[0:3 * HD, buf, 1, h, 512 * c:512 * c + w], start=True, stop=not own)
                        if own:
                            mm = pe.matmul(rowP[:, m % 2, w - P:w], identm[:, :], maskq[:, :], start=False, stop=True)
                        mm.then_inc(sm["row_ps"], 1)
                    elif kind == "max":
                        pe.wait_ge(sm["m_set"], m + 1)
                        if m:
                            pe.wait_ge(sm["m_rows"], m)
                        for t in range(BT):
                            mm = pe.transpose(mT[0:2 * HG, t * P:(t + 1) * P],
                                              mrow[:, t, :, :].rearrange("p h l -> p (h l)"), ident16[:, :])
                        mm.then_inc(sm["mT_ps"], 1)
                    elif kind == "col":
                        qc, kb, h = e[2:]
                        if (qc, kb, h) == (0, 0, 0):
                            pe.wait_ge(sm["mrow_in"], 16 * HG * (GROUPS * b + g + 1))
                            pe.wait_ge(sm["masks"], 3 + b)
                        if m >= 3:
                            pe.wait_ge(sm["exp_done"], m - 2)
                        q0 = max(0, kb * P - qc * 512)
                        own = kb * P >= qc * 512
                        mm = pe.matmul(colP[m % 3][:, q0:512], stack[0:3 * HD + 2, buf, 1, h, kb * P:(kb + 1) * P],
                                       stack[0:3 * HD + 2, buf, 0, h, qc * 512 + q0:(qc + 1) * 512],
                                       start=True, stop=not own)
                        if own:
                            mm = pe.matmul(colP[m % 3][:, q0:q0 + P], identm[:, :], maskk[:, :], start=False, stop=True)
                        mm.then_inc(sm["col_ps"], 1)
                    elif kind == "mix":
                        qc, kb = e[2:]
                        pe.wait_ge(sm["exp_done"], 4 * (m + 1))
                        if kb == 0 and n["norm"]:
                            pe.wait_ge(sm["norm_set"], n["norm"])
                        q0 = max(0, kb * P - qc * 512)
                        last = kb == 4 * qc + 3
                        for dst, own_v in ((mixP, True), (sumP, False)):
                            for h in range(HG):
                                v = V[:, kb, g * P + h * HD:g * P + (h + 1) * HD] if own_v else ones32
                                mm = pe.matmul(dst[h * HD:(h + 1) * HD, q0:512], v, PT[:, m % 2, h, q0:512],
                                               start=(kb == 0), stop=last, tile_position=(0, h * HD),
                                               skip_group_check=True)
                        mm.then_inc(sm["mix_done"], 1)
                pe.wait_ge(sm["attn_set"], (b + 1) * TOTAL["norm"])
                pe.wait_ge(sm["wo_in"], 16 * (b + 1))
                pe.wait_ge(sm["exp_done"], (b + 1) * TOTAL["col"])
                pe.wait_ge(sm["m_rows"], (b + 1) * GROUPS)
                for i in range(BT):
                    g = b * BT + i
                    if i >= 4:
                        pe.wait_ge(sm["x_att"], g - 3)
                    for k in range(KD):
                        mm = pe.matmul(zP[:, i % 4 * 512:(i % 4 + 1) * 512], attT[:, k, i * P:(i + 1) * P], wo_sb[:, k, :],
                                       start=(k == 0), stop=(k == KD - 1))
                    mm.then_inc(sm["o_ps"], 1)

            for f in range(NF):
                for s in slots:
                    for c in range(4):
                        i = at(s, S_OUT)
                        if i is not None:
                            h_turn(f, i, c)
                        i = at(s, 1)
                        if i is not None:
                            mm1(f, i, c)
                        i = at(s, S_OUT if c >= 2 else S_OUT + 1)
                        if i is not None:
                            mm2(f, i, c - 2 if c >= 2 else c + 2)
                        if c == 2:
                            i = at(s, 0)
                            if i is not None:
                                x_turn(f, i)
                    if f == 0 and s == 0:
                        partition_sum(oP[:, 0:4], wsum[:, 4:8], "abs_done", 8)
                        pe.wait_ge(sm["sum_read"], 2)
                        partition_sum(oP[:, 0:1], wsum[:, 8:9], "sq_done", 1)
                if f == 0:
                    barrier(pe, 1)
                    for b in range(2):
                        project(b)
                        barrier(pe, 2 + 2 * b)
                        core(b)
                        barrier(pe, 3 + 2 * b)

        @block.scalar
        def _(act):
            for n in range(2):
                for c in range(4):
                    act.wait_ge(sm[f"w{n + 1}_in{c}"], 16)
                    if n or c:
                        act.wait_ge(sm["abs_done"], 4 * n + c)
                    act.activation(junk[:, 0, :], Z[:, 4 * n + c, :], ACT.Abs,
                                   accum_out=wsum[:, 4 * n + c:4 * n + c + 1]).then_inc(sm["abs_done"], 1)
            act.wait_ge(sm["tern_done"], 1)
            act.wait_ge(sm["abs_done"], 8)
            act.activation(junk[:, 0, :], T1[:, 0, :], ACT.Square, accum_out=wsum[:, 8:9]).then_inc(sm["sq_done"], 1)
            act.wait_ge(sm["scales_set"], 1)
            act.wait_ge(sm["sq_done"], 1)

            def evac(f, i, c):
                g = f * NT + i
                act.wait_ge(sm["z_ps"], 4 * g + c + 1)
                if g >= ZR and c == 0:
                    act.wait_ge(sm["hT_ps"], 4 * (g - ZR) + 4)
                if g < 8 and c == 0:
                    act.wait_ge(sm["tern_done"], 4 if g < 4 else 8)
                act.activation(Z[:, g % ZR, c * CW:(c + 1) * CW], zP[:, c * CW:(c + 1) * CW], ACT.Copy,
                               scale=SC1).then_inc(sm["z_evac"], 1)

            def h_hi(f, i, c):
                g = f * NT + i
                act.wait_ge(sm["hT_ps"], 4 * g + c + 1)
                if g:
                    act.wait_ge(sm["mm2"], 4 * (g - 1) + c + 1)
                else:
                    act.wait_ge(sm["scales_set"], 2)
                act.activation(hThi[:, 4 * c:4 * c + 4, :].rearrange("p k t -> p (k t)"), hP[:, c % 2, :], ACT.Copy,
                               scale=SH).then_inc(sm["hT_hi"], 1)

            def x_hi(f, i):
                g = f * NT + i
                act.wait_ge(sm["xT_ps"], g + 1)
                if g >= 2:
                    act.wait_ge(sm["z_ps"], 4 * (g - 2) + 4)
                act.activation(xThi[:, g % 2, :, :].rearrange("p k t -> p (k t)"), xP[:, :], ACT.Copy,
                               scale=XSCALE).then_inc(sm["xT_hi"], 1)

            counted = [0]

            def count(f, s, k):
                i = at(s, 2 + k)
                if i is None:
                    return
                g = f * NT + i
                if k == 0:
                    act.wait_ge(sm["search_set"], 1)
                    act.wait_ge(sm["z_bias"], 4 * g + 4)
                if s >= FIRST_UPD:
                    act.wait_ge(sm["upd"], updates(f, s))
                elif f:
                    act.wait_ge(sm["upd"], updates(f - 1, LAST_UPD))
                if counted[0] >= 2:
                    act.wait_ge(sm["cnt"], counted[0] - 1)
                act.activation(junk[:, counted[0] % 2, :], Z[:, g % ZR, :], ACT.Sign, bias=X[:, 2, k:k + 1],
                               accum_out=S[:, k:k + 1]).then_inc(sm["cnt"], 1)
                counted[0] += 1

            def project(b):
                for i in range(BT):
                    g = b * BT + i
                    act.wait_ge(sm["a_turn"], g + 1)
                    act.activation(xnT[:, :, i * P:(i + 1) * P], hP[:, i % 2, :].rearrange("p (k t) -> p k t", k=KD),
                                   ACT.Copy).then_inc(sm["a_xT"], 1)
                if b == 0:
                    act.wait_ge(sm["ab_in"], 16)
                for n, (kind, j, tc) in enumerate(ITEMS):
                    g = b * len(ITEMS) + n
                    act.wait_ge(sm["p_ps"], g + 1)
                    o = zP[:, n % 4 * 512:(n % 4 + 1) * 512]
                    tok = slice(tc * 512, (tc + 1) * 512)
                    if kind == "val":
                        act.activation(V[:, j, :], o, ACT.Copy).then_inc(sm["p_out"], 1)
                        continue
                    if kind == "in":
                        dst, col = (lat[:, j, tok], j) if j < 2 else (qk[:, 1, j, tok], j)
                    else:
                        dst, col = (qk[:, 1, j, tok], 4 + j) if j < 2 else (qk[:, 0, j - 2, tok], 4 + j)
                    act.activation(dst, o, ACT.Identity, bias=bcols[:, col:col + 1]).then_inc(sm["p_out"], 1)
                act.wait_ge(sm["q_scale"], b + 1)
                for n, (w, k) in enumerate((w, k) for k in range(KD) for w in range(2)):
                    act.activation(parts[:, w, 0, k, :], qk[:, w, k, :], ACT.Copy, scale=asc[:, 8 + w:9 + w])\
                        .then_inc(sm["split_hi"], 1)

            def core(b):
                n = {k: b * v for k, v in TOTAL.items()}
                for e in ORDER:
                    kind, g = e[:2]
                    m = n[kind]
                    n[kind] += 1
                    if kind == "col":
                        qc, kb, h = e[2:]
                        act.wait_ge(sm["col_ps"], m + 1)
                        if m // 4 >= 2:
                            act.wait_ge(sm["mix_done"], m // 4 - 1)
                        q0 = max(0, kb * P - qc * 512)
                        act.activation(PT[:, m // 4 % 2, h, q0:512], colP[m % 3][:, q0:512], ACT.Exp,
                                       scale=asc[:, 10:11]).then_inc(sm["exp_done"], 1)
                    elif kind == "max":
                        act.wait_ge(sm["mT_ps"], m + 1)
                        if m:
                            act.wait_ge(sm["mrow_in"], 16 * HG * m)
                        act.activation(mrows, mT[0:2 * HG, :], ACT.Copy).then_inc(sm["m_rows"], 1)

            for f in range(NF):
                for s in slots:
                    for c in range(4):
                        i = at(s, 1)
                        if i is not None:
                            evac(f, i, c)
                        i = at(s, S_OUT)
                        if i is not None:
                            h_hi(f, i, c)
                        for k in ((4, 3), (2,), (1, 0), ())[c]:
                            count(f, s, k)
                    i = at(s, 0)
                    if i is not None:
                        x_hi(f, i)
                if f == 0:
                    barrier(act, 1)
                    for b in range(2):
                        project(b)
                        barrier(act, 2 + 2 * b)
                        core(b)
                        barrier(act, 3 + 2 * b)

        def counts_before(f, s):
            per_f = NC * NT
            return f * per_f + sum(1 for t in range(-1, s) for k in range(NC) if at(t, 2 + k) is not None)

        @block.gpsimd
        def _(pool):
            n = [0]

            def link(ins):
                n[0] += 1
                ins.then_inc(sm["ch_pool"], 1)
                pool.wait_ge(sm["ch_pool"], n[0])

            pool.memset(onesf[:, :], 1.0).then_inc(sm["ones_set"], 1)
            pool.memset(identf[:, :], 0.0).then_inc(sm["ident_set"], 1)
            pool.wait_ge(sm["ident_set"], 1)
            pool.affine_select(out=identf[:, :], in_=identf[:, :], compare_op=ALU.not_equal, fill=1.0, base=0,
                               pattern=[[-1, P]], channel_multiplier=1).then_inc(sm["ident_set"], 1)
            pool.wait_ge(sm["ident_set"], 2)
            link(pool.tensor_copy(ident16[:, :], identf[:, :]))
            link(pool.tensor_scalar(identm[:, :], identf[:, :], MASK, None, ALU.mult))
            link(pool.memset(maskq[:, :], 0.0))
            link(pool.memset(maskk[:, :], 0.0))
            pool.affine_select(out=maskq[:, :], in_=maskq[:, :], compare_op=ALU.is_ge, fill=-MASK, base=0,
                               pattern=[[-1, P]], channel_multiplier=1).then_inc(sm["masks"], 1)
            pool.affine_select(out=maskk[:, :], in_=maskk[:, :], compare_op=ALU.is_ge, fill=-MASK, base=0,
                               pattern=[[1, P]], channel_multiplier=-1).then_inc(sm["masks"], 1)
            link(pool.memset(nhalf[:, :], -0.5))
            link(pool.memset(half[:, :], 0.5))
            for k in range(8):
                pool.memset(iota8[:, k:k + 1], float(k)).then_inc(sm["consts_set"], 1)
                pool.wait_ge(sm["consts_set"], k + 1)
            def rstd1(f, i):
                g = f * NT + i
                pool.wait_ge(sm["stats1"], g + 1)
                link(pool.tensor_scalar(ln1[:, g % 2, 2:3], ln1[:, g % 2, 1:2], EPS, None, ALU.add))
                pool.tensor_tensor(ln1[:, g % 2, 3:4], ln1[:, g % 2, 2:3], nhalf[:, :], ALU.pow)\
                    .then_inc(sm["rstd1"], 1)

            def xbias(f, i):
                g = f * NT + i
                pool.wait_ge(sm["xn_done"], g + 1)
                if g == 0:
                    pool.wait_ge(sm["vec_in"], 64)
                if g >= XR:
                    pool.wait_ge(sm["y_set"], g - XR + 1)
                pool.tensor_tensor(xb[:, g % XR, :], xn[:, g % 2, :], bout[:, :], ALU.add).then_inc(sm["xb_set"], 1)

            def bias(f, i, c):
                g = f * NT + i
                pool.wait_ge(sm["z_evac"], 4 * g + c + 1)
                zz = Z[:, g % ZR, c * CW:(c + 1) * CW]
                pool.tensor_tensor(zz, zz, bsyn[:, c * CW:(c + 1) * CW], ALU.add).then_inc(sm["z_bias"], 1)

            def ok_sum(f, i):
                g = f * NT + i
                pool.wait_ge(sm["ok_set"], g + 1)
                link(pool.partition_all_reduce(okf[:, 1:2], okf[:, 0:1], P, bass.bass_isa.ReduceOp.add))
                pool.tensor_copy(oki[:, :], okf[:, 1:2]).then_inc(sm["ok_sum"], 1)

            def rstd2(f, i):
                g = f * NT + i
                pool.wait_ge(sm["stats2"], g + 1)
                link(pool.tensor_scalar(ln2[:, g % 2, 2:3], ln2[:, g % 2, 1:2], EPS, None, ALU.add))
                pool.tensor_tensor(ln2[:, g % 2, 3:4], ln2[:, g % 2, 2:3], nhalf[:, :], ALU.pow)\
                    .then_inc(sm["rstd2"], 1)

            def final(f, i):
                g = f * NT + i
                link(pool.tensor_tensor(x_sb[:, i, :], x_sb[:, i, :], bet[:, :], ALU.add))
                pool.wait_ge(sm["yn_set"], g + 1)
                link(pool.tensor_tensor(yt[:, g % 2, :], yt[:, g % 2, :], gam[:, :], ALU.mult))
                pool.tensor_tensor(x_sb[:, i, :], x_sb[:, i, :], yt[:, g % 2, :], ALU.add).then_inc(sm["x_new"], 1)

            def project(b):
                for i in range(BT):
                    g = b * BT + i
                    pool.wait_ge(sm["a_stats"], g + 1)
                    link(pool.tensor_scalar(aln[:, g % 2, 2:3], aln[:, g % 2, 1:2], EPS, None, ALU.add))
                    pool.tensor_tensor(aln[:, g % 2, 3:4], aln[:, g % 2, 2:3], nhalf[:, :], ALU.pow)\
                        .then_inc(sm["a_rstd"], 1)
                pool.wait_ge(sm["p_max"], b + 1)
                pool.partition_all_reduce(asc[:, 2:4], asc[:, 0:2], P, bass.bass_isa.ReduceOp.max).then_inc(sm["q_max"], 1)

            def core(b):
                pool.memset(stack[3 * HD:3 * HD + 2, :, 1, :, :], MUNIT).then_inc(sm["masks"], 1)
                pool.wait_ge(sm["masks"], 3 + b)
                pool.wait_ge(sm["bo_in"], 16 * (b + 1))
                for i in range(BT):
                    t = x_sb[:, b * BT + i, :]
                    pool.tensor_tensor(t, t, bo, ALU.add).then_inc(sm["bo_added"], 1)

            for f in range(NF):
                for s in slots:
                    i = at(s, -1)
                    if i is not None:
                        rstd1(f, i)
                    for c in range(4):
                        i = at(s, 1)
                        if i is not None:
                            bias(f, i, c)
                        if c == 1:
                            i = at(s, S_SEL)
                            if i is not None:
                                ok_sum(f, i)
                        if c == 2:
                            i = at(s, -1)
                            if i is not None:
                                xbias(f, i)
                    i = at(s, S_FIN)
                    if i is not None:
                        rstd2(f, i)
                        final(f, i)
                    if f == 0 and s == 0:
                        pool.wait_ge(sm["scales_set"], 3)
                        pool.tensor_tensor(SIG, sc[:, 16:17], half[:, :], ALU.pow).then_inc(sm["scales_set"], 1)
                        link(pool.tensor_scalar(gam[:, :], gam[:, :], 0.5, None, ALU.mult))
                        link(pool.tensor_scalar(bet[:, :], bet[:, :], 0.5, None, ALU.mult))
                if f == 0:
                    barrier(pool, 1)
                    for b in range(2):
                        project(b)
                        barrier(pool, 2 + 2 * b)
                        core(b)
                        barrier(pool, 3 + 2 * b)

        @block.vector
        def _(dve):
            n = [0]

            def link(ins):
                n[0] += 1
                ins.then_inc(sm["ch_dve"], 1)
                dve.wait_ge(sm["ch_dve"], n[0])

            def ternary(m, c):
                w = Z[:, 4 * m + c, :]
                low = M[:, 0:N // 2].bitcast(F16) if c % 2 else M[:, N // 2:N].bitcast(F16)
                link(dve.tensor_scalar(low, w, NTHR, None, ALU.is_lt))
                o = T1[:, c, :] if m == 0 else T2[:, 4 * c:4 * c + 4, :].rearrange("p k o -> p (k o)")
                dve.scalar_tensor_tensor(o, w, THR, low, ALU.is_gt, ALU.subtract).then_inc(sm["tern_done"], 1)
                dve.wait_ge(sm["tern_done"], 4 * m + c + 1)

            def scale_of(m, dst):
                dve.wait_ge(sm["sum_ps"], m + 1)
                dve.tensor_reduce(sc[:, 12 + m:13 + m], (xP, oP)[m][:, 0:4], AX.X, ALU.add).then_inc(sm["sum_read"], 1)
                dve.wait_ge(sm["sum_read"], m + 1)
                link(dve.tensor_scalar(dst, sc[:, 12 + m:13 + m], 1.0 / (N * D), None, ALU.mult))
                link(dve.tensor_scalar(THR, dst, 1e-8, 0.5, ALU.add, ALU.mult))
                link(dve.tensor_scalar(NTHR, THR, -1.0, None, ALU.mult))

            def constants():
                scale_of(1, S2)
                dve.wait_ge(sm["consts_set"], 8)
                dve.wait_ge(sm["vec_in"], 64)
                link(dve.tensor_reduce(sc[:, 17:18], bsyn[:, :], AX.X, ALU.max, apply_absolute_value=True))
                link(dve.scalar_tensor_tensor(sc[:, 18:19], S1, float(D), sc[:, 17:18], ALU.mult, ALU.add))
                link(dve.tensor_scalar(sc[:, 18:19], sc[:, 18:19], 1e-30, None, ALU.max))
                link(dve.tensor_scalar(sc[:, 19:20].bitcast(I32), sc[:, 18:19].bitcast(I32), 0x7F800000, None,
                                       ALU.bitwise_and))
                link(dve.reciprocal(sc[:, 20:21], sc[:, 19:20]))
                link(dve.tensor_scalar(SH, sc[:, 20:21], HTOP, None, ALU.mult))
                dve.scalar_tensor_tensor(SC2, S2, 1.0 / HTOP, sc[:, 19:20], ALU.mult, ALU.mult)\
                    .then_inc(sm["scales_set"], 1)
                dve.wait_ge(sm["stats1"], 2)
                for c in range(4):
                    link(dve.bn_stats(st6[:, 6 * c:6 * c + 6], bsyn[:, c * CW:(c + 1) * CW]))
                link(dve.bn_aggr(sc[:, 21:23], st6[:, :]))
                dve.wait_ge(sm["sum_ps"], 3)
                dve.tensor_scalar(sc[:, 23:24], oP[:, 0:1], float(D) / (P * N), None, ALU.mult).then_inc(sm["sum_read"], 1)
                dve.wait_ge(sm["sum_read"], 3)
                link(dve.tensor_tensor(sc[:, 24:25], S1, S1, ALU.mult))
                dve.scalar_tensor_tensor(sc[:, 16:17], sc[:, 24:25], sc[:, 23:24], sc[:, 22:23], ALU.mult, ALU.add)\
                    .then_inc(sm["scales_set"], 1)
                dve.wait_ge(sm["scales_set"], 4)
                link(dve.scalar_tensor_tensor(T0, SIG, 1.2816, sc[:, 21:22], ALU.mult, ALU.add))
                t0, sig = T0.broadcast_to([P, NC]), SIG.broadcast_to([P, NC])
                dve.memset(S[:, :], 0.0).then_inc(sm["consts2"], 1)
                dve.tensor_scalar(X[:, 0, :], t0, 1.0, None, ALU.mult).then_inc(sm["consts2"], 1)
                dve.tensor_scalar(X[:, 2, :], t0, -1.0, None, ALU.mult).then_inc(sm["consts2"], 1)
                for j in range(2):
                    dve.scalar_tensor_tensor(Bk[:, j, 0, :], sig, -0.3, t0, ALU.mult, ALU.add).then_inc(sm["consts2"], 1)
                    dve.scalar_tensor_tensor(Bk[:, j, 2, :], sig, -0.3, t0, ALU.mult, ALU.subtract)\
                        .then_inc(sm["consts2"], 1)
                dve.memset(Bk[:, :, 1, :], -248.0).then_inc(sm["consts2"], 1)
                dve.memset(Bk[:, :, 3, :], -183.0).then_inc(sm["consts2"], 1)
                dve.wait_ge(sm["consts2"], 9)
                dve.memset(sel[:, 15:16], 0.0).then_inc(sm["search_set"], 1)

            def stats1(f, i):
                g = f * NT + i
                if f == 0:
                    dve.wait_ge(sm[f"x_in{i // 4}"], 16)
                link(dve.bn_stats(st6[:, 0:6], x_sb[:, i, :]))
                if g >= 2:
                    dve.wait_ge(sm["rstd1"], g - 1)
                dve.bn_aggr(ln1[:, g % 2, 0:2], st6[:, 0:6]).then_inc(sm["stats1"], 1)

            def normal(f, i):
                g = f * NT + i
                dve.wait_ge(sm["stats1"], g + 1)
                dve.wait_ge(sm["rstd1"], g + 1)
                if g >= 2:
                    dve.wait_ge(sm["xT_ps"], g - 1)
                    dve.wait_ge(sm["xb_set"], g - 1)
                dve.tensor_scalar(xn[:, g % 2, :], x_sb[:, i, :], ln1[:, g % 2, 0:1], ln1[:, g % 2, 3:4],
                                  ALU.subtract, ALU.mult).then_inc(sm["xn_done"], 1)

            def x_lo(f, i):
                g = f * NT + i
                dve.wait_ge(sm["xT_hi"], g + 1)
                dve.scalar_tensor_tensor(xTlo[:, g % 2, :, :].rearrange("p k t -> p (k t)"), xP[:, :], XSCALE,
                                         xThi[:, g % 2, :, :].rearrange("p k t -> p (k t)"), ALU.mult,
                                         ALU.subtract).then_inc(sm["xT_lo"], 1)

            def h_lo(f, i, c):
                g = f * NT + i
                dve.wait_ge(sm["hT_hi"], 4 * g + c + 1)
                ks = slice(4 * c, 4 * c + 4)
                dve.scalar_tensor_tensor(hTlo[:, ks, :].rearrange("p k t -> p (k t)"), hP[:, c % 2, :], SH,
                                         hThi[:, ks, :].rearrange("p k t -> p (k t)"), ALU.mult,
                                         ALU.subtract).then_inc(sm["hT_lo"], 1)

            def update(f, s):
                u = updates(f, s)
                dve.wait_ge(sm["cnt"], counts_before(f, s))
                old, new = Bk[:, u % 2, :, :], Bk[:, (u + 1) % 2, :, :]
                w = NC - 1
                link(dve.tensor_scalar(X[:, 3, :], S[:, :], SSTAR, None, ALU.subtract))
                link(dve.tensor_scalar(X[:, 1, :], S[:, :], -1.0, SSTAR, ALU.mult, ALU.add))
                link(dve.tensor_copy(FIN[:, 0:4], X[:, :, NC - 1]))
                link(dve.tensor_copy(FIN[:, 4:5], old[:, 2, NC - 1:NC]))
                d = X[:, 3:4, 0:w].broadcast_to([P, 2, w])
                link(dve.tensor_scalar(G[:, 0:2, 0:w], d, 0.0, None, ALU.is_lt))
                link(dve.tensor_scalar(G[:, 2:4, 0:w], d, 0.0, None, ALU.is_ge))
                link(dve.scalar_tensor_tensor(Y4[:, :, 0:w], G[:, :, 0:w], -BIG, X[:, :, 0:w], ALU.mult, ALU.add))
                link(dve.tensor_tensor(new[:, :, 1:NC], old[:, :, 0:w], Y4[:, :, 0:w], ALU.max))
                link(dve.tensor_tensor(W2[:, :, 0:w], new[:, 0:2, 1:NC], new[:, 2:4, 1:NC], ALU.add))
                link(dve.reciprocal(E2[:, 0, 0:w], W2[:, 1, 0:w]))
                link(dve.tensor_tensor(E2[:, 1, 0:w], W2[:, 0, 0:w], new[:, 1, 1:NC], ALU.mult))
                link(dve.tensor_tensor(E2[:, 2, 0:w], E2[:, 1, 0:w], E2[:, 0, 0:w], ALU.mult))
                link(dve.tensor_tensor(X[:, 0, 1:NC], new[:, 0, 1:NC], E2[:, 2, 0:w], ALU.subtract))
                dve.tensor_tensor(X[:, 2, 1:NC], E2[:, 2, 0:w], new[:, 0, 1:NC], ALU.subtract).then_inc(sm["upd"], 1)

            TF, DF = FIN[:, 0:1], FIN[:, 3:4]
            TH, FND, IDX = sel[:, 0:1], sel[:, 1:2], sel[:, 2:3]
            OPEN, BOUND, ABOVE, HIT, TMP = (sel[:, j:j + 1] for j in range(3, 8))

            def below(f, i):
                g = f * NT + i
                link(dve.scalar_tensor_tensor(M[:, :], Z[:, g % ZR, :], TF, Z[:, g % ZR, :], ALU.is_le, ALU.mult))

            def pick(f, i):
                g = f * NT + i
                link(dve.max(m8[:, :], M[:, :]))
                link(dve.tensor_scalar(IDX, DF, -0.5, TOPK - 1 - TARGET, ALU.mult, ALU.add))
                link(dve.tensor_scalar(e8[:, :], iota8[:, :], IDX, None, ALU.is_equal, ALU.add, accum_out=FND))
                link(dve.scalar_tensor_tensor(e8[:, :], e8[:, :], 1.0, m8[:, :], ALU.mult, ALU.mult, accum_out=TH))
                if g:
                    dve.wait_ge(sm["ok_sum"], g)
                dve.scalar_tensor_tensor(okf[:, 0:1], m8[:, 0:1], TF, FND, ALU.is_lt, ALU.mult)\
                    .then_inc(sm["ok_set"], 1)

            def search_down(z):
                def step(ins):
                    dve.drain()
                    return ins

                def add_found(found, value):
                    step(dve.tensor_scalar(TMP, value, 0.0, None, ALU.max))
                    step(dve.scalar_tensor_tensor(TH, TMP, found, TH, ALU.mult, ALU.add))
                    step(dve.tensor_tensor(OPEN, OPEN, found, ALU.subtract))

                dve.drain()
                step(dve.tensor_scalar(OPEN, okf[:, 0:1], -1.0, 1.0, ALU.mult, ALU.add))
                step(dve.tensor_tensor(TH, TH, okf[:, 0:1], ALU.mult))
                step(dve.tensor_scalar(BOUND, FIN[:, 4:5], -1.0, None, ALU.mult))
                step(dve.tensor_scalar(M, z, BOUND, None, ALU.is_ge, ALU.add, accum_out=ABOVE))
                step(dve.tensor_scalar(HIT, ABOVE, float(TOPK), None, ALU.is_lt))
                step(dve.tensor_tensor(BOUND, BOUND, HIT, ALU.mult))
                step(dve.tensor_tensor(ABOVE, ABOVE, HIT, ALU.mult))
                step(dve.tensor_scalar(HIT, HIT, -3e38, 3e38, ALU.mult, ALU.add))
                step(dve.tensor_tensor(BOUND, BOUND, HIT, ALU.add))
                step(dve.memset(flags[:, :], 0.0))

                def still_open():
                    step(dve.tensor_copy(flags[:, 0:1], OPEN))
                    step(dve.transpose(flagsT[:, :], flags[:, :]))
                    step(dve.tensor_reduce(TMP, flagsT[:, :], AX.X, ALU.max))
                    step(dve.tensor_copy(flagi[:, :], TMP))
                    return sum(dve.value_load(flagi[q:q + 1, :], min_val=0, max_val=1) for q in range(0, P, 32))

                with dve.While(lambda: still_open() > 0):
                    step(dve.scalar_tensor_tensor(M, z, BOUND, z, ALU.is_lt, ALU.mult))
                    step(dve.max(m8[:, :], M))
                    step(dve.tensor_scalar(IDX, ABOVE, -1.0, TOPK - 1.0, ALU.mult, ALU.add))
                    step(dve.tensor_scalar(e8[:, :], iota8[:, :], IDX, None, ALU.is_equal, ALU.add, accum_out=HIT))
                    step(dve.scalar_tensor_tensor(e8[:, :], e8[:, :], 1.0, m8[:, :], ALU.mult, ALU.mult,
                                                  accum_out=BOUND))
                    step(dve.tensor_tensor(HIT, HIT, OPEN, ALU.mult))
                    add_found(HIT, BOUND)
                    step(dve.tensor_copy(BOUND, m8[:, 7:8]))
                    step(dve.tensor_scalar(M, z, BOUND, None, ALU.is_ge, ALU.add, accum_out=ABOVE))
                    step(dve.tensor_scalar(HIT, ABOVE, float(TOPK), None, ALU.is_ge))
                    step(dve.tensor_scalar(TMP, BOUND, 0.0, None, ALU.is_le))
                    step(dve.tensor_tensor(HIT, HIT, TMP, ALU.max))
                    step(dve.tensor_tensor(HIT, HIT, OPEN, ALU.mult))
                    add_found(HIT, BOUND)

            def keep_top(f, i):
                g = f * NT + i
                dve.wait_ge(sm["ok_sum"], g + 1)
                with dve.If(dve.value_load(oki[0:1, 0:1], min_val=0, max_val=P) < P):
                    search_down(Z[:, g % ZR, :])
                dve.scalar_tensor_tensor(Z[:, g % ZR, :], Z[:, g % ZR, :], TH, Z[:, g % ZR, :], ALU.is_ge, ALU.mult)\
                    .then_inc(sm["h_set"], 1)

            def residual(f, i):
                g = f * NT + i
                dve.wait_ge(sm["mm2"], 4 * g + 4)
                dve.wait_ge(sm["xb_set"], g + 1)
                dve.scalar_tensor_tensor(y[:, g % 2, :], oP[:, :], SC2, xb[:, g % XR, :], ALU.mult, ALU.add)\
                    .then_inc(sm["y_set"], 1)
                dve.wait_ge(sm["y_set"], g + 1)
                link(dve.bn_stats(st6[:, 6:12], y[:, g % 2, :]))
                dve.bn_aggr(ln2[:, g % 2, 0:2], st6[:, 6:12]).then_inc(sm["stats2"], 1)

            def normal2(f, i):
                g = f * NT + i
                dve.wait_ge(sm["stats2"], g + 1)
                dve.wait_ge(sm["rstd2"], g + 1)
                if g >= 2:
                    dve.wait_ge(sm["x_new"], g - 1)
                dve.tensor_scalar(yt[:, g % 2, :], y[:, g % 2, :], ln2[:, g % 2, 0:1], ln2[:, g % 2, 3:4],
                                  ALU.subtract, ALU.mult).then_inc(sm["yn_set"], 1)

            def project(b):
                for i in range(BT):
                    g = b * BT + i
                    link(dve.bn_stats(st6[:, 0:6], x_sb[:, g, :]))
                    if g >= 2:
                        dve.wait_ge(sm["a_rstd"], g - 1)
                    dve.bn_aggr(aln[:, g % 2, 0:2], st6[:, 0:6]).then_inc(sm["a_stats"], 1)
                    dve.wait_ge(sm["a_rstd"], g + 1)
                    dve.wait_ge(sm["a_stats"], g + 1)
                    if g >= 2:
                        dve.wait_ge(sm["a_turn"], g - 1)
                    dve.tensor_scalar(axn[:, g % 2, :], x_sb[:, g, :], aln[:, g % 2, 0:1], aln[:, g % 2, 3:4],
                                      ALU.subtract, ALU.mult).then_inc(sm["a_xn"], 1)
                seen_w = [0, 0]
                for n, (kind, j, tc) in enumerate(ITEMS):
                    if kind == "val" or (kind == "in" and j < 2):
                        continue
                    dve.wait_ge(sm["p_out"], b * len(ITEMS) + n + 1)
                    w, k = (1, j) if kind == "in" or j < 2 else (0, j - 2)
                    link(dve.tensor_reduce(mxq[:, w, seen_w[w]:seen_w[w] + 1], qk[:, w, k, tc * 512:(tc + 1) * 512],
                                           AX.X, ALU.max, apply_absolute_value=True))
                    seen_w[w] += 1
                dve.tensor_reduce(asc[:, 0:2], mxq[:, :, :], AX.X, ALU.max).then_inc(sm["p_max"], 1)
                dve.wait_ge(sm["q_max"], b + 1)
                link(dve.tensor_scalar(asc[:, 4:6].bitcast(I32), asc[:, 2:4].bitcast(I32), 0x7F800000, None,
                                       ALU.bitwise_and))
                link(dve.tensor_scalar(asc[:, 4:6], asc[:, 4:6], 0.5, None, ALU.max))
                link(dve.reciprocal(asc[:, 6:8], asc[:, 4:6]))
                link(dve.tensor_tensor(asc[:, 11:12], asc[:, 4:5], asc[:, 5:6], ALU.mult))
                link(dve.tensor_scalar(asc[:, 10:11], asc[:, 11:12], ATT_SCALE / 16384.0, None, ALU.mult))
                dve.tensor_scalar(asc[:, 8:10], asc[:, 6:8], 128.0, None, ALU.mult).then_inc(sm["q_scale"], 1)
                dve.wait_ge(sm["q_scale"], b + 1)
                for n, (w, k) in enumerate((w, k) for k in range(KD) for w in range(2)):
                    dve.wait_ge(sm["split_hi"], 8 * b + n + 1)
                    dve.scalar_tensor_tensor(parts[:, w, 1, k, :], qk[:, w, k, :], asc[:, 8 + w:9 + w],
                                             parts[:, w, 0, k, :], ALU.mult, ALU.subtract).then_inc(sm["split_lo"], 1)

            def core(b):
                n = {k: b * v for k, v in TOTAL.items()}
                for e in ORDER:
                    kind, g = e[:2]
                    m = n[kind]
                    n[kind] += 1
                    if kind == "row":
                        h, t, c = e[2:]
                        w = min(512, (t + 1) * P - 512 * c)
                        dve.wait_ge(sm["row_ps"], m + 1)
                        dve.tensor_reduce(mx[:, h, t, c:c + 1], rowP[:, m % 2, 0:w], AX.X, ALU.max)\
                            .then_inc(sm["row_max"], 1)
                    elif kind == "max":
                        dve.wait_ge(sm["row_max"], n["row"])
                        link(dve.tensor_reduce(mm_[:, :], mx[:, :, :, :].rearrange("p h t c -> p (h t) c"),
                                               AX.X, ALU.max))
                        link(dve.tensor_scalar(mm_[:, :], mm_[:, :], -1.0 / MUNIT, None, ALU.mult))
                        if m:
                            dve.wait_ge(sm["mT_ps"], m)
                        mv = mm_[:, :].rearrange("p (h t) -> p t h", h=HG)
                        link(dve.tensor_copy(mrow[:, :, :, 0], mv))
                        dve.tensor_tensor(mrow[:, :, :, 1], mv, mrow[:, :, :, 0], ALU.subtract).then_inc(sm["m_set"], 1)
                    elif kind == "norm":
                        qc = e[2]
                        dve.wait_ge(sm["mix_done"], n["mix"])
                        if m:
                            dve.wait_ge(sm["norm_set"], m)
                        link(dve.reciprocal(rec, sumP[:, :]))
                        a = attT[:, g, qc * 512:(qc + 1) * 512]
                        dve.tensor_tensor(a, mixP[:, :], rec, ALU.mult).then_inc(sm["norm_set"], 1)
                        dve.wait_ge(sm["norm_set"], m + 1)
                        dve.tensor_scalar(a, a, bcols[:, 10 + g:11 + g], None, ALU.add).then_inc(sm["attn_set"], 1)
                for i in range(BT):
                    g = b * BT + i
                    dve.wait_ge(sm["o_ps"], g + 1)
                    dve.wait_ge(sm["bo_added"], g + 1)
                    dve.tensor_tensor(x_sb[:, g, :], zP[:, i % 4 * 512:(i % 4 + 1) * 512], x_sb[:, g, :], ALU.add)\
                        .then_inc(sm["x_att"], 1)

            def do(stage, f, s, off, *a):
                i = at(s, off)
                if i is not None:
                    stage(f, i, *a)

            scale_of(0, S1)
            dve.tensor_scalar(SC1, S1, 1.0 / XSCALE, None, ALU.mult).then_inc(sm["scales_set"], 1)
            for c in range(4):
                ternary(0, c)
            for f in range(NF):
                for s in slots:
                    if f == 0 and s == 1:
                        constants()
                    if f == 0 and 1 <= s < 5:
                        ternary(1, s - 1)
                    if FIRST_UPD <= s <= LAST_UPD:
                        update(f, s)
                    do(h_lo, f, s, S_OUT, 0)
                    do(below, f, s, S_SEL)
                    do(h_lo, f, s, S_OUT, 1)
                    do(pick, f, s, S_SEL)
                    do(stats1, f, s, -1)
                    do(residual, f, s, S_FIN)
                    do(keep_top, f, s, S_SEL)
                    do(normal, f, s, -1)
                    do(h_lo, f, s, S_OUT, 2)
                    do(normal2, f, s, S_FIN)
                    do(h_lo, f, s, S_OUT, 3)
                    do(x_lo, f, s, 0)
                if f == 0:
                    barrier(dve, 1)
                    link(dve.memset(mx[:, :, :, :], -BIG))
                    for b in range(2):
                        project(b)
                        barrier(dve, 2 + 2 * b)
                        core(b)
                        barrier(dve, 3 + 2 * b)


def kernel(**inputs):
    import numpy as np
    import concourse.bacc as bacc
    from concourse.bass_utils import run_bass_kernel_spmd

    nc = bacc.Bacc("TRN2", target_bir_lowering=False, num_devices=1)
    x = np.ascontiguousarray(inputs["L0_attn_x"]).reshape(TOKENS, D)
    arrays = {
        "x": x,
        "w_synT": np.ascontiguousarray(np.asarray(inputs["L0_ffn_W_syn"]).T),
        "b_syn": np.ascontiguousarray(inputs["L0_ffn_b_syn"]),
        "w_outT": np.ascontiguousarray(np.asarray(inputs["L0_ffn_W_out"]).T),
        "b_out": np.ascontiguousarray(inputs["L0_ffn_b_out"]),
        "gamma": np.ascontiguousarray(inputs["L0_ffn_gamma"]),
        "beta": np.ascontiguousarray(inputs["L0_ffn_beta"]),
    }
    for n in ("w_kv", "w_q", "w_kr", "w_ku", "w_qu", "w_qr", "w_vu", "w_o"):
        arrays[n] = np.ascontiguousarray(inputs["L0_attn_" + n])
    cols = [np.asarray(inputs["L0_attn_" + n]).reshape(-1, P) for n in ("b_kv", "b_q", "b_kr", "b_ku", "b_qu", "b_qr", "b_vu")]
    arrays["b_cols"] = np.ascontiguousarray(np.concatenate(cols).T)
    arrays["b_o"] = np.ascontiguousarray(inputs["L0_attn_b_o"])
    aps = [nc.dram_tensor("in_" + k, v.shape, F32, kind="ExternalInput").ap() for k, v in arrays.items()]
    o = nc.dram_tensor("out_dram", (TOKENS, D), F32, kind="ExternalOutput").ap()
    program(nc, *aps, o)
    r = run_bass_kernel_spmd(nc, [{"in_" + k: v for k, v in arrays.items()}], core_ids=[0])
    return r.results[0]["out_dram"].reshape(2, 1024, D)
```

```python
import concourse.bass as bass
from concourse import mybir
from contextlib import ExitStack

F32 = mybir.dt.float32
F16 = mybir.dt.float16
BF16 = mybir.dt.bfloat16
I32 = mybir.dt.int32
I8 = mybir.dt.int8
ALU = mybir.AluOpType
ACT = mybir.ActivationFunctionType
AX = mybir.AxisListType

P = 128
TOKENS, D, N = 2048, 512, 2048
NT = TOKENS // P
KD = D // P
KN = N // P
CH = 4
CW = N // CH
TOPK = int(N * (1.0 - 0.9))
EPS = 1e-5

NC = 5
TARGET = TOPK - 4.5
SSTAR = 2 * TARGET - N
BIG = 1e30
S_SEL, S_OUT, S_FIN = 2 + NC, 3 + NC, 4 + NC
ZR = 8
XR = 11
XSCALE = 256.0
HTOP = 16384.0
NF = 2

HEADS, HD = 16, 32
SEQ = 1024
BT = SEQ // P
HG = 4
GROUPS = HEADS // HG
MUNIT = 64.0
MASK = 32768.0
ROW_LEAD = 8
ROW_STEPS = 8
ATT_SCALE = 1.0 / HD ** 0.5


def group_order(first, second):
    rows = []
    if first is not None:
        rows = [("row", first, h, t, c) for t in range(BT) for h in range(HG) for c in range(t // 4 + 1)]
    if second is None:
        return sorted(rows, key=lambda e: e[2]) + [("max", first), ("turn", first)]
    order = rows[:ROW_LEAD] if second == 0 else []
    done = len(order)
    work = [c for qc in range(2) for c in [512] * (4 * qc + 1) + [384, 256, 128]]
    blocks = [(qc, kb) for qc in range(2) for kb in range(4 * qc + 4)]
    for n, (qc, kb) in enumerate(blocks):
        col = [("col", second, qc, kb, h) for h in range(HG)]
        if kb:
            col.append(("mix", second, qc, kb - 1))
        if kb == 4 * qc + 3:
            col += [("mix", second, qc, kb), ("norm", second, qc)]
        if n < ROW_STEPS:
            upto = max(done, -(-len(rows) * sum(work[:n + 1]) // sum(work[:ROW_STEPS])))
        new = rows[done:upto]
        done = upto
        for j in range(max(len(new), len(col))):
            order += new[j:j + 1] + col[j:j + 1]
        if rows and n == ROW_STEPS - 1:
            order.append(("max", first))
        if rows and n == ROW_STEPS:
            order.append(("turn", first))
    return order


def core_order():
    steps = group_order(0, None)
    for g in range(GROUPS):
        steps += group_order(g + 1 if g + 1 < GROUPS else None, g)
    order, waiting = [], []
    for e in steps:
        order.append(e)
        if waiting and (e[0] == "mix" or e[0] == "col" and e[4] == 1):
            order.append(waiting.pop(0))
        if e[0] == "norm":
            waiting += [("rec", *e[1:], j) for j in range(4)]
    return order + waiting


def program(nc, x, w_synT, b_syn, w_outT, b_out, gamma, beta, w_kv, w_q, w_kr, w_ku, w_qu, w_qr, w_vu, w_o, b_cols,
            b_o, out):
    ctx = ExitStack()
    with ctx:
        def sb(name, shape, dt):
            return ctx.enter_context(nc.sbuf_tensor(name, shape, dt))

        def pb(name, shape, dt):
            return ctx.enter_context(nc.psum_tensor(name, shape, dt))

        def sem(name):
            return ctx.enter_context(nc.semaphore(name))

        x_sb = sb("x_sb", [P, NT, D], F32)
        T1 = sb("T1", [P, KD, N], F16)
        T2 = sb("T2", [P, KN, D], F16)
        bsyn = sb("bsyn", [P, N], F32)
        bout = sb("bout", [P, D], F32)
        gam = sb("gam", [P, D], F32)
        bet = sb("bet", [P, D], F32)
        identf = sb("identf", [P, P], F32)
        onesf = sb("onesf", [P, P], F32)
        iota8 = sb("iota8", [P, 8], F32)
        nhalf = sb("nhalf", [P, 1], F32)
        half = sb("half", [P, 1], F32)
        ARENA = (4 * ZR * N + 4 * N + 2 * 2 * N + 2 * 2 * KN * P + 2 * 2 * 2 * KD * P + 4 * 2 * D + 4 * XR * D
                 + 2 * 4 * 2 * D) // 4
        arena = sb("arena", [P, ARENA], F32)
        taken = [0]

        def carve(words, dt=F32):
            a = arena[:, taken[0]:taken[0] + words]
            taken[0] += words
            assert taken[0] <= ARENA
            return a if dt == F32 else a.bitcast(dt)

        Z = carve(ZR * N).rearrange("p (z n) -> p z n", z=ZR)
        M = carve(N)
        junk = carve(N // 2, I8).rearrange("p (b n) -> p b n", b=2)
        hThi = carve(KN * P // 2, F16).rearrange("p (k t) -> p k t", k=KN)
        hTlo = carve(KN * P // 2, F16).rearrange("p (k t) -> p k t", k=KN)
        xThi = carve(KD * P, F16).rearrange("p (b k t) -> p b k t", b=2, k=KD)
        xTlo = carve(KD * P, F16).rearrange("p (b k t) -> p b k t", b=2, k=KD)
        xn = carve(2 * D).rearrange("p (b d) -> p b d", b=2)
        xb = carve(XR * D).rearrange("p (b d) -> p b d", b=XR)
        y = carve(2 * D).rearrange("p (b d) -> p b d", b=2)
        yt = carve(2 * D).rearrange("p (b d) -> p b d", b=2)

        G = carve(4 * NC).rearrange("p (g k) -> p g k", g=4)
        Y4 = carve(4 * NC).rearrange("p (g k) -> p g k", g=4)
        W2 = carve(2 * NC).rearrange("p (g k) -> p g k", g=2)
        E2 = carve(3 * NC).rearrange("p (g k) -> p g k", g=3)
        flags, flagsT = carve(32), carve(32)

        taken[0] = 0
        def as_stack(a):
            return a.bitcast(F16).rearrange("p (w h t) -> p w h t", w=2, h=HG)

        HALF = KD * SEQ
        xnT_mem = carve(HALF)
        xnT = xnT_mem.rearrange("p (k t) -> p k t", k=KD)
        w_in = carve(KD * D).rearrange("p (k n) -> p k n", k=KD)
        wo_sb = w_in
        PT = carve(2 * HG * 512).rearrange("p (b h q) -> p b h q", b=2, h=HG)
        lat = PT.rearrange("p b h q -> p (b h q)")[:, 0:2 * SEQ].rearrange("p (l t) -> p l t", l=2)
        qk_mem = carve(2 * HALF)
        qk = qk_mem.rearrange("p (w k t) -> p w k t", w=2, k=KD)
        attT = qk[:, 0, :, :]
        parts_mem = carve(2 * HALF)
        parts = parts_mem.bitcast(F16).rearrange("p (k w l t) -> p k w l t", w=2, l=2, k=KD)
        axn = parts_mem[:, 0:2 * D].rearrange("p (b d) -> p b d", b=2)
        stacks = [as_stack(xnT_mem), as_stack(qk_mem[:, HALF:2 * HALF]), as_stack(parts_mem[:, 0:HALF])]
        V = carve(BT * D).rearrange("p (t n) -> p t n", t=BT)
        tail = taken[0]
        w_lat = carve(5 * 256).rearrange("p (k n) -> p k n", k=5)
        taken[0] = tail
        rec = carve(512)
        mrows = carve(SEQ // 2, F16)[0:2 * HG, :]
        bo = carve(D)
        flagi = sb("flagi", [P, 1], I32)
        bcols = sb("bcols", [P, 14], F32)
        ident16 = sb("ident16", [P, P], F16)
        identm = sb("identm", [P, P], F16)
        maskq = sb("maskq", [P, P], F16)
        maskk = sb("maskk", [P, P], F16)
        mx = sb("mx", [P, HG, BT, 2], F32)
        mm_ = sb("mm_", [P, HG * BT], F32)
        mrow = sb("mrow", [P, BT, HG, 2], F16)
        aln = sb("aln", [P, 2, 4], F32)
        mxq = sb("mxq", [P, 2, 8], F32)
        asc = sb("asc", [P, 16], F32)
        st6 = sb("st6", [P, 24], F32)
        ln1 = sb("ln1", [P, 2, 4], F32)
        ln2 = sb("ln2", [P, 2, 4], F32)
        wsum = sb("wsum", [P, 16], F32)
        sc = sb("sc", [P, 32], F32)
        X = sb("X", [P, 4, NC], F32)
        Bk = sb("Bk", [P, 2, 4, NC], F32)
        S = sb("S", [P, NC], F32)
        FIN = sb("FIN", [P, 8], F32)
        m8 = sb("m8", [P, 8], F32)
        e8 = sb("e8", [P, 8], F32)
        sel = sb("sel", [P, 16], F32)
        okf = sb("okf", [P, 2], F32)
        oki = sb("oki", [P, 1], I32)

        zP = pb("zP", [P, N], F32)
        hP = pb("hP", [P, 2, CW], F32)
        oP = pb("oP", [P, D], F32)
        xP = pb("xP", [P, KD * P], F32)
        ones32 = onesf[:, 0:HD]
        rowP = hP
        colP = [zP[:, j * 512:(j + 1) * 512] for j in range(4)]
        mT = hP[:, 0, :].bitcast(F16)
        mixP, sumP = oP, xP

        SC1, THR, NTHR, S1, S2, SH, SC2, SIG, T0 = (sc[:, i:i + 1] for i in range(9))

        names = ("vec_in x_in0 x_in1 x_in2 x_in3 w1_in0 w1_in1 w1_in2 w1_in3 w2_in0 w2_in1 w2_in2 w2_in3 "
                 "ones_set ident_set consts_set abs_done sum_ps sum_read tern_done sq_done scales_set search_set "
                 "stats1 xn_done rstd1 xT_ps xT_hi xT_lo z_ps z_evac z_bias upd cnt ok_set ok_sum "
                 "h_set hT_ps hT_hi hT_lo mm2 out_ps y_set stats2 rstd2 yn_set x_new xb_set out_done "
                 "consts2 ch_dve ch_act ch_pool phase "
                 "aw_in ab_in a_stats a_rstd a_xn a_turn a_xT p_ps p_out p_max q_max q_scale split_hi split_lo wo_in bo_in "
                 "stq0 stq1 stq2 stq3 stk0 stk1 stk2 stk3 stack1 stack2 stack3 sum_out mix_out rec_set unit_set mrow_in row_ps row_max m_set mT_ps m_rows col_ps exp_done mix_done norm_set "
                 "o_ps x_att masks bo_added attn_set")
        sm = {n: sem(n) for n in names.split()}

        block = ctx.enter_context(nc.Block())
        slots = range(-1, NT + S_FIN + 1)

        ORDER = core_order()

        def seen(kind, upto, g=None):
            return sum(1 for e in ORDER[:upto] if e[0] == kind)

        ITEMS = [(kind, j, tc) for tc in range(2) for kind, js in (("in", range(4)), ("up", range(6))) for j in js]
        ITEMS += [("val", i, 0) for i in range(BT)]

        TOTAL = {k: seen(k, len(ORDER)) for k in ("row", "max", "turn", "col", "mix", "norm", "rec")}
        IN_DONE = max(n for n, e in enumerate(ITEMS) if e[0] == "in") + 1
        STACK_OF = (0, 1, 2, 0)
        SPLITS = [(k, w) for k in range(KD) for w in range(2)]

        def wait_stack(eng, b, g, heads=range(HG)):
            if g:
                eng.wait_ge(sm[f"stack{g}"], 16 * 6 * HG * (b + 1))
            else:
                for h in heads:
                    eng.wait_ge(sm[f"stq{h}"], 16 * 3 * (b + 1))
                    eng.wait_ge(sm[f"stk{h}"], 16 * 3 * (b + 1))

        def load_stack(eng, b, g, w):
            if g == 0:
                eng.wait_ge(sm["split_hi"], 8 * b + 2)
                eng.wait_ge(sm["split_lo"], 8 * b + 2)
                eng.wait_ge(sm["p_ps"], b * len(ITEMS) + IN_DONE)
            elif g == 1:
                eng.wait_ge(sm["split_hi"], 8 * b + 8)
                eng.wait_ge(sm["split_lo"], 8 * b + 8)
            elif g == 2:
                wait_stack(eng, b, 0)
                wait_stack(eng, b, 1)
            else:
                eng.wait_ge(sm["mix_done"], b * TOTAL["mix"] + TOTAL["mix"] // GROUPS)
            for h in range(HG):
                done = sm[f"st{'qk'[w]}{h}" if g == 0 else f"stack{g}"]
                for j, part in enumerate(((0, 0, 1), (0, 1, 0))[w]):
                    eng.dma_start(stacks[STACK_OF[g]][HD * j:HD * (j + 1), w, h, :],
                                  parts[HD * h:HD * (h + 1), g, w, part, :]).then_inc(done, 16)

        def barrier(eng, k):
            eng.drain().then_inc(sm["phase"], 1)
            eng.wait_ge(sm["phase"], 5 * k)

        def at(s, off):
            i = s - off
            return i if 0 <= i < NT else None

        def do(stage, f, s, off, *a):
            i = at(s, off)
            if i is not None:
                stage(f, i, *a)

        FIRST_UPD, LAST_UPD = 3, NT + S_SEL - 1

        def updates(f, s):
            return f * (LAST_UPD - FIRST_UPD + 1) + s - FIRST_UPD + 1

        @block.sync
        def _(eng):
            xv = x.rearrange("(t p) d -> p t d", p=P)
            for c in range(4):
                eng.dma_start(Z[:, c, :], w_synT[c * P:(c + 1) * P, :]).then_inc(sm[f"w1_in{c}"], 16)
                if c == 0:
                    eng.dma_start(x_sb[:, 0:4, :], xv[:, 0:4, :]).then_inc(sm["x_in0"], 16)
            for v, d in ((b_syn, bsyn), (b_out, bout), (gamma, gam), (beta, bet)):
                eng.dma_start(d[:, :], v.partition_broadcast(P)).then_inc(sm["vec_in"], 16)
            w2v = w_outT.rearrange("(k p) o -> p k o", p=P)
            for c in range(4):
                eng.dma_start(Z[:, 4 + c, :].rearrange("p (k o) -> p k o", o=D),
                              w2v[:, 4 * c:4 * c + 4, :]).then_inc(sm[f"w2_in{c}"], 16)
            for c in range(1, 4):
                eng.dma_start(x_sb[:, 4 * c:4 * c + 4, :], xv[:, 4 * c:4 * c + 4, :]).then_inc(sm[f"x_in{c}"], 16)
            barrier(eng, 1)
            for b in range(2):
                for k in range(KD):
                    for w, lo in ((w_kv, 0), (w_q, 128), (w_kr, 256)):
                        eng.dma_start(w_in[:, k, lo:lo + w.shape[1]], w[k * P:(k + 1) * P, :]).then_inc(sm["aw_in"], 16)
                for k, w in ((0, w_ku), (1, w_qu), (2, w_qr), (3, w_vu)):
                    eng.dma_start(w_lat[:, k:k + w.shape[1] // 256, :].rearrange("p k n -> p (k n)"), w)\
                        .then_inc(sm["aw_in"], 16)
                if b == 0:
                    eng.dma_start(bcols[:, :], b_cols).then_inc(sm["ab_in"], 16)

                def max_rows(g):
                    eng.wait_ge(sm["m_rows"], b * GROUPS + g + 1)
                    for h in range(HG):
                        eng.dma_start(stacks[STACK_OF[g]][3 * HD:3 * HD + 2, 0, h, :], mrows[2 * h:2 * h + 2, :])\
                            .then_inc(sm["mrow_in"], 16)

                load_stack(eng, b, 0, 0)
                load_stack(eng, b, 1, 0)
                load_stack(eng, b, 1, 1)
                eng.dma_start(wo_sb, w_o.rearrange("(k p) n -> p k n", p=P)).then_inc(sm["wo_in"], 16)
                eng.wait_ge(sm["p_ps"], (b + 1) * len(ITEMS))
                eng.dma_start(bo, b_o.partition_broadcast(P)).then_inc(sm["bo_in"], 16)
                for g in range(GROUPS):
                    max_rows(g)
                    if 0 < g + 2 < GROUPS:
                        load_stack(eng, b, g + 2, 0)
                        load_stack(eng, b, g + 2, 1)
                barrier(eng, 2 + b)
            ov = out.rearrange("(t p) d -> p t d", p=P)
            for i in range(NT):
                eng.wait_ge(sm["x_new"], (NF - 1) * NT + i + 1)
                eng.dma_start(ov[:, i, :], x_sb[:, i, :]).then_inc(sm["out_done"], 16)
            eng.wait_ge(sm["out_done"], 16 * NT)

        @block.tensor
        def _(pe):
            def partition_sum(out_, in_, ready, value):
                pe.wait_ge(sm[ready], value)
                pe.matmul(out_, onesf[:, :], in_, start=True, stop=True).then_inc(sm["sum_ps"], 1)

            pe.wait_ge(sm["ones_set"], 1)
            pe.wait_ge(sm["ident_set"], 2)
            partition_sum(xP[:, 0:4], wsum[:, 0:4], "abs_done", 4)
            pe.wait_ge(sm["sum_read"], 1)

            def x_turn(f, i):
                g = f * NT + i
                pe.wait_ge(sm["xn_done"], g + 1)
                if g:
                    pe.wait_ge(sm["xT_lo"], g)
                for k in range(KD):
                    mm = pe.transpose(xP[:, k * P:(k + 1) * P], xn[:, g % 2, k * P:(k + 1) * P], identf[:, :])
                mm.then_inc(sm["xT_ps"], 1)

            def mm1(f, i, c):
                g = f * NT + i
                if c == 0:
                    pe.wait_ge(sm["xT_lo"], g + 1)
                    pe.wait_ge(sm["tern_done"], 4)
                if g:
                    pe.wait_ge(sm["z_evac"], 4 * (g - 1) + c + 1)
                for n, part in enumerate((xThi, xTlo)):
                    for k in range(KD):
                        mm = pe.matmul(zP[:, c * CW:(c + 1) * CW], part[:, g % 2, k, :], T1[:, k, c * CW:(c + 1) * CW],
                                       start=(n == 0 and k == 0), stop=(n == 1 and k == KD - 1))
                mm.then_inc(sm["z_ps"], 1)

            def h_turn(f, i, c):
                g = f * NT + i
                if c == 0:
                    pe.wait_ge(sm["h_set"], g + 1)
                q = 4 * g + c
                if q >= 2:
                    pe.wait_ge(sm["hT_lo"], q - 1)
                for k in range(4):
                    n0 = c * CW + k * P
                    mm = pe.transpose(hP[:, c % 2, k * P:(k + 1) * P], Z[:, g % ZR, n0:n0 + P], identf[:, :])
                mm.then_inc(sm["hT_ps"], 1)

            def mm2(f, i, c):
                g = f * NT + i
                pe.wait_ge(sm["hT_lo"], 4 * g + c + 1)
                if c == 0:
                    pe.wait_ge(sm["tern_done"], 8)
                    pe.wait_ge(sm["sum_read"], 3)
                    if g:
                        pe.wait_ge(sm["y_set"], g)
                for n, part in enumerate((hThi, hTlo)):
                    for k in range(4 * c, 4 * c + 4):
                        mm = pe.matmul(oP[:, :], part[:, k, :], T2[:, k, :],
                                       start=(c == 0 and n == 0 and k == 0), stop=(c == 3 and n == 1 and k == KN - 1))
                mm.then_inc(sm["mm2"], 1)

            def project(b):
                for i in range(BT):
                    g = b * BT + i
                    pe.wait_ge(sm["a_xn"], g + 1)
                    if g >= 2:
                        pe.wait_ge(sm["a_xT"], g - 1)
                    for k in range(KD):
                        mm = pe.transpose(hP[:, i % 2, k * P:(k + 1) * P], axn[:, g % 2, k * P:(k + 1) * P], identf[:, :])
                    mm.then_inc(sm["a_turn"], 1)
                pe.wait_ge(sm["aw_in"], 16 * 16 * (b + 1))
                for n, (kind, j, tc) in enumerate(ITEMS):
                    g = b * len(ITEMS) + n
                    if g >= 4:
                        pe.wait_ge(sm["p_out"], g - 3)
                    o = zP[:, n % 4 * 512:(n % 4 + 1) * 512]
                    tok = slice(tc * 512, (tc + 1) * 512)
                    if kind == "in":
                        pe.wait_ge(sm["a_xT"], b * BT + 4 * (tc + 1))
                        for k in range(KD):
                            mm = pe.matmul(o, w_in[:, k, j * P:(j + 1) * P], xnT[:, k, tok],
                                           start=(k == 0), stop=(k == KD - 1))
                    elif kind == "up":
                        src = 0 if j < 2 else 1
                        pe.wait_ge(sm["p_out"], b * len(ITEMS) + ITEMS.index(("in", src, tc)) + 1)
                        mm = pe.matmul(o, w_lat[:, j // 2, (j % 2) * P:(j % 2 + 1) * P], lat[:, src, tok],
                                       start=True, stop=True)
                    else:
                        mm = pe.matmul(o, lat[:, 0, j * P:(j + 1) * P],
                                       w_lat[:, 3:5, :].rearrange("p k n -> p (k n)"), start=True, stop=True)
                    mm.then_inc(sm["p_ps"], 1)

            def core(b):
                n = {k: b * v for k, v in TOTAL.items()}
                for e in ORDER:
                    kind, g = e[:2]
                    stack = stacks[STACK_OF[g]]
                    m = n[kind]
                    n[kind] += 1
                    if kind == "row":
                        h, t, c = e[2:]
                        if g == 0 and (t, c) == (0, 0):
                            wait_stack(pe, b, g, [h])
                        if (h, t, c) == (0, 0, 0):
                            if g:
                                wait_stack(pe, b, g)
                            pe.wait_ge(sm["masks"], 2)
                            if g:
                                pe.wait_ge(sm["m_rows"], b * GROUPS + g)
                        if m >= 2:
                            pe.wait_ge(sm["row_max"], m - 1)
                        w = min(512, (t + 1) * P - 512 * c)
                        own = c == t // 4
                        mm = pe.matmul(rowP[:, m % 2, 0:w], stack[0:3 * HD, 0, h, t * P:(t + 1) * P],
                                       stack[0:3 * HD, 1, h, 512 * c:512 * c + w], start=True, stop=not own)
                        if own:
                            mm = pe.matmul(rowP[:, m % 2, w - P:w], identm[:, :], maskq[:, :], start=False, stop=True)
                        mm.then_inc(sm["row_ps"], 1)
                    elif kind == "turn":
                        pe.wait_ge(sm["m_set"], m + 1)
                        if m:
                            pe.wait_ge(sm["m_rows"], m)
                        for t in range(BT):
                            mm = pe.transpose(mT[0:2 * HG, t * P:(t + 1) * P],
                                              mrow[:, t, :, :].rearrange("p h l -> p (h l)"), ident16[:, :])
                        mm.then_inc(sm["mT_ps"], 1)
                    elif kind == "col":
                        qc, kb, h = e[2:]
                        if (qc, kb, h) == (0, 0, 0):
                            pe.wait_ge(sm["mrow_in"], 16 * HG * (GROUPS * b + g + 1))
                            pe.wait_ge(sm["unit_set"], 3 * b + min(g, 2) + 1)
                            pe.wait_ge(sm["p_out"], (b + 1) * len(ITEMS))
                        if m >= 4:
                            pe.wait_ge(sm["exp_done"], m - 3)
                        q0 = max(0, kb * P - qc * 512)
                        own = kb * P >= qc * 512
                        mm = pe.matmul(colP[m % 4][:, q0:512], stack[0:3 * HD + 2, 1, h, kb * P:(kb + 1) * P],
                                       stack[0:3 * HD + 2, 0, h, qc * 512 + q0:(qc + 1) * 512],
                                       start=True, stop=not own)
                        if own:
                            mm = pe.matmul(colP[m % 4][:, q0:q0 + P], identm[:, :], maskk[:, :], start=False, stop=True)
                        mm.then_inc(sm["col_ps"], 1)
                    elif kind == "mix":
                        qc, kb = e[2:]
                        pe.wait_ge(sm["exp_done"], 4 * (m + 1))
                        if kb == 0 and n["norm"]:
                            pe.wait_ge(sm["mix_out"], n["norm"])
                            pe.wait_ge(sm["sum_out"], n["norm"])
                        q0 = max(0, kb * P - qc * 512)
                        last = kb == 4 * qc + 3
                        for dst, own_v in ((mixP, True), (sumP, False)):
                            for h in range(HG):
                                v = V[:, kb, g * P + h * HD:g * P + (h + 1) * HD] if own_v else ones32
                                mm = pe.matmul(dst[h * HD:(h + 1) * HD, q0:512], v, PT[:, m % 2, h, q0:512],
                                               start=(kb == 0), stop=last, tile_position=(0, h * HD),
                                               skip_group_check=True)
                        mm.then_inc(sm["mix_done"], 1)
                pe.wait_ge(sm["attn_set"], (b + 1) * TOTAL["norm"])
                pe.wait_ge(sm["wo_in"], 16 * (b + 1))
                pe.wait_ge(sm["exp_done"], (b + 1) * TOTAL["col"])
                pe.wait_ge(sm["m_rows"], (b + 1) * GROUPS)
                for i in range(BT):
                    g = b * BT + i
                    if i >= 4:
                        pe.wait_ge(sm["x_att"], g - 3)
                    for k in range(KD):
                        mm = pe.matmul(zP[:, i % 4 * 512:(i % 4 + 1) * 512], attT[:, k, i * P:(i + 1) * P], wo_sb[:, k, :],
                                       start=(k == 0), stop=(k == KD - 1))
                    mm.then_inc(sm["o_ps"], 1)

            for f in range(NF):
                for s in slots:
                    for c in range(4):
                        do(mm1, f, s, 1, c)
                        do(h_turn, f, s, S_OUT, c)
                        if c == 0:
                            do(x_turn, f, s, 0)
                        if c < 2:
                            do(mm2, f, s, S_OUT + 1, c + 2)
                        else:
                            do(mm2, f, s, S_OUT, c - 2)
                    if f == 0 and s == 0:
                        partition_sum(oP[:, 0:4], wsum[:, 4:8], "abs_done", 8)
                        pe.wait_ge(sm["sum_read"], 2)
                        partition_sum(oP[:, 0:1], wsum[:, 8:9], "sq_done", 1)
                if f == 0:
                    barrier(pe, 1)
                    for b in range(2):
                        project(b)
                        core(b)
                        barrier(pe, 2 + b)

        @block.scalar
        def _(act):
            for n in range(2):
                for c in range(4):
                    act.wait_ge(sm[f"w{n + 1}_in{c}"], 16)
                    if n or c:
                        act.wait_ge(sm["abs_done"], 4 * n + c)
                    act.activation(junk[:, 0, :], Z[:, 4 * n + c, :], ACT.Abs,
                                   accum_out=wsum[:, 4 * n + c:4 * n + c + 1]).then_inc(sm["abs_done"], 1)
            act.wait_ge(sm["tern_done"], 1)
            act.wait_ge(sm["abs_done"], 8)
            act.activation(junk[:, 0, :], T1[:, 0, :], ACT.Square, accum_out=wsum[:, 8:9]).then_inc(sm["sq_done"], 1)
            act.wait_ge(sm["scales_set"], 1)
            act.wait_ge(sm["sq_done"], 1)

            def evac(f, i, c):
                g = f * NT + i
                act.wait_ge(sm["z_ps"], 4 * g + c + 1)
                if g >= ZR and c == 0:
                    act.wait_ge(sm["hT_ps"], 4 * (g - ZR) + 4)
                if g < 8 and c == 0:
                    act.wait_ge(sm["tern_done"], 4 if g < 4 else 8)
                act.activation(Z[:, g % ZR, c * CW:(c + 1) * CW], zP[:, c * CW:(c + 1) * CW], ACT.Copy,
                               scale=SC1).then_inc(sm["z_evac"], 1)

            def h_hi(f, i, c):
                g = f * NT + i
                act.wait_ge(sm["hT_ps"], 4 * g + c + 1)
                if g:
                    act.wait_ge(sm["mm2"], 4 * (g - 1) + c + 1)
                else:
                    act.wait_ge(sm["scales_set"], 2)
                act.activation(hThi[:, 4 * c:4 * c + 4, :].rearrange("p k t -> p (k t)"), hP[:, c % 2, :], ACT.Copy,
                               scale=SH).then_inc(sm["hT_hi"], 1)

            def x_hi(f, i):
                g = f * NT + i
                act.wait_ge(sm["xT_ps"], g + 1)
                if g >= 2:
                    act.wait_ge(sm["z_ps"], 4 * (g - 2) + 4)
                act.activation(xThi[:, g % 2, :, :].rearrange("p k t -> p (k t)"), xP[:, :], ACT.Copy,
                               scale=XSCALE).then_inc(sm["xT_hi"], 1)

            counted = [0]

            def count(f, s, k):
                i = at(s, 2 + k)
                if i is None:
                    return
                g = f * NT + i
                if k == 0:
                    act.wait_ge(sm["search_set"], 1)
                    act.wait_ge(sm["z_bias"], 4 * g + 4)
                if s >= FIRST_UPD:
                    act.wait_ge(sm["upd"], updates(f, s))
                elif f:
                    act.wait_ge(sm["upd"], updates(f - 1, LAST_UPD))
                if counted[0] >= 2:
                    act.wait_ge(sm["cnt"], counted[0] - 1)
                act.activation(junk[:, counted[0] % 2, :], Z[:, g % ZR, :], ACT.Sign, bias=X[:, 2, k:k + 1],
                               accum_out=S[:, k:k + 1]).then_inc(sm["cnt"], 1)
                counted[0] += 1

            def project(b):
                for i in range(BT):
                    g = b * BT + i
                    act.wait_ge(sm["a_turn"], g + 1)
                    act.activation(xnT[:, :, i * P:(i + 1) * P], hP[:, i % 2, :].rearrange("p (k t) -> p k t", k=KD),
                                   ACT.Copy).then_inc(sm["a_xT"], 1)
                if b == 0:
                    act.wait_ge(sm["ab_in"], 16)
                def split_hi(n):
                    k, w = SPLITS[n]
                    if n == 0:
                        act.wait_ge(sm["q_scale"], b + 1)
                    act.activation(parts[:, k, w, 0, :], qk[:, w, k, :], ACT.Copy, scale=asc[:, 8 + w:9 + w])\
                        .then_inc(sm["split_hi"], 1)

                split = 0
                for n, (kind, j, tc) in enumerate(ITEMS):
                    if kind == "val" and j >= 4:
                        for _ in range(2):
                            split_hi(split)
                            split += 1
                    g = b * len(ITEMS) + n
                    act.wait_ge(sm["p_ps"], g + 1)
                    o = zP[:, n % 4 * 512:(n % 4 + 1) * 512]
                    tok = slice(tc * 512, (tc + 1) * 512)
                    if kind == "val":
                        act.activation(V[:, j, :], o, ACT.Copy).then_inc(sm["p_out"], 1)
                        continue
                    if kind == "in":
                        dst, col = (lat[:, j, tok], j) if j < 2 else (qk[:, 1, j, tok], j)
                    else:
                        dst, col = (qk[:, 1, j, tok], 4 + j) if j < 2 else (qk[:, 0, j - 2, tok], 4 + j)
                    act.activation(dst, o, ACT.Identity, bias=bcols[:, col:col + 1]).then_inc(sm["p_out"], 1)

            def core(b):
                n = {k: b * v for k, v in TOTAL.items()}
                for e in ORDER:
                    kind, g = e[:2]
                    m = n[kind]
                    n[kind] += 1
                    if kind == "col":
                        qc, kb, h = e[2:]
                        act.wait_ge(sm["col_ps"], m + 1)
                        if m // 4 >= 2:
                            act.wait_ge(sm["mix_done"], m // 4 - 1)
                        q0 = max(0, kb * P - qc * 512)
                        act.activation(PT[:, m // 4 % 2, h, q0:512], colP[m % 4][:, q0:512], ACT.Exp,
                                       scale=asc[:, 10:11]).then_inc(sm["exp_done"], 1)
                    elif kind == "norm":
                        act.wait_ge(sm["mix_done"], n["mix"])
                        if m:
                            act.wait_ge(sm["attn_set"], m)
                        act.activation(rec, sumP[:, :], ACT.Copy).then_inc(sm["sum_out"], 1)
                    elif kind == "turn":
                        act.wait_ge(sm["mT_ps"], m + 1)
                        if not g:
                            act.wait_ge(sm["p_ps"], (b + 1) * len(ITEMS))
                        if m:
                            act.wait_ge(sm["mrow_in"], 16 * HG * m)
                        act.activation(mrows, mT[0:2 * HG, :], ACT.Copy).then_inc(sm["m_rows"], 1)

            for f in range(NF):
                for s in slots:
                    do(evac, f, s, 2, 3)
                    do(h_hi, f, s, S_OUT + 1, 3)
                    do(evac, f, s, 1, 0)
                    do(h_hi, f, s, S_OUT, 0)
                    do(x_hi, f, s, 0)
                    count(f, s, 4)
                    count(f, s, 3)
                    do(evac, f, s, 1, 1)
                    do(h_hi, f, s, S_OUT, 1)
                    count(f, s, 2)
                    count(f, s, 1)
                    do(evac, f, s, 1, 2)
                    do(h_hi, f, s, S_OUT, 2)
                    count(f, s, 0)
                if f == 0:
                    barrier(act, 1)
                    for b in range(2):
                        project(b)
                        core(b)
                        barrier(act, 2 + b)

        def counts_before(f, s):
            per_f = NC * NT
            return f * per_f + sum(1 for t in range(-1, s) for k in range(NC) if at(t, 2 + k) is not None)

        @block.gpsimd
        def _(pool):
            n = [0]

            def link(ins):
                n[0] += 1
                ins.then_inc(sm["ch_pool"], 1)
                pool.wait_ge(sm["ch_pool"], n[0])

            pool.memset(onesf[:, :], 1.0).then_inc(sm["ones_set"], 1)
            pool.memset(identf[:, :], 0.0).then_inc(sm["ident_set"], 1)
            pool.wait_ge(sm["ident_set"], 1)
            pool.affine_select(out=identf[:, :], in_=identf[:, :], compare_op=ALU.not_equal, fill=1.0, base=0,
                               pattern=[[-1, P]], channel_multiplier=1).then_inc(sm["ident_set"], 1)
            pool.wait_ge(sm["ident_set"], 2)
            link(pool.tensor_copy(ident16[:, :], identf[:, :]))
            link(pool.tensor_scalar(identm[:, :], identf[:, :], MASK, None, ALU.mult))
            link(pool.memset(maskq[:, :], 0.0))
            link(pool.memset(maskk[:, :], 0.0))
            pool.affine_select(out=maskq[:, :], in_=maskq[:, :], compare_op=ALU.is_ge, fill=-MASK, base=0,
                               pattern=[[-1, P]], channel_multiplier=1).then_inc(sm["masks"], 1)
            pool.affine_select(out=maskk[:, :], in_=maskk[:, :], compare_op=ALU.is_ge, fill=-MASK, base=0,
                               pattern=[[1, P]], channel_multiplier=-1).then_inc(sm["masks"], 1)
            link(pool.memset(nhalf[:, :], -0.5))
            link(pool.memset(half[:, :], 0.5))
            for k in range(8):
                pool.memset(iota8[:, k:k + 1], float(k)).then_inc(sm["consts_set"], 1)
                pool.wait_ge(sm["consts_set"], k + 1)
            def rstd1(f, i):
                g = f * NT + i
                pool.wait_ge(sm["stats1"], g + 1)
                link(pool.tensor_scalar(ln1[:, g % 2, 2:3], ln1[:, g % 2, 1:2], EPS, None, ALU.add))
                pool.tensor_tensor(ln1[:, g % 2, 3:4], ln1[:, g % 2, 2:3], nhalf[:, :], ALU.pow)\
                    .then_inc(sm["rstd1"], 1)

            def xbias(f, i):
                g = f * NT + i
                pool.wait_ge(sm["xn_done"], g + 1)
                if g == 0:
                    pool.wait_ge(sm["vec_in"], 64)
                if g >= XR:
                    pool.wait_ge(sm["y_set"], g - XR + 1)
                pool.tensor_tensor(xb[:, g % XR, :], xn[:, g % 2, :], bout[:, :], ALU.add).then_inc(sm["xb_set"], 1)

            def bias(f, i, c):
                g = f * NT + i
                pool.wait_ge(sm["z_evac"], 4 * g + c + 1)
                zz = Z[:, g % ZR, c * CW:(c + 1) * CW]
                pool.tensor_tensor(zz, zz, bsyn[:, c * CW:(c + 1) * CW], ALU.add).then_inc(sm["z_bias"], 1)

            def ok_sum(f, i):
                g = f * NT + i
                pool.wait_ge(sm["ok_set"], g + 1)
                link(pool.partition_all_reduce(okf[:, 1:2], okf[:, 0:1], P, bass.bass_isa.ReduceOp.add))
                pool.tensor_copy(oki[:, :], okf[:, 1:2]).then_inc(sm["ok_sum"], 1)

            def rstd2(f, i):
                g = f * NT + i
                pool.wait_ge(sm["stats2"], g + 1)
                link(pool.tensor_scalar(ln2[:, g % 2, 2:3], ln2[:, g % 2, 1:2], EPS, None, ALU.add))
                pool.tensor_tensor(ln2[:, g % 2, 3:4], ln2[:, g % 2, 2:3], nhalf[:, :], ALU.pow)\
                    .then_inc(sm["rstd2"], 1)

            def final(f, i):
                g = f * NT + i
                link(pool.tensor_tensor(x_sb[:, i, :], x_sb[:, i, :], bet[:, :], ALU.add))
                pool.wait_ge(sm["yn_set"], g + 1)
                link(pool.tensor_tensor(yt[:, g % 2, :], yt[:, g % 2, :], gam[:, :], ALU.mult))
                pool.tensor_tensor(x_sb[:, i, :], x_sb[:, i, :], yt[:, g % 2, :], ALU.add).then_inc(sm["x_new"], 1)

            def project(b):
                for i in range(BT):
                    g = b * BT + i
                    pool.wait_ge(sm["a_stats"], g + 1)
                    link(pool.tensor_scalar(aln[:, g % 2, 2:3], aln[:, g % 2, 1:2], EPS, None, ALU.add))
                    pool.tensor_tensor(aln[:, g % 2, 3:4], aln[:, g % 2, 2:3], nhalf[:, :], ALU.pow)\
                        .then_inc(sm["a_rstd"], 1)
                pool.wait_ge(sm["p_max"], b + 1)
                pool.partition_all_reduce(asc[:, 2:4], asc[:, 0:2], P, bass.bass_isa.ReduceOp.max).then_inc(sm["q_max"], 1)

            def core(b):
                pool.wait_ge(sm["q_max"], b + 1)
                load_stack(pool, b, 0, 1)
                for g in range(3):
                    if g == 1:
                        pool.wait_ge(sm["split_hi"], 8 * b + 8)
                        pool.wait_ge(sm["split_lo"], 8 * b + 8)
                    elif g == 2:
                        wait_stack(pool, b, 0)
                        wait_stack(pool, b, 1)
                    pool.memset(stacks[g][3 * HD:3 * HD + 2, 1, :, :], MUNIT).then_inc(sm["unit_set"], 1)
                    pool.wait_ge(sm["unit_set"], 3 * b + g + 1)
                pool.wait_ge(sm["bo_in"], 16 * (b + 1))
                pool.wait_ge(sm["a_xn"], (b + 1) * BT)
                for i in range(BT):
                    t = x_sb[:, b * BT + i, :]
                    pool.tensor_tensor(t, t, bo, ALU.add).then_inc(sm["bo_added"], 1)
                for m in range(TOTAL["norm"]):
                    g, qc = m // 2, m % 2
                    a = attT[:, g, qc * 512:(qc + 1) * 512]
                    pool.wait_ge(sm["mix_out"], b * TOTAL["norm"] + m + 1)
                    pool.wait_ge(sm["rec_set"], 4 * (b * TOTAL["norm"] + m + 1))
                    link(pool.tensor_tensor(a, a, rec, ALU.mult))
                    pool.tensor_scalar(a, a, bcols[:, 10 + g:11 + g], None, ALU.add).then_inc(sm["attn_set"], 1)

            for f in range(NF):
                for s in slots:
                    do(bias, f, s, 2, 3)
                    do(xbias, f, s, 0)
                    do(bias, f, s, 1, 0)
                    do(final, f, s, S_FIN + 1)
                    do(bias, f, s, 1, 1)
                    do(ok_sum, f, s, S_SEL)
                    do(rstd2, f, s, S_FIN)
                    do(rstd1, f, s, -1)
                    do(bias, f, s, 1, 2)
                    if f == 0 and s == 0:
                        pool.wait_ge(sm["scales_set"], 3)
                        pool.tensor_tensor(SIG, sc[:, 16:17], half[:, :], ALU.pow).then_inc(sm["scales_set"], 1)
                        link(pool.tensor_scalar(gam[:, :], gam[:, :], 0.5, None, ALU.mult))
                        link(pool.tensor_scalar(bet[:, :], bet[:, :], 0.5, None, ALU.mult))
                if f == 0:
                    barrier(pool, 1)
                    for b in range(2):
                        project(b)
                        core(b)
                        barrier(pool, 2 + b)

        @block.vector
        def _(dve):
            n = [0]

            def link(ins):
                n[0] += 1
                ins.then_inc(sm["ch_dve"], 1)
                dve.wait_ge(sm["ch_dve"], n[0])

            def ternary(m, c):
                w = Z[:, 4 * m + c, :]
                low = M[:, 0:N // 2].bitcast(F16) if c % 2 else M[:, N // 2:N].bitcast(F16)
                link(dve.tensor_scalar(low, w, NTHR, None, ALU.is_lt))
                o = T1[:, c, :] if m == 0 else T2[:, 4 * c:4 * c + 4, :].rearrange("p k o -> p (k o)")
                dve.scalar_tensor_tensor(o, w, THR, low, ALU.is_gt, ALU.subtract).then_inc(sm["tern_done"], 1)
                dve.wait_ge(sm["tern_done"], 4 * m + c + 1)

            def scale_of(m, dst):
                dve.wait_ge(sm["sum_ps"], m + 1)
                dve.tensor_reduce(sc[:, 12 + m:13 + m], (xP, oP)[m][:, 0:4], AX.X, ALU.add).then_inc(sm["sum_read"], 1)
                dve.wait_ge(sm["sum_read"], m + 1)
                link(dve.tensor_scalar(dst, sc[:, 12 + m:13 + m], 1.0 / (N * D), None, ALU.mult))
                link(dve.tensor_scalar(THR, dst, 1e-8, 0.5, ALU.add, ALU.mult))
                link(dve.tensor_scalar(NTHR, THR, -1.0, None, ALU.mult))

            def constants():
                scale_of(1, S2)
                dve.wait_ge(sm["consts_set"], 8)
                dve.wait_ge(sm["vec_in"], 64)
                link(dve.tensor_reduce(sc[:, 17:18], bsyn[:, :], AX.X, ALU.max, apply_absolute_value=True))
                link(dve.scalar_tensor_tensor(sc[:, 18:19], S1, float(D), sc[:, 17:18], ALU.mult, ALU.add))
                link(dve.tensor_scalar(sc[:, 18:19], sc[:, 18:19], 1e-30, None, ALU.max))
                link(dve.tensor_scalar(sc[:, 19:20].bitcast(I32), sc[:, 18:19].bitcast(I32), 0x7F800000, None,
                                       ALU.bitwise_and))
                link(dve.reciprocal(sc[:, 20:21], sc[:, 19:20]))
                link(dve.tensor_scalar(SH, sc[:, 20:21], HTOP, None, ALU.mult))
                dve.scalar_tensor_tensor(SC2, S2, 1.0 / HTOP, sc[:, 19:20], ALU.mult, ALU.mult)\
                    .then_inc(sm["scales_set"], 1)
                dve.wait_ge(sm["stats1"], 2)
                for c in range(4):
                    link(dve.bn_stats(st6[:, 6 * c:6 * c + 6], bsyn[:, c * CW:(c + 1) * CW]))
                link(dve.bn_aggr(sc[:, 21:23], st6[:, :]))
                dve.wait_ge(sm["sum_ps"], 3)
                dve.tensor_scalar(sc[:, 23:24], oP[:, 0:1], float(D) / (P * N), None, ALU.mult).then_inc(sm["sum_read"], 1)
                dve.wait_ge(sm["sum_read"], 3)
                link(dve.tensor_tensor(sc[:, 24:25], S1, S1, ALU.mult))
                dve.scalar_tensor_tensor(sc[:, 16:17], sc[:, 24:25], sc[:, 23:24], sc[:, 22:23], ALU.mult, ALU.add)\
                    .then_inc(sm["scales_set"], 1)
                dve.wait_ge(sm["scales_set"], 4)
                link(dve.scalar_tensor_tensor(T0, SIG, 1.2816, sc[:, 21:22], ALU.mult, ALU.add))
                t0, sig = T0.broadcast_to([P, NC]), SIG.broadcast_to([P, NC])
                dve.memset(S[:, :], 0.0).then_inc(sm["consts2"], 1)
                dve.tensor_scalar(X[:, 0, :], t0, 1.0, None, ALU.mult).then_inc(sm["consts2"], 1)
                dve.tensor_scalar(X[:, 2, :], t0, -1.0, None, ALU.mult).then_inc(sm["consts2"], 1)
                for j in range(2):
                    dve.scalar_tensor_tensor(Bk[:, j, 0, :], sig, -0.3, t0, ALU.mult, ALU.add).then_inc(sm["consts2"], 1)
                    dve.scalar_tensor_tensor(Bk[:, j, 2, :], sig, -0.3, t0, ALU.mult, ALU.subtract)\
                        .then_inc(sm["consts2"], 1)
                dve.memset(Bk[:, :, 1, :], -248.0).then_inc(sm["consts2"], 1)
                dve.memset(Bk[:, :, 3, :], -183.0).then_inc(sm["consts2"], 1)
                dve.wait_ge(sm["consts2"], 9)
                dve.memset(sel[:, 15:16], 0.0).then_inc(sm["search_set"], 1)

            def stats1(f, i):
                g = f * NT + i
                if f == 0:
                    dve.wait_ge(sm[f"x_in{i // 4}"], 16)
                link(dve.bn_stats(st6[:, 0:6], x_sb[:, i, :]))
                if g >= 2:
                    dve.wait_ge(sm["rstd1"], g - 1)
                dve.bn_aggr(ln1[:, g % 2, 0:2], st6[:, 0:6]).then_inc(sm["stats1"], 1)

            def normal(f, i):
                g = f * NT + i
                dve.wait_ge(sm["stats1"], g + 1)
                dve.wait_ge(sm["rstd1"], g + 1)
                if g >= 2:
                    dve.wait_ge(sm["xT_ps"], g - 1)
                    dve.wait_ge(sm["xb_set"], g - 1)
                dve.tensor_scalar(xn[:, g % 2, :], x_sb[:, i, :], ln1[:, g % 2, 0:1], ln1[:, g % 2, 3:4],
                                  ALU.subtract, ALU.mult).then_inc(sm["xn_done"], 1)

            def x_lo(f, i):
                g = f * NT + i
                dve.wait_ge(sm["xT_hi"], g + 1)
                dve.scalar_tensor_tensor(xTlo[:, g % 2, :, :].rearrange("p k t -> p (k t)"), xP[:, :], XSCALE,
                                         xThi[:, g % 2, :, :].rearrange("p k t -> p (k t)"), ALU.mult,
                                         ALU.subtract).then_inc(sm["xT_lo"], 1)

            def h_lo(f, i, c):
                g = f * NT + i
                dve.wait_ge(sm["hT_hi"], 4 * g + c + 1)
                ks = slice(4 * c, 4 * c + 4)
                dve.scalar_tensor_tensor(hTlo[:, ks, :].rearrange("p k t -> p (k t)"), hP[:, c % 2, :], SH,
                                         hThi[:, ks, :].rearrange("p k t -> p (k t)"), ALU.mult,
                                         ALU.subtract).then_inc(sm["hT_lo"], 1)

            def update(f, s):
                u = updates(f, s)
                dve.wait_ge(sm["cnt"], counts_before(f, s))
                old, new = Bk[:, u % 2, :, :], Bk[:, (u + 1) % 2, :, :]
                w = NC - 1
                link(dve.tensor_scalar(X[:, 3, :], S[:, :], SSTAR, None, ALU.subtract))
                link(dve.tensor_scalar(X[:, 1, :], S[:, :], -1.0, SSTAR, ALU.mult, ALU.add))
                link(dve.tensor_copy(FIN[:, 0:4], X[:, :, NC - 1]))
                link(dve.tensor_copy(FIN[:, 4:5], old[:, 2, NC - 1:NC]))
                d = X[:, 3:4, 0:w].broadcast_to([P, 2, w])
                link(dve.tensor_scalar(G[:, 0:2, 0:w], d, 0.0, None, ALU.is_lt))
                link(dve.tensor_scalar(G[:, 2:4, 0:w], d, 0.0, None, ALU.is_ge))
                link(dve.scalar_tensor_tensor(Y4[:, :, 0:w], G[:, :, 0:w], -BIG, X[:, :, 0:w], ALU.mult, ALU.add))
                link(dve.tensor_tensor(new[:, :, 1:NC], old[:, :, 0:w], Y4[:, :, 0:w], ALU.max))
                link(dve.tensor_tensor(W2[:, :, 0:w], new[:, 0:2, 1:NC], new[:, 2:4, 1:NC], ALU.add))
                link(dve.reciprocal(E2[:, 0, 0:w], W2[:, 1, 0:w]))
                link(dve.tensor_tensor(E2[:, 1, 0:w], W2[:, 0, 0:w], new[:, 1, 1:NC], ALU.mult))
                link(dve.tensor_tensor(E2[:, 2, 0:w], E2[:, 1, 0:w], E2[:, 0, 0:w], ALU.mult))
                link(dve.tensor_tensor(X[:, 0, 1:NC], new[:, 0, 1:NC], E2[:, 2, 0:w], ALU.subtract))
                dve.tensor_tensor(X[:, 2, 1:NC], E2[:, 2, 0:w], new[:, 0, 1:NC], ALU.subtract).then_inc(sm["upd"], 1)

            TF, DF = FIN[:, 0:1], FIN[:, 3:4]
            TH, FND, IDX = sel[:, 0:1], sel[:, 1:2], sel[:, 2:3]
            OPEN, BOUND, ABOVE, HIT, TMP = (sel[:, j:j + 1] for j in range(3, 8))

            def below(f, i):
                g = f * NT + i
                link(dve.scalar_tensor_tensor(M[:, :], Z[:, g % ZR, :], TF, Z[:, g % ZR, :], ALU.is_le, ALU.mult))

            def pick(f, i):
                g = f * NT + i
                link(dve.max(m8[:, :], M[:, :]))
                link(dve.tensor_scalar(IDX, DF, -0.5, TOPK - 1 - TARGET, ALU.mult, ALU.add))
                link(dve.tensor_scalar(e8[:, :], iota8[:, :], IDX, None, ALU.is_equal, ALU.add, accum_out=FND))
                link(dve.scalar_tensor_tensor(e8[:, :], e8[:, :], 1.0, m8[:, :], ALU.mult, ALU.mult, accum_out=TH))
                if g:
                    dve.wait_ge(sm["ok_sum"], g)
                dve.scalar_tensor_tensor(okf[:, 0:1], m8[:, 0:1], TF, FND, ALU.is_lt, ALU.mult)\
                    .then_inc(sm["ok_set"], 1)

            def search_down(z):
                def step(ins):
                    dve.drain()
                    return ins

                def add_found(found, value):
                    step(dve.tensor_scalar(TMP, value, 0.0, None, ALU.max))
                    step(dve.scalar_tensor_tensor(TH, TMP, found, TH, ALU.mult, ALU.add))
                    step(dve.tensor_tensor(OPEN, OPEN, found, ALU.subtract))

                dve.drain()
                step(dve.tensor_scalar(OPEN, okf[:, 0:1], -1.0, 1.0, ALU.mult, ALU.add))
                step(dve.tensor_tensor(TH, TH, okf[:, 0:1], ALU.mult))
                step(dve.tensor_scalar(BOUND, FIN[:, 4:5], -1.0, None, ALU.mult))
                step(dve.tensor_scalar(M, z, BOUND, None, ALU.is_ge, ALU.add, accum_out=ABOVE))
                step(dve.tensor_scalar(HIT, ABOVE, float(TOPK), None, ALU.is_lt))
                step(dve.tensor_tensor(BOUND, BOUND, HIT, ALU.mult))
                step(dve.tensor_tensor(ABOVE, ABOVE, HIT, ALU.mult))
                step(dve.tensor_scalar(HIT, HIT, -3e38, 3e38, ALU.mult, ALU.add))
                step(dve.tensor_tensor(BOUND, BOUND, HIT, ALU.add))
                step(dve.memset(flags[:, :], 0.0))

                def still_open():
                    step(dve.tensor_copy(flags[:, 0:1], OPEN))
                    step(dve.transpose(flagsT[:, :], flags[:, :]))
                    step(dve.tensor_reduce(TMP, flagsT[:, :], AX.X, ALU.max))
                    step(dve.tensor_copy(flagi[:, :], TMP))
                    return sum(dve.value_load(flagi[q:q + 1, :], min_val=0, max_val=1) for q in range(0, P, 32))

                with dve.While(lambda: still_open() > 0):
                    step(dve.scalar_tensor_tensor(M, z, BOUND, z, ALU.is_lt, ALU.mult))
                    step(dve.max(m8[:, :], M))
                    step(dve.tensor_scalar(IDX, ABOVE, -1.0, TOPK - 1.0, ALU.mult, ALU.add))
                    step(dve.tensor_scalar(e8[:, :], iota8[:, :], IDX, None, ALU.is_equal, ALU.add, accum_out=HIT))
                    step(dve.scalar_tensor_tensor(e8[:, :], e8[:, :], 1.0, m8[:, :], ALU.mult, ALU.mult,
                                                  accum_out=BOUND))
                    step(dve.tensor_tensor(HIT, HIT, OPEN, ALU.mult))
                    add_found(HIT, BOUND)
                    step(dve.tensor_copy(BOUND, m8[:, 7:8]))
                    step(dve.tensor_scalar(M, z, BOUND, None, ALU.is_ge, ALU.add, accum_out=ABOVE))
                    step(dve.tensor_scalar(HIT, ABOVE, float(TOPK), None, ALU.is_ge))
                    step(dve.tensor_scalar(TMP, BOUND, 0.0, None, ALU.is_le))
                    step(dve.tensor_tensor(HIT, HIT, TMP, ALU.max))
                    step(dve.tensor_tensor(HIT, HIT, OPEN, ALU.mult))
                    add_found(HIT, BOUND)

            def keep_top(f, i):
                g = f * NT + i
                dve.wait_ge(sm["ok_sum"], g + 1)
                with dve.If(dve.value_load(oki[0:1, 0:1], min_val=0, max_val=P) < P):
                    search_down(Z[:, g % ZR, :])
                dve.scalar_tensor_tensor(Z[:, g % ZR, :], Z[:, g % ZR, :], TH, Z[:, g % ZR, :], ALU.is_ge, ALU.mult)\
                    .then_inc(sm["h_set"], 1)

            def residual(f, i):
                g = f * NT + i
                dve.wait_ge(sm["mm2"], 4 * g + 4)
                dve.wait_ge(sm["xb_set"], g + 1)
                dve.scalar_tensor_tensor(y[:, g % 2, :], oP[:, :], SC2, xb[:, g % XR, :], ALU.mult, ALU.add)\
                    .then_inc(sm["y_set"], 1)
                dve.wait_ge(sm["y_set"], g + 1)
                link(dve.bn_stats(st6[:, 6:12], y[:, g % 2, :]))
                dve.bn_aggr(ln2[:, g % 2, 0:2], st6[:, 6:12]).then_inc(sm["stats2"], 1)

            def normal2(f, i):
                g = f * NT + i
                dve.wait_ge(sm["stats2"], g + 1)
                dve.wait_ge(sm["rstd2"], g + 1)
                if g >= 2:
                    dve.wait_ge(sm["x_new"], g - 1)
                dve.tensor_scalar(yt[:, g % 2, :], y[:, g % 2, :], ln2[:, g % 2, 0:1], ln2[:, g % 2, 3:4],
                                  ALU.subtract, ALU.mult).then_inc(sm["yn_set"], 1)

            def project(b):
                def stats(i):
                    g = b * BT + i
                    raw = st6[:, 6 * (i % 2):6 * (i % 2) + 6]
                    if g:
                        dve.wait_ge(sm["a_stats"], g)
                    link(dve.bn_stats(raw, x_sb[:, g, :]))
                    if g >= 2:
                        dve.wait_ge(sm["a_rstd"], g - 1)
                        dve.wait_ge(sm["a_xn"], g - 1)
                    dve.bn_aggr(aln[:, g % 2, 0:2], raw).then_inc(sm["a_stats"], 1)

                stats(0)
                for i in range(BT):
                    g = b * BT + i
                    if i + 1 < BT:
                        stats(i + 1)
                    dve.wait_ge(sm["a_rstd"], g + 1)
                    dve.wait_ge(sm["a_stats"], g + 1)
                    if g >= 2:
                        dve.wait_ge(sm["a_turn"], g - 1)
                    dve.tensor_scalar(axn[:, g % 2, :], x_sb[:, g, :], aln[:, g % 2, 0:1], aln[:, g % 2, 3:4],
                                      ALU.subtract, ALU.mult).then_inc(sm["a_xn"], 1)
                seen_w = [0, 0]
                for n, (kind, j, tc) in enumerate(ITEMS):
                    if kind == "val" or (kind == "in" and j < 2):
                        continue
                    dve.wait_ge(sm["p_out"], b * len(ITEMS) + n + 1)
                    w, k = (1, j) if kind == "in" or j < 2 else (0, j - 2)
                    link(dve.tensor_reduce(mxq[:, w, seen_w[w]:seen_w[w] + 1], qk[:, w, k, tc * 512:(tc + 1) * 512],
                                           AX.X, ALU.max, apply_absolute_value=True))
                    seen_w[w] += 1
                dve.tensor_reduce(asc[:, 0:2], mxq[:, :, :], AX.X, ALU.max).then_inc(sm["p_max"], 1)
                dve.wait_ge(sm["q_max"], b + 1)
                link(dve.tensor_scalar(asc[:, 4:6].bitcast(I32), asc[:, 2:4].bitcast(I32), 0x7F800000, None,
                                       ALU.bitwise_and))
                link(dve.tensor_scalar(asc[:, 4:6], asc[:, 4:6], 0.5, None, ALU.max))
                link(dve.reciprocal(asc[:, 6:8], asc[:, 4:6]))
                link(dve.tensor_tensor(asc[:, 11:12], asc[:, 4:5], asc[:, 5:6], ALU.mult))
                link(dve.tensor_scalar(asc[:, 10:11], asc[:, 11:12], ATT_SCALE / 16384.0, None, ALU.mult))
                dve.tensor_scalar(asc[:, 8:10], asc[:, 6:8], 128.0, None, ALU.mult).then_inc(sm["q_scale"], 1)
                dve.wait_ge(sm["q_scale"], b + 1)
                for n, (k, w) in enumerate(SPLITS):
                    dve.wait_ge(sm["split_hi"], 8 * b + n + 1)
                    dve.scalar_tensor_tensor(parts[:, k, w, 1, :], qk[:, w, k, :], asc[:, 8 + w:9 + w],
                                             parts[:, k, w, 0, :], ALU.mult, ALU.subtract).then_inc(sm["split_lo"], 1)

            def core(b):
                n = {k: b * v for k, v in TOTAL.items()}
                for e in ORDER:
                    kind, g = e[:2]
                    m = n[kind]
                    n[kind] += 1
                    if kind == "row":
                        h, t, c = e[2:]
                        w = min(512, (t + 1) * P - 512 * c)
                        dve.wait_ge(sm["row_ps"], m + 1)
                        dve.tensor_reduce(mx[:, h, t, c:c + 1], rowP[:, m % 2, 0:w], AX.X, ALU.max)\
                            .then_inc(sm["row_max"], 1)
                    elif kind == "max":
                        dve.wait_ge(sm["row_max"], n["row"])
                        link(dve.tensor_reduce(mm_[:, :], mx[:, :, :, :].rearrange("p h t c -> p (h t) c"),
                                               AX.X, ALU.max))
                        link(dve.tensor_scalar(mm_[:, :], mm_[:, :], -1.0 / MUNIT, None, ALU.mult))
                        if m:
                            dve.wait_ge(sm["mT_ps"], m)
                        mv = mm_[:, :].rearrange("p (h t) -> p t h", h=HG)
                        link(dve.tensor_copy(mrow[:, :, :, 0], mv))
                        dve.tensor_tensor(mrow[:, :, :, 1], mv, mrow[:, :, :, 0], ALU.subtract).then_inc(sm["m_set"], 1)
                    elif kind == "norm":
                        qc = e[2]
                        dve.wait_ge(sm["mix_done"], n["mix"])
                        if not qc and not g:
                            dve.wait_ge(sm["p_ps"], (b + 1) * len(ITEMS))
                        dve.tensor_copy(attT[:, g, qc * 512:(qc + 1) * 512], mixP[:, :]).then_inc(sm["mix_out"], 1)
                    elif kind == "rec":
                        dve.wait_ge(sm["sum_out"], m // 4 + 1)
                        r = rec[:, m % 4 * P:(m % 4 + 1) * P]
                        dve.reciprocal(r, r).then_inc(sm["rec_set"], 1)
                for i in range(BT):
                    g = b * BT + i
                    dve.wait_ge(sm["o_ps"], g + 1)
                    dve.wait_ge(sm["bo_added"], g + 1)
                    dve.tensor_tensor(x_sb[:, g, :], zP[:, i % 4 * 512:(i % 4 + 1) * 512], x_sb[:, g, :], ALU.add)\
                        .then_inc(sm["x_att"], 1)

            scale_of(0, S1)
            dve.tensor_scalar(SC1, S1, 1.0 / XSCALE, None, ALU.mult).then_inc(sm["scales_set"], 1)
            for c in range(4):
                ternary(0, c)
            for f in range(NF):
                for s in slots:
                    if f == 0 and s == 1:
                        constants()
                    if f == 0 and 1 <= s < 5:
                        ternary(1, s - 1)
                    if FIRST_UPD <= s <= LAST_UPD:
                        update(f, s)
                    do(h_lo, f, s, S_OUT + 1, 3)
                    do(below, f, s, S_SEL)
                    do(h_lo, f, s, S_OUT, 0)
                    do(pick, f, s, S_SEL)
                    do(x_lo, f, s, 0)
                    do(h_lo, f, s, S_OUT, 1)
                    do(residual, f, s, S_FIN)
                    do(stats1, f, s, -1)
                    do(keep_top, f, s, S_SEL)
                    do(h_lo, f, s, S_OUT, 2)
                    do(normal, f, s, -1)
                    do(normal2, f, s, S_FIN)
                if f == 0:
                    barrier(dve, 1)
                    link(dve.memset(mx[:, :, :, :], -BIG))
                    for b in range(2):
                        project(b)
                        core(b)
                        barrier(dve, 2 + b)


def kernel(**inputs):
    import numpy as np
    import concourse.bacc as bacc
    from concourse.bass_utils import run_bass_kernel_spmd

    nc = bacc.Bacc("TRN2", target_bir_lowering=False, num_devices=1)
    x = np.ascontiguousarray(inputs["L0_attn_x"]).reshape(TOKENS, D)
    arrays = {
        "x": x,
        "w_synT": np.ascontiguousarray(np.asarray(inputs["L0_ffn_W_syn"]).T),
        "b_syn": np.ascontiguousarray(inputs["L0_ffn_b_syn"]),
        "w_outT": np.ascontiguousarray(np.asarray(inputs["L0_ffn_W_out"]).T),
        "b_out": np.ascontiguousarray(inputs["L0_ffn_b_out"]),
        "gamma": np.ascontiguousarray(inputs["L0_ffn_gamma"]),
        "beta": np.ascontiguousarray(inputs["L0_ffn_beta"]),
    }
    for n in ("w_kv", "w_q", "w_kr", "w_ku", "w_qu", "w_qr", "w_vu", "w_o"):
        arrays[n] = np.ascontiguousarray(inputs["L0_attn_" + n])
    cols = [np.asarray(inputs["L0_attn_" + n]).reshape(-1, P) for n in ("b_kv", "b_q", "b_kr", "b_ku", "b_qu", "b_qr", "b_vu")]
    arrays["b_cols"] = np.ascontiguousarray(np.concatenate(cols).T)
    arrays["b_o"] = np.ascontiguousarray(inputs["L0_attn_b_o"])
    aps = [nc.dram_tensor("in_" + k, v.shape, F32, kind="ExternalInput").ap() for k, v in arrays.items()]
    o = nc.dram_tensor("out_dram", (TOKENS, D), F32, kind="ExternalOutput").ap()
    program(nc, *aps, o)
    r = run_bass_kernel_spmd(nc, [{"in_" + k: v for k, v in arrays.items()}], core_ids=[0])
    return r.results[0]["out_dram"].reshape(2, 1024, D)
```

```python
import concourse.bass as bass
from concourse import mybir
from contextlib import ExitStack

F32 = mybir.dt.float32
F16 = mybir.dt.float16
BF16 = mybir.dt.bfloat16
I32 = mybir.dt.int32
I8 = mybir.dt.int8
ALU = mybir.AluOpType
ACT = mybir.ActivationFunctionType
AX = mybir.AxisListType

P = 128
TOKENS, D, N = 2048, 512, 2048
NT = TOKENS // P
KD = D // P
KN = N // P
CH = 4
CW = N // CH
TOPK = int(N * (1.0 - 0.9))
EPS = 1e-5

NC = 5
TARGET = TOPK - 4.5
SSTAR = 2 * TARGET - N
BIG = 1e30
S_SEL, S_OUT, S_FIN = 2 + NC, 3 + NC, 4 + NC
ZR = 8
XR = 11
XSCALE = 256.0
HTOP = 16384.0
NF = 2

HEADS, HD = 16, 32
SEQ = 1024
BT = SEQ // P
HG = 4
GROUPS = HEADS // HG
MUNIT = 64.0
MASK = 32768.0
TURN_AFTER, LEAD = 3, 8
MIX_LAG = 1
SPLIT_LAG = 2
ROW_END = 5.5
ATT_SCALE = 1.0 / HD ** 0.5


def core_order():
    units = [(g, qc) for g in range(GROUPS) for qc in range(2)]
    rows, start = [], {}
    turn = None
    for g, qc in units:
        unit = [("row", g, h, t, c) for t in range(4 * qc, 4 * qc + 4) for h in range(HG) for c in range(qc + 1)]
        if (g, qc) == (0, 0):
            unit.sort(key=lambda e: e[2])
            others = [[("val", n)] + ([("lo", n + 3)] if 1 <= n <= 4 else []) for n in range(BT)]
            unit = [e for n in range(BT) for e in others[n] + unit[2 * n:2 * n + 2]]
        if turn:
            unit.insert(TURN_AFTER, turn)
        rows += unit + [("max", g, qc)]
        turn = ("turn", g, qc)
    rows.append(turn)
    for u in units:
        start[u] = min(len(rows), rows.index(("turn", *u)) + 1 + LEAD)

    ends = [0]
    for e in rows:
        ends.append(ends[-1] + (min(512, (e[3] + 1) * P - 512 * e[4]) if e[0] == "row" else 0))

    def columns(qc, kbs):
        return sum(min(512, (4 * qc + 4 - kb) * P) for kb in range(kbs))

    total = sum(columns(qc, 4 * qc + 4) for g, qc in units)
    until = total * ROW_END / len(units)
    order, at_row, before = rows[:start[units[0]]], start[units[0]], 0
    lead = ends[at_row]
    last = None
    for n, (g, qc) in enumerate(units):
        first, here = ends[at_row], columns(qc, 4 * qc + 4)
        goal = ends[start[units[n + 1]]] if n + 1 < len(units) else ends[-1]
        for kb in range(4 * qc + 4):
            step = [("col", g, qc, kb, h) for h in range(HG)]
            if last:
                step.insert(len(step) - MIX_LAG, ("mix_v", *last))
                step.append(("mix", *last))
            if kb == 0 and n:
                step.append(("norm", *units[n - 1]))
            last = (g, qc, kb)
            part = columns(qc, kb + 1)
            upto = max(first + (goal - first) * part / here, lead + (ends[-1] - lead) * (before + part) / until)
            ahead = []
            while at_row < len(rows) and (ends[at_row] < upto or kb == 4 * qc + 3 and n + 1 < len(units)
                                          and at_row < start[units[n + 1]]):
                ahead.append(rows[at_row])
                at_row += 1
            passes = [{"col": 1, "norm": 0}.get(e[0], 3) for e in step]
            done = 0
            for j, e in enumerate(step):
                order.append(e)
                upto = len(ahead) * sum(passes[:j + 1]) // sum(passes)
                order += ahead[done:upto]
                done = upto
        before += here
    order += rows[at_row:] + [("mix_v", *last), ("mix", *last), ("norm", *units[-1])]
    spread, waiting = [], []
    left = len(rows)
    for e in order:
        spread.append(e)
        left -= e in rows
        ready = waiting and (left == 0 or waiting[0][1] < 2)
        if ready and (e[0] in ("mix", "mix_v") or e[0] == "col" and e[4] == 1):
            spread.append(waiting.pop(0))
        if e[0] == "norm":
            waiting += [("rec", *e[1:], j) for j in range(4)]
    return spread + waiting


def program(nc, x, w_synT, b_syn, w_outT, b_out, gamma, beta, w_kv, w_q, w_kr, w_ku, w_qu, w_qr, w_vu, w_o, b_cols,
            b_o, out):
    ctx = ExitStack()
    with ctx:
        def sb(name, shape, dt):
            return ctx.enter_context(nc.sbuf_tensor(name, shape, dt))

        def pb(name, shape, dt):
            return ctx.enter_context(nc.psum_tensor(name, shape, dt))

        def sem(name):
            return ctx.enter_context(nc.semaphore(name))

        x_sb = sb("x_sb", [P, NT, D], F32)
        T1 = sb("T1", [P, KD, N], F16)
        T2 = sb("T2", [P, KN, D], F16)
        bsyn = sb("bsyn", [P, N], F32)
        bout = sb("bout", [P, D], F32)
        gam = sb("gam", [P, D], F32)
        bet = sb("bet", [P, D], F32)
        identf = sb("identf", [P, P], F32)
        onesf = sb("onesf", [P, P], F32)
        iota8 = sb("iota8", [P, 8], F32)
        nhalf = sb("nhalf", [P, 1], F32)
        half = sb("half", [P, 1], F32)
        ARENA = (4 * ZR * N + 4 * N + 2 * 2 * N + 2 * 2 * KN * P + 2 * 2 * 2 * KD * P + 4 * 2 * D + 4 * XR * D
                 + 2 * 4 * 2 * D) // 4
        arena = sb("arena", [P, ARENA], F32)
        taken = [0]

        def carve(words, dt=F32):
            a = arena[:, taken[0]:taken[0] + words]
            taken[0] += words
            assert taken[0] <= ARENA
            return a if dt == F32 else a.bitcast(dt)

        Z = carve(ZR * N).rearrange("p (z n) -> p z n", z=ZR)
        M = carve(N)
        junk = carve(N // 2, I8).rearrange("p (b n) -> p b n", b=2)
        hThi = carve(KN * P // 2, F16).rearrange("p (k t) -> p k t", k=KN)
        hTlo = carve(KN * P // 2, F16).rearrange("p (k t) -> p k t", k=KN)
        xThi = carve(KD * P, F16).rearrange("p (b k t) -> p b k t", b=2, k=KD)
        xTlo = carve(KD * P, F16).rearrange("p (b k t) -> p b k t", b=2, k=KD)
        xn = carve(2 * D).rearrange("p (b d) -> p b d", b=2)
        xb = carve(XR * D).rearrange("p (b d) -> p b d", b=XR)
        y = carve(2 * D).rearrange("p (b d) -> p b d", b=2)
        yt = carve(2 * D).rearrange("p (b d) -> p b d", b=2)

        G = carve(4 * NC).rearrange("p (g k) -> p g k", g=4)
        Y4 = carve(4 * NC).rearrange("p (g k) -> p g k", g=4)
        W2 = carve(2 * NC).rearrange("p (g k) -> p g k", g=2)
        E2 = carve(3 * NC).rearrange("p (g k) -> p g k", g=3)
        flags, flagsT = carve(32), carve(32)

        taken[0] = 0
        def as_stack(a):
            return a.bitcast(F16).rearrange("p (w h t) -> p w h t", w=2, h=HG)

        HALF = KD * SEQ
        xnT_mem = carve(HALF)
        xnT = xnT_mem.rearrange("p (k t) -> p k t", k=KD)
        w_in = carve(KD * D).rearrange("p (k n) -> p k n", k=KD)
        PT = carve(2 * HG * 512).rearrange("p (b h q) -> p b h q", b=2, h=HG)
        lat = PT.rearrange("p b h q -> p (b h q)")[:, 0:2 * SEQ].rearrange("p (l t) -> p l t", l=2)
        qk_mem = carve(2 * HALF)
        qk = qk_mem.rearrange("p (w k t) -> p w k t", w=2, k=KD)
        attT = qk[:, 0, :, :]
        wo_sb = M.rearrange("p (k n) -> p k n", k=KD)
        parts_mem = carve(2 * HALF)
        parts = parts_mem.bitcast(F16).rearrange("p (k w l t) -> p k w l t", w=2, l=2, k=KD)
        axn = parts_mem[:, 0:2 * D].rearrange("p (b d) -> p b d", b=2)
        V = xnT_mem.rearrange("p (t n) -> p t n", t=BT)
        stacks = [as_stack(carve(HALF)), as_stack(qk_mem[:, HALF:2 * HALF]), as_stack(parts_mem[:, 0:HALF])]
        tail = taken[0]
        w_lat = carve(5 * 256).rearrange("p (k n) -> p k n", k=5)
        taken[0] = tail
        rec = carve(512)
        later = parts_mem[:, HALF:2 * HALF].rearrange("p (m q) -> p m q", m=2 * GROUPS)

        def rec_of(m):
            return rec if m < 4 else later[:, m, :]

        mrows = carve(256, F16)[0:2 * HG, :]
        bo = carve(D)
        flagi = sb("flagi", [P, 1], I32)
        bcols = sb("bcols", [P, 14], F32)
        ident16 = sb("ident16", [P, P], F16)
        identm = sb("identm", [P, P], F16)
        maskq = sb("maskq", [P, P], F16)
        maskk = sb("maskk", [P, P], F16)
        mx = sb("mx", [P, HG, BT, 2], F32)
        mm_ = sb("mm_", [P, HG * 4], F32)
        mrow = sb("mrow", [P, 4, HG, 2], F16)
        aln = sb("aln", [P, 2, 4], F32)
        mxq = sb("mxq", [P, GROUPS, 2, 2], F32)
        asc = sb("asc", [P, GROUPS, 12], F32)
        st6 = sb("st6", [P, 24], F32)
        ln1 = sb("ln1", [P, 2, 4], F32)
        ln2 = sb("ln2", [P, 2, 4], F32)
        wsum = sb("wsum", [P, 16], F32)
        sc = sb("sc", [P, 32], F32)
        X = sb("X", [P, 4, NC], F32)
        Bk = sb("Bk", [P, 2, 4, NC], F32)
        S = sb("S", [P, NC], F32)
        FIN = sb("FIN", [P, 8], F32)
        m8 = sb("m8", [P, 8], F32)
        e8 = sb("e8", [P, 8], F32)
        sel = sb("sel", [P, 16], F32)
        okf = sb("okf", [P, 2], F32)
        oki = sb("oki", [P, 1], I32)

        zP = pb("zP", [P, N], F32)
        hP = pb("hP", [P, 2, CW], F32)
        oP = pb("oP", [P, D], F32)
        xP = pb("xP", [P, KD * P], F32)
        ones32 = onesf[:, 0:HD]
        rowP = [hP[:, 0, :], hP[:, 1, :], zP[:, 3 * 512:4 * 512]]
        colP = [zP[:, j * 512:(j + 1) * 512] for j in range(3)]
        mixP, sumP = oP, xP

        SC1, THR, NTHR, S1, S2, SH, SC2, SIG, T0 = (sc[:, i:i + 1] for i in range(9))

        names = ("vec_in x_in0 x_in1 x_in2 x_in3 w1_in0 w1_in1 w1_in2 w1_in3 w2_in0 w2_in1 w2_in2 w2_in3 "
                 "ones_set ident_set consts_set abs_done sum_ps sum_read tern_done sq_done scales_set search_set "
                 "stats1 xn_done rstd1 xT_ps xT_hi xT_lo z_ps z_evac z_bias upd cnt ok_set ok_sum "
                 "h_set hT_ps hT_hi hT_lo mm2 out_ps y_set stats2 rstd2 yn_set x_new xb_set out_done "
                 "consts2 ch_dve ch_act ch_pool phase "
                 "aw_in al_in ab_in a_stats a_rstd a_xn a_turn a_xT p_ps p_out p_max q_max q_scale split_hi split_lo wo_in bo_in "
                 "stq0 stq1 stq2 stq3 stk0 stk1 stk2 stk3 stack1 stack1k stack2 stack3 sum_out mix_out rec_set unit_set mrow_in row_ps row_max m_set mT_ps m_rows col_ps exp_done mix_done norm_set "
                 "o_ps x_att masks bo_added attn_set")
        sm = {n: sem(n) for n in names.split()}

        block = ctx.enter_context(nc.Block())
        slots = range(-1, NT + S_FIN + 1)

        ORDER = core_order()

        ITEMS = [("in", j, tc) for tc in range(2) for j in (0, 1)]
        ITEMS += [("up", j, tc) for j in (0, 2, 1, 3, 4, 5) for tc in range(2)]
        ITEMS += [("in", j, tc) for j in (2, 3) for tc in range(2)]
        VALUES = len(ITEMS)
        ITEMS += [("val", i, 0) for i in range(BT)]

        def plane(item):
            kind, j, tc = item
            if kind == "up":
                return (1, j, tc) if j < 2 else (0, j - 2, tc)
            return (1, j, tc) if kind == "in" and j >= 2 else None

        COMPLETE = [max(n for n, e in enumerate(ITEMS) if plane(e) and plane(e)[1] == g) for g in range(GROUPS)]

        TOTAL = {k: sum(e[0] == k for e in ORDER) for k in ("row", "max", "turn", "col", "mix", "norm", "rec", "mix_v", "val", "lo")}
        RING = [e for e in ORDER if e[0] in ("row", "turn")]

        def ring_steps(b):
            free, n = [], {"row": b * TOTAL["row"], "turn": b * TOTAL["turn"]}
            for j, e in enumerate(RING):
                n[e[0]] += 1
                free.append((sm["row_max" if e[0] == "row" else "m_rows"], n[e[0]]))
                yield j % len(rowP), free[j - len(rowP)] if j >= len(rowP) else None

        def out_banks(b):
            return [zP[:, j * 512:(j + 1) * 512] for j in range(4)] if b == 0 else [hP[:, 0, :], hP[:, 1, :]]

        def out_tiles(f, s):
            return () if f == 0 else (0, 1) if s == -1 else (s + 2,) if 0 <= s < BT - 2 else ()

        STACK_OF = (0, 1, 2, 0)
        SPLITS = [(k, w) for k in range(KD) for w in range(2)]

        def wait_stack(eng, b, g, heads=range(HG)):
            if g == 1:
                eng.wait_ge(sm["stack1"], 16 * 3 * HG * (b + 1))
                eng.wait_ge(sm["stack1k"], 16 * 3 * HG * (b + 1))
            elif g:
                eng.wait_ge(sm[f"stack{g}"], 16 * 6 * HG * (b + 1))
            else:
                for h in heads:
                    eng.wait_ge(sm[f"stq{h}"], 16 * 3 * (b + 1))
                    eng.wait_ge(sm[f"stk{h}"], 16 * 3 * (b + 1))

        def load_stack(eng, b, g, w, heads=range(HG)):
            if g == 0:
                eng.wait_ge(sm["split_hi"], 8 * b + 2)
                eng.wait_ge(sm["split_lo"], 8 * b + 2)
            elif g == 1:
                eng.wait_ge(sm["split_hi"], 8 * b + 8)
                eng.wait_ge(sm["split_lo"], 8 * b + 8)
            elif g == 2:
                wait_stack(eng, b, 0)
                wait_stack(eng, b, 1)
            else:
                eng.wait_ge(sm["mix_done"], b * TOTAL["mix"] + TOTAL["mix"] // GROUPS)
            for h in heads:
                done = sm[f"st{'qk'[w]}{h}" if g == 0 else "stack1k" if (g, w) == (1, 1) else f"stack{g}"]
                for j, part in enumerate(((0, 0, 1), (0, 1, 0))[w]):
                    eng.dma_start(stacks[STACK_OF[g]][HD * j:HD * (j + 1), w, h, :],
                                  parts[HD * h:HD * (h + 1), g, w, part, :]).then_inc(done, 16)

        def barrier(eng, k):
            eng.drain().then_inc(sm["phase"], 1)
            eng.wait_ge(sm["phase"], 5 * k)

        def at(s, off):
            i = s - off
            return i if 0 <= i < NT else None

        def do(stage, f, s, off, *a):
            i = at(s, off)
            if i is not None:
                stage(f, i, *a)

        FIRST_UPD, LAST_UPD = 3, NT + S_SEL - 1

        def updates(f, s):
            return f * (LAST_UPD - FIRST_UPD + 1) + s - FIRST_UPD + 1

        @block.sync
        def _(eng):
            xv = x.rearrange("(t p) d -> p t d", p=P)
            for c in range(4):
                eng.dma_start(Z[:, c, :], w_synT[c * P:(c + 1) * P, :]).then_inc(sm[f"w1_in{c}"], 16)
                if c == 0:
                    eng.dma_start(x_sb[:, 0:4, :], xv[:, 0:4, :]).then_inc(sm["x_in0"], 16)
            for v, d in ((b_syn, bsyn), (b_out, bout), (gamma, gam), (beta, bet)):
                eng.dma_start(d[:, :], v.partition_broadcast(P)).then_inc(sm["vec_in"], 16)
            w2v = w_outT.rearrange("(k p) o -> p k o", p=P)
            for c in range(4):
                eng.dma_start(Z[:, 4 + c, :].rearrange("p (k o) -> p k o", o=D),
                              w2v[:, 4 * c:4 * c + 4, :]).then_inc(sm[f"w2_in{c}"], 16)
            for c in range(1, 4):
                eng.dma_start(x_sb[:, 4 * c:4 * c + 4, :], xv[:, 4 * c:4 * c + 4, :]).then_inc(sm[f"x_in{c}"], 16)
            eng.wait_ge(sm["hT_ps"], 4 * NT)
            for k in range(KD):
                for w, lo in ((w_kv, 0), (w_q, 128), (w_kr, 256)):
                    eng.dma_start(w_in[:, k, lo:lo + w.shape[1]], w[k * P:(k + 1) * P, :]).then_inc(sm["aw_in"], 16)
            barrier(eng, 1)
            for b in range(2):
                for k, w in ((0, w_ku), (1, w_qu), (2, w_qr), (3, w_vu)):
                    eng.dma_start(w_lat[:, k:k + w.shape[1] // 256, :].rearrange("p k n -> p (k n)"), w)\
                        .then_inc(sm["al_in"], 16)
                if b == 0:
                    eng.dma_start(bcols[:, :], b_cols).then_inc(sm["ab_in"], 16)

                def max_rows(g, qc):
                    eng.wait_ge(sm["m_rows"], b * TOTAL["turn"] + 2 * g + qc + 1)
                    for h in range(HG):
                        eng.dma_start(stacks[STACK_OF[g]][3 * HD:3 * HD + 2, 0, h, 512 * qc:512 * (qc + 1)],
                                      mrows[2 * h:2 * h + 2, :])\
                            .then_inc(sm["mrow_in"], 16)

                for h in range(HG):
                    for w in range(2):
                        load_stack(eng, b, 0, w, [h])
                max_rows(0, 0)
                load_stack(eng, b, 1, 0)
                eng.wait_ge(sm["p_ps"], (b + 1) * len(ITEMS))
                eng.dma_start(bo, b_o.partition_broadcast(P)).then_inc(sm["bo_in"], 16)
                max_rows(0, 1)
                load_stack(eng, b, 2, 0)
                max_rows(1, 0)
                load_stack(eng, b, 2, 1)
                max_rows(1, 1)
                load_stack(eng, b, 3, 0)
                max_rows(2, 0)
                load_stack(eng, b, 3, 1)
                max_rows(2, 1)
                eng.wait_ge(sm["mix_done"], b * TOTAL["mix"] + TOTAL["mix"] // 2)
                eng.dma_start(wo_sb, w_o.rearrange("(k p) n -> p k n", p=P)).then_inc(sm["wo_in"], 16)
                max_rows(3, 0)
                max_rows(3, 1)
                barrier(eng, 2 + b)
            ov = out.rearrange("(t p) d -> p t d", p=P)
            for i in range(NT):
                eng.wait_ge(sm["x_new"], (NF - 1) * NT + i + 1)
                eng.dma_start(ov[:, i, :], x_sb[:, i, :]).then_inc(sm["out_done"], 16)
            eng.wait_ge(sm["out_done"], 16 * NT)

        @block.tensor
        def _(pe):
            def partition_sum(out_, in_, ready, value):
                pe.wait_ge(sm[ready], value)
                pe.matmul(out_, onesf[:, :], in_, start=True, stop=True).then_inc(sm["sum_ps"], 1)

            pe.wait_ge(sm["ones_set"], 1)
            pe.wait_ge(sm["ident_set"], 2)
            partition_sum(xP[:, 0:4], wsum[:, 0:4], "abs_done", 4)
            pe.wait_ge(sm["sum_read"], 1)

            def x_turn(f, i):
                g = f * NT + i
                pe.wait_ge(sm["xn_done"], g + 1)
                if g:
                    pe.wait_ge(sm["xT_lo"], g)
                for k in range(KD):
                    mm = pe.transpose(xP[:, k * P:(k + 1) * P], xn[:, g % 2, k * P:(k + 1) * P], identf[:, :])
                mm.then_inc(sm["xT_ps"], 1)

            def mm1(f, i, c):
                g = f * NT + i
                if c == 0:
                    pe.wait_ge(sm["xT_lo"], g + 1)
                    pe.wait_ge(sm["tern_done"], 4)
                if g:
                    pe.wait_ge(sm["z_evac"], 4 * (g - 1) + c + 1)
                for n, part in enumerate((xThi, xTlo)):
                    for k in range(KD):
                        mm = pe.matmul(zP[:, c * CW:(c + 1) * CW], part[:, g % 2, k, :], T1[:, k, c * CW:(c + 1) * CW],
                                       start=(n == 0 and k == 0), stop=(n == 1 and k == KD - 1))
                mm.then_inc(sm["z_ps"], 1)

            def h_turn(f, i, c):
                g = f * NT + i
                if c == 0:
                    pe.wait_ge(sm["h_set"], g + 1)
                q = 4 * g + c
                if q == 4 * NT:
                    pe.wait_ge(sm["x_att"], 2 * BT)
                if q >= 2:
                    pe.wait_ge(sm["hT_lo"], q - 1)
                for k in range(4):
                    n0 = c * CW + k * P
                    mm = pe.transpose(hP[:, c % 2, k * P:(k + 1) * P], Z[:, g % ZR, n0:n0 + P], identf[:, :])
                mm.then_inc(sm["hT_ps"], 1)

            def mm2(f, i, c):
                g = f * NT + i
                pe.wait_ge(sm["hT_lo"], 4 * g + c + 1)
                if c == 0:
                    pe.wait_ge(sm["tern_done"], 8)
                    pe.wait_ge(sm["sum_read"], 3)
                    if g:
                        pe.wait_ge(sm["y_set"], g)
                for n, part in enumerate((hThi, hTlo)):
                    for k in range(4 * c, 4 * c + 4):
                        mm = pe.matmul(oP[:, :], part[:, k, :], T2[:, k, :],
                                       start=(c == 0 and n == 0 and k == 0), stop=(c == 3 and n == 1 and k == KN - 1))
                mm.then_inc(sm["mm2"], 1)

            def turn_rows(b, i):
                g = b * BT + i
                pe.wait_ge(sm["a_xn"], g + 1)
                if g >= 2:
                    pe.wait_ge(sm["a_xT"], g - 1)
                for k in range(KD):
                    mm = pe.transpose(hP[:, i % 2, k * P:(k + 1) * P], axn[:, g % 2, k * P:(k + 1) * P], identf[:, :])
                mm.then_inc(sm["a_turn"], 1)

            def project(b):
                pe.wait_ge(sm["aw_in"], 16 * 3 * KD)
                for n in range(VALUES):
                    item(b, n)

            def item(b, n):
                kind, j, tc = ITEMS[n]
                if n >= 3:
                    pe.wait_ge(sm["p_out"], b * len(ITEMS) + n - 2)
                o = zP[:, n % 3 * 512:(n % 3 + 1) * 512]
                tok = slice(tc * 512, (tc + 1) * 512)
                if kind == "in":
                    pe.wait_ge(sm["a_xT"], b * BT + 4 * (tc + 1))
                    for k in range(KD):
                        mm = pe.matmul(o, w_in[:, k, j * P:(j + 1) * P], xnT[:, k, tok],
                                       start=(k == 0), stop=(k == KD - 1))
                elif kind == "up":
                    src = 0 if j < 2 else 1
                    pe.wait_ge(sm["al_in"], 16 * 4 * (b + 1))
                    pe.wait_ge(sm["p_out"], b * len(ITEMS) + ITEMS.index(("in", src, tc)) + 1)
                    mm = pe.matmul(o, w_lat[:, j // 2, (j % 2) * P:(j % 2 + 1) * P], lat[:, src, tok],
                                   start=True, stop=True)
                else:
                    mm = pe.matmul(o, lat[:, 0, j * P:(j + 1) * P],
                                   w_lat[:, 3:5, :].rearrange("p k n -> p (k n)"), start=True, stop=True)
                mm.then_inc(sm["p_ps"], 1)

            def core(b):
                n = {k: b * v for k, v in TOTAL.items()}
                ring = ring_steps(b)
                for e in ORDER:
                    kind, g = e[:2]
                    stack = stacks[STACK_OF[g]] if g < GROUPS else None
                    if kind in ("row", "turn"):
                        bank, free = next(ring)
                        if free:
                            pe.wait_ge(*free)
                    elif kind == "val":
                        item(b, VALUES + g)
                    m = n[kind]
                    n[kind] += 1
                    if kind == "row":
                        h, t, c = e[2:]
                        if g == 0 and (t, c) == (0, 0):
                            wait_stack(pe, b, g, [h])
                        if (h, t, c) == (0, 0, 0):
                            if g:
                                wait_stack(pe, b, g)
                            pe.wait_ge(sm["masks"], 2)
                            pe.wait_ge(sm["a_xT"], (b + 1) * BT)
                        w = min(512, (t + 1) * P - 512 * c)
                        own = c == t // 4
                        mm = pe.matmul(rowP[bank][:, 0:w], stack[0:3 * HD, 0, h, t * P:(t + 1) * P],
                                       stack[0:3 * HD, 1, h, 512 * c:512 * c + w], start=True, stop=not own)
                        if own:
                            mm = pe.matmul(rowP[bank][:, w - P:w], identm[:, :], maskq[:, :], start=False, stop=True)
                        mm.then_inc(sm["row_ps"], 1)
                    elif kind == "turn":
                        pe.wait_ge(sm["m_set"], m + 1)
                        for t in range(4):
                            mm = pe.transpose(rowP[bank].bitcast(F16)[0:2 * HG, t * P:(t + 1) * P],
                                              mrow[:, t, :, :].rearrange("p h l -> p (h l)"), ident16[:, :])
                        mm.then_inc(sm["mT_ps"], 1)
                    elif kind == "col":
                        qc, kb, h = e[2:]
                        if (kb, h) == (0, 0):
                            pe.wait_ge(sm["mrow_in"], 16 * HG * (TOTAL["turn"] * b + 2 * g + qc + 1))
                            pe.wait_ge(sm["unit_set"], 3 * b + min(g, 2) + 1)
                            pe.wait_ge(sm["p_out"], (b + 1) * len(ITEMS))
                        if m >= 3:
                            pe.wait_ge(sm["exp_done"], m - 2)
                        q0 = max(0, kb * P - qc * 512)
                        own = kb * P >= qc * 512
                        mm = pe.matmul(colP[m % 3][:, q0:512], stack[0:3 * HD + 2, 1, h, kb * P:(kb + 1) * P],
                                       stack[0:3 * HD + 2, 0, h, qc * 512 + q0:(qc + 1) * 512],
                                       start=True, stop=not own)
                        if own:
                            mm = pe.matmul(colP[m % 3][:, q0:q0 + P], identm[:, :], maskk[:, :], start=False, stop=True)
                        mm.then_inc(sm["col_ps"], 1)
                    elif kind in ("mix_v", "mix"):
                        qc, kb = e[2:]
                        pe.wait_ge(sm["exp_done"], 4 * (m + 1))
                        if kb == 0 and n["norm"]:
                            pe.wait_ge(sm["mix_out"], n["norm"])
                            pe.wait_ge(sm["sum_out"], n["norm"])
                        q0 = max(0, kb * P - qc * 512)
                        last = kb == 4 * qc + 3
                        for h in range(HG):
                            v = V[:, kb, g * P + h * HD:g * P + (h + 1) * HD] if kind == "mix_v" else ones32
                            mm = pe.matmul((mixP if kind == "mix_v" else sumP)[h * HD:(h + 1) * HD, q0:512], v,
                                           PT[:, m % 2, h, q0:512], start=(kb == 0), stop=last,
                                           tile_position=(0, h * HD), skip_group_check=True)
                        if kind == "mix":
                            mm.then_inc(sm["mix_done"], 1)
                if b == 0:
                    for i in range(BT):
                        out_proj(b, i)
                        turn_rows(1, i)

            def out_proj(b, i):
                g = b * BT + i
                if i == 0:
                    pe.wait_ge(sm["wo_in"], 16 * (b + 1))
                    pe.wait_ge(sm["exp_done"], (b + 1) * TOTAL["col"])
                    pe.wait_ge(sm["m_rows"], (b + 1) * TOTAL["turn"])
                    pe.wait_ge(sm["row_max"], (b + 1) * TOTAL["row"])
                if i % 4 == 0:
                    pe.wait_ge(sm["attn_set"], (b + 1) * TOTAL["norm"] - 1 + i // 4)
                banks = out_banks(b)
                if i >= len(banks):
                    pe.wait_ge(sm["x_att"], g - len(banks) + 1)
                for k in range(KD):
                    mm = pe.matmul(banks[i % len(banks)], attT[:, k, i * P:(i + 1) * P], wo_sb[:, k, :],
                                   start=(k == 0), stop=(k == KD - 1))
                mm.then_inc(sm["o_ps"], 1)

            for f in range(NF):
                for s in slots:
                    for c in range(4):
                        do(mm1, f, s, 1, c)
                        do(h_turn, f, s, S_OUT, c)
                        if c == 0:
                            do(x_turn, f, s, 0)
                        if c < 2:
                            do(mm2, f, s, S_OUT + 1, c + 2)
                        else:
                            do(mm2, f, s, S_OUT, c - 2)
                    for i in out_tiles(f, s):
                        out_proj(1, i)
                    if f == 0 and s == 0:
                        partition_sum(oP[:, 0:4], wsum[:, 4:8], "abs_done", 8)
                        pe.wait_ge(sm["sum_read"], 2)
                        partition_sum(oP[:, 0:1], wsum[:, 8:9], "sq_done", 1)
                if f == 0:
                    barrier(pe, 1)
                    for i in range(BT):
                        turn_rows(0, i)
                    for b in range(2):
                        project(b)
                        core(b)
                        barrier(pe, 2 + b)

        @block.scalar
        def _(act):
            for n in range(2):
                for c in range(4):
                    act.wait_ge(sm[f"w{n + 1}_in{c}"], 16)
                    if n or c:
                        act.wait_ge(sm["abs_done"], 4 * n + c)
                    act.activation(junk[:, 0, :], Z[:, 4 * n + c, :], ACT.Abs,
                                   accum_out=wsum[:, 4 * n + c:4 * n + c + 1]).then_inc(sm["abs_done"], 1)
            act.wait_ge(sm["tern_done"], 1)
            act.wait_ge(sm["abs_done"], 8)
            act.activation(junk[:, 0, :], T1[:, 0, :], ACT.Square, accum_out=wsum[:, 8:9]).then_inc(sm["sq_done"], 1)
            act.wait_ge(sm["scales_set"], 1)
            act.wait_ge(sm["sq_done"], 1)

            def evac(f, i, c):
                g = f * NT + i
                act.wait_ge(sm["z_ps"], 4 * g + c + 1)
                if g >= ZR and c == 0:
                    act.wait_ge(sm["hT_ps"], 4 * (g - ZR) + 4)
                if g < 8 and c == 0:
                    act.wait_ge(sm["tern_done"], 4 if g < 4 else 8)
                act.activation(Z[:, g % ZR, c * CW:(c + 1) * CW], zP[:, c * CW:(c + 1) * CW], ACT.Copy,
                               scale=SC1).then_inc(sm["z_evac"], 1)

            def h_hi(f, i, c):
                g = f * NT + i
                act.wait_ge(sm["hT_ps"], 4 * g + c + 1)
                if g:
                    act.wait_ge(sm["mm2"], 4 * (g - 1) + c + 1)
                else:
                    act.wait_ge(sm["scales_set"], 2)
                act.activation(hThi[:, 4 * c:4 * c + 4, :].rearrange("p k t -> p (k t)"), hP[:, c % 2, :], ACT.Copy,
                               scale=SH).then_inc(sm["hT_hi"], 1)

            def x_hi(f, i):
                g = f * NT + i
                act.wait_ge(sm["xT_ps"], g + 1)
                if g >= 2:
                    act.wait_ge(sm["z_ps"], 4 * (g - 2) + 4)
                act.activation(xThi[:, g % 2, :, :].rearrange("p k t -> p (k t)"), xP[:, :], ACT.Copy,
                               scale=XSCALE).then_inc(sm["xT_hi"], 1)

            counted = [0]

            def count(f, s, k):
                i = at(s, 2 + k)
                if i is None:
                    return
                g = f * NT + i
                if k == 0:
                    act.wait_ge(sm["search_set"], 1)
                    act.wait_ge(sm["z_bias"], 4 * g + 4)
                if s >= FIRST_UPD:
                    act.wait_ge(sm["upd"], updates(f, s))
                elif f:
                    act.wait_ge(sm["upd"], updates(f - 1, LAST_UPD))
                if counted[0] >= 2:
                    act.wait_ge(sm["cnt"], counted[0] - 1)
                act.activation(junk[:, counted[0] % 2, :], Z[:, g % ZR, :], ACT.Sign, bias=X[:, 2, k:k + 1],
                               accum_out=S[:, k:k + 1]).then_inc(sm["cnt"], 1)
                counted[0] += 1

            def take_rows(b):
                for i in range(BT):
                    act.wait_ge(sm["a_turn"], b * BT + i + 1)
                    act.activation(xnT[:, :, i * P:(i + 1) * P], hP[:, i % 2, :].rearrange("p (k t) -> p k t", k=KD),
                                   ACT.Copy).then_inc(sm["a_xT"], 1)

            def project(b):
                if b == 0:
                    act.wait_ge(sm["ab_in"], 16)
                for n in range(VALUES):
                    evac_item(b, n)
                    if n - SPLIT_LAG in COMPLETE:
                        split_hi(b, COMPLETE.index(n - SPLIT_LAG))
                split_hi(b, 3)

            def split_hi(b, g):
                act.wait_ge(sm["q_scale"], b * GROUPS + g + 1)
                for w in range(2):
                    act.activation(parts[:, g, w, 0, :], qk[:, w, g, :], ACT.Copy,
                                   scale=asc[:, g, 8 + w:9 + w]).then_inc(sm["split_hi"], 1)

            def evac_item(b, n):
                kind, j, tc = ITEMS[n]
                act.wait_ge(sm["p_ps"], b * len(ITEMS) + n + 1)
                o = zP[:, n % 3 * 512:(n % 3 + 1) * 512]
                if kind == "val":
                    act.activation(V[:, j, :], o, ACT.Copy).then_inc(sm["p_out"], 1)
                    return
                tok = slice(tc * 512, (tc + 1) * 512)
                col = j if kind == "in" else 4 + j
                w, g = plane(ITEMS[n])[:2] if plane(ITEMS[n]) else (0, 0)
                dst = qk[:, w, g, tok] if plane(ITEMS[n]) else lat[:, j, tok]
                act.activation(dst, o, ACT.Identity, bias=bcols[:, col:col + 1]).then_inc(sm["p_out"], 1)

            def core(b):
                n = {k: b * v for k, v in TOTAL.items()}
                ring = ring_steps(b)
                for e in ORDER:
                    kind, g = e[:2]
                    m = n[kind]
                    n[kind] += 1
                    if kind in ("row", "turn"):
                        bank, _ = next(ring)
                    if kind == "val":
                        evac_item(b, VALUES + g)
                    if kind == "col":
                        qc, kb, h = e[2:]
                        act.wait_ge(sm["col_ps"], m + 1)
                        if m // 4 >= 2:
                            act.wait_ge(sm["mix_done"], m // 4 - 1)
                        q0 = max(0, kb * P - qc * 512)
                        act.activation(PT[:, m // 4 % 2, h, q0:512], colP[m % 3][:, q0:512], ACT.Exp,
                                       scale=asc[:, g, 10:11]).then_inc(sm["exp_done"], 1)
                    elif kind == "norm":
                        qc, u = e[2], m % TOTAL["norm"]
                        act.wait_ge(sm["mix_done"], n["mix"])
                        act.activation(attT[:, g, qc * 512:(qc + 1) * 512], mixP[:, :], ACT.Copy)\
                            .then_inc(sm["mix_out"], 1)
                        if u < 4:
                            if m:
                                act.wait_ge(sm["attn_set"], m)
                        else:
                            wait_stack(act, b, 2)
                            wait_stack(act, b, 3)
                        act.activation(rec_of(u), sumP[:, :], ACT.Copy).then_inc(sm["sum_out"], 1)
                    elif kind == "turn":
                        act.wait_ge(sm["mT_ps"], m + 1)
                        if not m % TOTAL["turn"]:
                            act.wait_ge(sm["p_ps"], (b + 1) * len(ITEMS))
                        if m:
                            act.wait_ge(sm["mrow_in"], 16 * HG * m)
                        act.activation(mrows, rowP[bank].bitcast(F16)[0:2 * HG, 0:512], ACT.Copy).then_inc(sm["m_rows"], 1)

            for f in range(NF):
                for s in slots:
                    do(evac, f, s, 2, 3)
                    do(h_hi, f, s, S_OUT + 1, 3)
                    do(evac, f, s, 1, 0)
                    do(h_hi, f, s, S_OUT, 0)
                    do(x_hi, f, s, 0)
                    count(f, s, 4)
                    count(f, s, 3)
                    do(evac, f, s, 1, 1)
                    do(h_hi, f, s, S_OUT, 1)
                    count(f, s, 2)
                    count(f, s, 1)
                    do(evac, f, s, 1, 2)
                    do(h_hi, f, s, S_OUT, 2)
                    count(f, s, 0)
                if f == 0:
                    barrier(act, 1)
                    take_rows(0)
                    for b in range(2):
                        project(b)
                        core(b)
                        if b == 0:
                            take_rows(1)
                        barrier(act, 2 + b)

        def counts_before(f, s):
            per_f = NC * NT
            return f * per_f + sum(1 for t in range(-1, s) for k in range(NC) if at(t, 2 + k) is not None)

        @block.gpsimd
        def _(pool):
            n = [0]

            def link(ins):
                n[0] += 1
                ins.then_inc(sm["ch_pool"], 1)
                pool.wait_ge(sm["ch_pool"], n[0])

            pool.memset(onesf[:, :], 1.0).then_inc(sm["ones_set"], 1)
            pool.memset(identf[:, :], 0.0).then_inc(sm["ident_set"], 1)
            pool.wait_ge(sm["ident_set"], 1)
            pool.affine_select(out=identf[:, :], in_=identf[:, :], compare_op=ALU.not_equal, fill=1.0, base=0,
                               pattern=[[-1, P]], channel_multiplier=1).then_inc(sm["ident_set"], 1)
            pool.wait_ge(sm["ident_set"], 2)
            link(pool.tensor_copy(ident16[:, :], identf[:, :]))
            link(pool.tensor_scalar(identm[:, :], identf[:, :], MASK, None, ALU.mult))
            link(pool.memset(maskq[:, :], 0.0))
            link(pool.memset(maskk[:, :], 0.0))
            pool.affine_select(out=maskq[:, :], in_=maskq[:, :], compare_op=ALU.is_ge, fill=-MASK, base=0,
                               pattern=[[-1, P]], channel_multiplier=1).then_inc(sm["masks"], 1)
            pool.affine_select(out=maskk[:, :], in_=maskk[:, :], compare_op=ALU.is_ge, fill=-MASK, base=0,
                               pattern=[[1, P]], channel_multiplier=-1).then_inc(sm["masks"], 1)
            link(pool.memset(nhalf[:, :], -0.5))
            link(pool.memset(half[:, :], 0.5))
            for k in range(8):
                pool.memset(iota8[:, k:k + 1], float(k)).then_inc(sm["consts_set"], 1)
                pool.wait_ge(sm["consts_set"], k + 1)
            def rstd1(f, i):
                g = f * NT + i
                pool.wait_ge(sm["stats1"], g + 1)
                link(pool.tensor_scalar(ln1[:, g % 2, 2:3], ln1[:, g % 2, 1:2], EPS, None, ALU.add))
                pool.tensor_tensor(ln1[:, g % 2, 3:4], ln1[:, g % 2, 2:3], nhalf[:, :], ALU.pow)\
                    .then_inc(sm["rstd1"], 1)

            def xbias(f, i):
                g = f * NT + i
                pool.wait_ge(sm["xn_done"], g + 1)
                if g == 0:
                    pool.wait_ge(sm["vec_in"], 64)
                if g >= XR:
                    pool.wait_ge(sm["y_set"], g - XR + 1)
                pool.tensor_tensor(xb[:, g % XR, :], xn[:, g % 2, :], bout[:, :], ALU.add).then_inc(sm["xb_set"], 1)

            def bias(f, i, c):
                g = f * NT + i
                pool.wait_ge(sm["z_evac"], 4 * g + c + 1)
                zz = Z[:, g % ZR, c * CW:(c + 1) * CW]
                pool.tensor_tensor(zz, zz, bsyn[:, c * CW:(c + 1) * CW], ALU.add).then_inc(sm["z_bias"], 1)

            def ok_sum(f, i):
                g = f * NT + i
                pool.wait_ge(sm["ok_set"], g + 1)
                link(pool.partition_all_reduce(okf[:, 1:2], okf[:, 0:1], P, bass.bass_isa.ReduceOp.add))
                pool.tensor_copy(oki[:, :], okf[:, 1:2]).then_inc(sm["ok_sum"], 1)

            def rstd2(f, i):
                g = f * NT + i
                pool.wait_ge(sm["stats2"], g + 1)
                link(pool.tensor_scalar(ln2[:, g % 2, 2:3], ln2[:, g % 2, 1:2], EPS, None, ALU.add))
                pool.tensor_tensor(ln2[:, g % 2, 3:4], ln2[:, g % 2, 2:3], nhalf[:, :], ALU.pow)\
                    .then_inc(sm["rstd2"], 1)

            def final(f, i):
                g = f * NT + i
                link(pool.tensor_tensor(x_sb[:, i, :], x_sb[:, i, :], bet[:, :], ALU.add))
                pool.wait_ge(sm["yn_set"], g + 1)
                link(pool.tensor_tensor(yt[:, g % 2, :], yt[:, g % 2, :], gam[:, :], ALU.mult))
                pool.tensor_tensor(x_sb[:, i, :], x_sb[:, i, :], yt[:, g % 2, :], ALU.add).then_inc(sm["x_new"], 1)

            def rstd_rows(b, tiles):
                for i in tiles:
                    g = b * BT + i
                    pool.wait_ge(sm["a_stats"], g + 1)
                    link(pool.tensor_scalar(aln[:, g % 2, 2:3], aln[:, g % 2, 1:2], EPS, None, ALU.add))
                    pool.tensor_tensor(aln[:, g % 2, 3:4], aln[:, g % 2, 2:3], nhalf[:, :], ALU.pow)\
                        .then_inc(sm["a_rstd"], 1)

            def project(b):
                for g in range(GROUPS):
                    all_max(b, g)

            def all_max(b, g):
                pool.wait_ge(sm["p_max"], b * GROUPS + g + 1)
                pool.partition_all_reduce(asc[:, g, 2:4], asc[:, g, 0:2], P, bass.bass_isa.ReduceOp.max)\
                    .then_inc(sm["q_max"], 1)
                pool.wait_ge(sm["q_max"], b * GROUPS + g + 1)

            def core(b):
                for g in range(3):
                    if g == 1:
                        load_stack(pool, b, 1, 1)
                    elif g == 2:
                        wait_stack(pool, b, 0)
                        wait_stack(pool, b, 1)
                    pool.memset(stacks[g][3 * HD:3 * HD + 2, 1, :, :], MUNIT).then_inc(sm["unit_set"], 1)
                    pool.wait_ge(sm["unit_set"], 3 * b + g + 1)
                pool.wait_ge(sm["bo_in"], 16 * (b + 1))
                pool.wait_ge(sm["a_xn"], (b + 1) * BT)
                for i in range(BT):
                    t = x_sb[:, b * BT + i, :]
                    pool.tensor_tensor(t, t, bo, ALU.add).then_inc(sm["bo_added"], 1)
                for m in range(TOTAL["norm"]):
                    if b == 0 and m == TOTAL["norm"] - 1:
                        rstd_rows(1, range(2))
                    g, qc = m // 2, m % 2
                    a = attT[:, g, qc * 512:(qc + 1) * 512]
                    pool.wait_ge(sm["mix_out"], b * TOTAL["norm"] + m + 1)
                    pool.wait_ge(sm["rec_set"], 4 * (b * TOTAL["norm"] + m + 1))
                    link(pool.tensor_tensor(a, a, rec_of(m), ALU.mult))
                    pool.tensor_scalar(a, a, bcols[:, 10 + g:11 + g], None, ALU.add).then_inc(sm["attn_set"], 1)

            for f in range(NF):
                for s in slots:
                    do(bias, f, s, 2, 3)
                    do(xbias, f, s, 0)
                    do(bias, f, s, 1, 0)
                    do(final, f, s, S_FIN + 1)
                    do(bias, f, s, 1, 1)
                    do(ok_sum, f, s, S_SEL)
                    do(rstd2, f, s, S_FIN)
                    do(rstd1, f, s, -1)
                    do(bias, f, s, 1, 2)
                    if f == 0 and s == 0:
                        pool.wait_ge(sm["scales_set"], 3)
                        pool.tensor_tensor(SIG, sc[:, 16:17], half[:, :], ALU.pow).then_inc(sm["scales_set"], 1)
                        link(pool.tensor_scalar(gam[:, :], gam[:, :], 0.5, None, ALU.mult))
                        link(pool.tensor_scalar(bet[:, :], bet[:, :], 0.5, None, ALU.mult))
                if f == 0:
                    barrier(pool, 1)
                    rstd_rows(0, range(BT))
                    for b in range(2):
                        project(b)
                        core(b)
                        if b == 0:
                            rstd_rows(1, range(2, BT))
                        barrier(pool, 2 + b)

        @block.vector
        def _(dve):
            n = [0]

            def link(ins):
                n[0] += 1
                ins.then_inc(sm["ch_dve"], 1)
                dve.wait_ge(sm["ch_dve"], n[0])

            def step(ins):
                n[0] += 1
                ins.then_inc(sm["ch_dve"], 1)

            def after(back):
                dve.wait_ge(sm["ch_dve"], n[0] - back)

            def ternary(m, c):
                w = Z[:, 4 * m + c, :]
                low = M[:, 0:N // 2].bitcast(F16) if c % 2 else M[:, N // 2:N].bitcast(F16)
                link(dve.tensor_scalar(low, w, NTHR, None, ALU.is_lt))
                o = T1[:, c, :] if m == 0 else T2[:, 4 * c:4 * c + 4, :].rearrange("p k o -> p (k o)")
                dve.scalar_tensor_tensor(o, w, THR, low, ALU.is_gt, ALU.subtract).then_inc(sm["tern_done"], 1)
                dve.wait_ge(sm["tern_done"], 4 * m + c + 1)

            def scale_of(m, dst):
                dve.wait_ge(sm["sum_ps"], m + 1)
                dve.tensor_reduce(sc[:, 12 + m:13 + m], (xP, oP)[m][:, 0:4], AX.X, ALU.add).then_inc(sm["sum_read"], 1)
                dve.wait_ge(sm["sum_read"], m + 1)
                link(dve.tensor_scalar(dst, sc[:, 12 + m:13 + m], 1.0 / (N * D), None, ALU.mult))
                link(dve.tensor_scalar(THR, dst, 1e-8, 0.5, ALU.add, ALU.mult))
                link(dve.tensor_scalar(NTHR, THR, -1.0, None, ALU.mult))

            def constants():
                scale_of(1, S2)
                dve.wait_ge(sm["consts_set"], 8)
                dve.wait_ge(sm["vec_in"], 64)
                link(dve.tensor_reduce(sc[:, 17:18], bsyn[:, :], AX.X, ALU.max, apply_absolute_value=True))
                link(dve.scalar_tensor_tensor(sc[:, 18:19], S1, float(D), sc[:, 17:18], ALU.mult, ALU.add))
                link(dve.tensor_scalar(sc[:, 18:19], sc[:, 18:19], 1e-30, None, ALU.max))
                link(dve.tensor_scalar(sc[:, 19:20].bitcast(I32), sc[:, 18:19].bitcast(I32), 0x7F800000, None,
                                       ALU.bitwise_and))
                link(dve.reciprocal(sc[:, 20:21], sc[:, 19:20]))
                link(dve.tensor_scalar(SH, sc[:, 20:21], HTOP, None, ALU.mult))
                dve.scalar_tensor_tensor(SC2, S2, 1.0 / HTOP, sc[:, 19:20], ALU.mult, ALU.mult)\
                    .then_inc(sm["scales_set"], 1)
                dve.wait_ge(sm["stats1"], 2)
                for c in range(4):
                    link(dve.bn_stats(st6[:, 6 * c:6 * c + 6], bsyn[:, c * CW:(c + 1) * CW]))
                link(dve.bn_aggr(sc[:, 21:23], st6[:, :]))
                dve.wait_ge(sm["sum_ps"], 3)
                dve.tensor_scalar(sc[:, 23:24], oP[:, 0:1], float(D) / (P * N), None, ALU.mult).then_inc(sm["sum_read"], 1)
                dve.wait_ge(sm["sum_read"], 3)
                link(dve.tensor_tensor(sc[:, 24:25], S1, S1, ALU.mult))
                dve.scalar_tensor_tensor(sc[:, 16:17], sc[:, 24:25], sc[:, 23:24], sc[:, 22:23], ALU.mult, ALU.add)\
                    .then_inc(sm["scales_set"], 1)
                dve.wait_ge(sm["scales_set"], 4)
                link(dve.scalar_tensor_tensor(T0, SIG, 1.2816, sc[:, 21:22], ALU.mult, ALU.add))
                t0, sig = T0.broadcast_to([P, NC]), SIG.broadcast_to([P, NC])
                dve.memset(S[:, :], 0.0).then_inc(sm["consts2"], 1)
                dve.tensor_scalar(X[:, 0, :], t0, 1.0, None, ALU.mult).then_inc(sm["consts2"], 1)
                dve.tensor_scalar(X[:, 2, :], t0, -1.0, None, ALU.mult).then_inc(sm["consts2"], 1)
                for j in range(2):
                    dve.scalar_tensor_tensor(Bk[:, j, 0, :], sig, -0.3, t0, ALU.mult, ALU.add).then_inc(sm["consts2"], 1)
                    dve.scalar_tensor_tensor(Bk[:, j, 2, :], sig, -0.3, t0, ALU.mult, ALU.subtract)\
                        .then_inc(sm["consts2"], 1)
                dve.memset(Bk[:, :, 1, :], -248.0).then_inc(sm["consts2"], 1)
                dve.memset(Bk[:, :, 3, :], -183.0).then_inc(sm["consts2"], 1)
                dve.wait_ge(sm["consts2"], 9)
                dve.memset(sel[:, 15:16], 0.0).then_inc(sm["search_set"], 1)

            def stats1(f, i):
                g = f * NT + i
                if f == 0:
                    dve.wait_ge(sm[f"x_in{i // 4}"], 16)
                elif i >= BT:
                    dve.wait_ge(sm["x_att"], i + 1)
                link(dve.bn_stats(st6[:, 0:6], x_sb[:, i, :]))
                if g >= 2:
                    dve.wait_ge(sm["rstd1"], g - 1)
                dve.bn_aggr(ln1[:, g % 2, 0:2], st6[:, 0:6]).then_inc(sm["stats1"], 1)

            def normal(f, i):
                g = f * NT + i
                dve.wait_ge(sm["stats1"], g + 1)
                dve.wait_ge(sm["rstd1"], g + 1)
                if g >= 2:
                    dve.wait_ge(sm["xT_ps"], g - 1)
                    dve.wait_ge(sm["xb_set"], g - 1)
                dve.tensor_scalar(xn[:, g % 2, :], x_sb[:, i, :], ln1[:, g % 2, 0:1], ln1[:, g % 2, 3:4],
                                  ALU.subtract, ALU.mult).then_inc(sm["xn_done"], 1)

            def x_lo(f, i):
                g = f * NT + i
                dve.wait_ge(sm["xT_hi"], g + 1)
                dve.scalar_tensor_tensor(xTlo[:, g % 2, :, :].rearrange("p k t -> p (k t)"), xP[:, :], XSCALE,
                                         xThi[:, g % 2, :, :].rearrange("p k t -> p (k t)"), ALU.mult,
                                         ALU.subtract).then_inc(sm["xT_lo"], 1)

            def h_lo(f, i, c):
                g = f * NT + i
                dve.wait_ge(sm["hT_hi"], 4 * g + c + 1)
                ks = slice(4 * c, 4 * c + 4)
                dve.scalar_tensor_tensor(hTlo[:, ks, :].rearrange("p k t -> p (k t)"), hP[:, c % 2, :], SH,
                                         hThi[:, ks, :].rearrange("p k t -> p (k t)"), ALU.mult,
                                         ALU.subtract).then_inc(sm["hT_lo"], 1)

            def update(f, s):
                u = updates(f, s)
                dve.wait_ge(sm["cnt"], counts_before(f, s))
                old, new = Bk[:, u % 2, :, :], Bk[:, (u + 1) % 2, :, :]
                w = NC - 1
                d = X[:, 3:4, 0:w].broadcast_to([P, 2, w])
                step(dve.tensor_scalar(X[:, 3, :], S[:, :], SSTAR, None, ALU.subtract))
                step(dve.tensor_scalar(X[:, 1, :], S[:, :], -1.0, SSTAR, ALU.mult, ALU.add))
                step(dve.tensor_copy(FIN[:, 4:5], old[:, 2, NC - 1:NC]))
                after(2)
                step(dve.tensor_scalar(G[:, 0:2, 0:w], d, 0.0, None, ALU.is_lt))
                step(dve.tensor_scalar(G[:, 2:4, 0:w], d, 0.0, None, ALU.is_ge))
                after(3)
                step(dve.tensor_copy(FIN[:, 0:4], X[:, :, NC - 1]))
                after(1)
                step(dve.scalar_tensor_tensor(Y4[:, :, 0:w], G[:, :, 0:w], -BIG, X[:, :, 0:w], ALU.mult, ALU.add))
                after(0)
                step(dve.tensor_tensor(new[:, :, 1:NC], old[:, :, 0:w], Y4[:, :, 0:w], ALU.max))
                after(0)
                step(dve.tensor_tensor(W2[:, :, 0:w], new[:, 0:2, 1:NC], new[:, 2:4, 1:NC], ALU.add))
                after(0)
                step(dve.reciprocal(E2[:, 0, 0:w], W2[:, 1, 0:w]))
                step(dve.tensor_tensor(E2[:, 1, 0:w], W2[:, 0, 0:w], new[:, 1, 1:NC], ALU.mult))
                after(0)
                step(dve.tensor_tensor(E2[:, 2, 0:w], E2[:, 1, 0:w], E2[:, 0, 0:w], ALU.mult))
                after(0)
                step(dve.tensor_tensor(X[:, 0, 1:NC], new[:, 0, 1:NC], E2[:, 2, 0:w], ALU.subtract))
                dve.tensor_tensor(X[:, 2, 1:NC], E2[:, 2, 0:w], new[:, 0, 1:NC], ALU.subtract).then_inc(sm["upd"], 1)

            TF, DF = FIN[:, 0:1], FIN[:, 3:4]
            TH, FND, IDX = sel[:, 0:1], sel[:, 1:2], sel[:, 2:3]
            OPEN, BOUND, ABOVE, HIT, TMP = (sel[:, j:j + 1] for j in range(3, 8))

            def below(f, i):
                g = f * NT + i
                link(dve.scalar_tensor_tensor(M[:, :], Z[:, g % ZR, :], TF, Z[:, g % ZR, :], ALU.is_le, ALU.mult))

            def pick(f, i):
                g = f * NT + i
                link(dve.tensor_scalar(IDX, DF, -0.5, TOPK - 1 - TARGET, ALU.mult, ALU.add))
                step(dve.tensor_scalar(e8[:, :], iota8[:, :], IDX, None, ALU.is_equal, ALU.add, accum_out=FND))
                link(dve.max(m8[:, :], M[:, :]))
                link(dve.scalar_tensor_tensor(e8[:, :], e8[:, :], 1.0, m8[:, :], ALU.mult, ALU.mult, accum_out=TH))
                if g:
                    dve.wait_ge(sm["ok_sum"], g)
                dve.scalar_tensor_tensor(okf[:, 0:1], m8[:, 0:1], TF, FND, ALU.is_lt, ALU.mult)\
                    .then_inc(sm["ok_set"], 1)

            def search_down(z):
                def step(ins):
                    dve.drain()
                    return ins

                def add_found(found, value):
                    step(dve.tensor_scalar(TMP, value, 0.0, None, ALU.max))
                    step(dve.scalar_tensor_tensor(TH, TMP, found, TH, ALU.mult, ALU.add))
                    step(dve.tensor_tensor(OPEN, OPEN, found, ALU.subtract))

                dve.drain()
                step(dve.tensor_scalar(OPEN, okf[:, 0:1], -1.0, 1.0, ALU.mult, ALU.add))
                step(dve.tensor_tensor(TH, TH, okf[:, 0:1], ALU.mult))
                step(dve.tensor_scalar(BOUND, FIN[:, 4:5], -1.0, None, ALU.mult))
                step(dve.tensor_scalar(M, z, BOUND, None, ALU.is_ge, ALU.add, accum_out=ABOVE))
                step(dve.tensor_scalar(HIT, ABOVE, float(TOPK), None, ALU.is_lt))
                step(dve.tensor_tensor(BOUND, BOUND, HIT, ALU.mult))
                step(dve.tensor_tensor(ABOVE, ABOVE, HIT, ALU.mult))
                step(dve.tensor_scalar(HIT, HIT, -3e38, 3e38, ALU.mult, ALU.add))
                step(dve.tensor_tensor(BOUND, BOUND, HIT, ALU.add))
                step(dve.memset(flags[:, :], 0.0))

                def still_open():
                    step(dve.tensor_copy(flags[:, 0:1], OPEN))
                    step(dve.transpose(flagsT[:, :], flags[:, :]))
                    step(dve.tensor_reduce(TMP, flagsT[:, :], AX.X, ALU.max))
                    step(dve.tensor_copy(flagi[:, :], TMP))
                    return sum(dve.value_load(flagi[q:q + 1, :], min_val=0, max_val=1) for q in range(0, P, 32))

                with dve.While(lambda: still_open() > 0):
                    step(dve.scalar_tensor_tensor(M, z, BOUND, z, ALU.is_lt, ALU.mult))
                    step(dve.max(m8[:, :], M))
                    step(dve.tensor_scalar(IDX, ABOVE, -1.0, TOPK - 1.0, ALU.mult, ALU.add))
                    step(dve.tensor_scalar(e8[:, :], iota8[:, :], IDX, None, ALU.is_equal, ALU.add, accum_out=HIT))
                    step(dve.scalar_tensor_tensor(e8[:, :], e8[:, :], 1.0, m8[:, :], ALU.mult, ALU.mult,
                                                  accum_out=BOUND))
                    step(dve.tensor_tensor(HIT, HIT, OPEN, ALU.mult))
                    add_found(HIT, BOUND)
                    step(dve.tensor_copy(BOUND, m8[:, 7:8]))
                    step(dve.tensor_scalar(M, z, BOUND, None, ALU.is_ge, ALU.add, accum_out=ABOVE))
                    step(dve.tensor_scalar(HIT, ABOVE, float(TOPK), None, ALU.is_ge))
                    step(dve.tensor_scalar(TMP, BOUND, 0.0, None, ALU.is_le))
                    step(dve.tensor_tensor(HIT, HIT, TMP, ALU.max))
                    step(dve.tensor_tensor(HIT, HIT, OPEN, ALU.mult))
                    add_found(HIT, BOUND)

            def keep_top(f, i):
                g = f * NT + i
                dve.wait_ge(sm["ok_sum"], g + 1)
                with dve.If(dve.value_load(oki[0:1, 0:1], min_val=0, max_val=P) < P):
                    search_down(Z[:, g % ZR, :])
                dve.scalar_tensor_tensor(Z[:, g % ZR, :], Z[:, g % ZR, :], TH, Z[:, g % ZR, :], ALU.is_ge, ALU.mult)\
                    .then_inc(sm["h_set"], 1)

            def residual(f, i):
                g = f * NT + i
                dve.wait_ge(sm["mm2"], 4 * g + 4)
                dve.wait_ge(sm["xb_set"], g + 1)
                dve.scalar_tensor_tensor(y[:, g % 2, :], oP[:, :], SC2, xb[:, g % XR, :], ALU.mult, ALU.add)\
                    .then_inc(sm["y_set"], 1)
                dve.wait_ge(sm["y_set"], g + 1)
                link(dve.bn_stats(st6[:, 6:12], y[:, g % 2, :]))
                dve.bn_aggr(ln2[:, g % 2, 0:2], st6[:, 6:12]).then_inc(sm["stats2"], 1)

            def normal2(f, i):
                g = f * NT + i
                dve.wait_ge(sm["stats2"], g + 1)
                dve.wait_ge(sm["rstd2"], g + 1)
                if g >= 2:
                    dve.wait_ge(sm["x_new"], g - 1)
                dve.tensor_scalar(yt[:, g % 2, :], y[:, g % 2, :], ln2[:, g % 2, 0:1], ln2[:, g % 2, 3:4],
                                  ALU.subtract, ALU.mult).then_inc(sm["yn_set"], 1)

            def normal_rows(b, i):
                def stats(i):
                    g = b * BT + i
                    raw = st6[:, 6 * (i % 2):6 * (i % 2) + 6]
                    if g:
                        dve.wait_ge(sm["a_stats"], g)
                    link(dve.bn_stats(raw, x_sb[:, g, :]))
                    if g >= 2:
                        dve.wait_ge(sm["a_rstd"], g - 1)
                        dve.wait_ge(sm["a_xn"], g - 1)
                    dve.bn_aggr(aln[:, g % 2, 0:2], raw).then_inc(sm["a_stats"], 1)

                g = b * BT + i
                if i == 0:
                    if b == 0:
                        dve.wait_ge(sm["cnt"], NC * NT)
                        dve.wait_ge(sm["x_new"], BT)
                    else:
                        dve.wait_ge(sm["mix_done"], TOTAL["mix"] * (GROUPS - 1) // GROUPS)
                    stats(0)
                if i + 1 < BT:
                    stats(i + 1)
                dve.wait_ge(sm["a_rstd"], g + 1)
                dve.wait_ge(sm["a_stats"], g + 1)
                if g >= 2:
                    dve.wait_ge(sm["a_turn"], g - 1)
                dve.tensor_scalar(axn[:, g % 2, :], x_sb[:, g, :], aln[:, g % 2, 0:1], aln[:, g % 2, 3:4],
                                  ALU.subtract, ALU.mult).then_inc(sm["a_xn"], 1)

            def project(b):
                for n in range(VALUES):
                    if not plane(ITEMS[n]):
                        continue
                    w, g, tc = plane(ITEMS[n])
                    if ITEMS[n] == ("in", 2, 0):
                        for m in range(4):
                            split_lo(b, m)
                    dve.wait_ge(sm["p_out"], b * len(ITEMS) + n + 1)
                    step(dve.tensor_reduce(mxq[:, g, w, tc:tc + 1], qk[:, w, g, tc * 512:(tc + 1) * 512],
                                           AX.X, ALU.max, apply_absolute_value=True))
                    if n in COMPLETE:
                        after(0)
                        dve.tensor_reduce(asc[:, g, 0:2], mxq[:, g, :, :], AX.X, ALU.max).then_inc(sm["p_max"], 1)
                        scale(b, g)

            def scale(b, g):
                dve.wait_ge(sm["q_max"], b * GROUPS + g + 1)
                link(dve.tensor_scalar(asc[:, g, 4:6].bitcast(I32), asc[:, g, 2:4].bitcast(I32), 0x7F800000, None,
                                       ALU.bitwise_and))
                link(dve.tensor_scalar(asc[:, g, 4:6], asc[:, g, 4:6], 0.5, None, ALU.max))
                link(dve.reciprocal(asc[:, g, 6:8], asc[:, g, 4:6]))
                link(dve.tensor_tensor(asc[:, g, 11:12], asc[:, g, 4:5], asc[:, g, 5:6], ALU.mult))
                link(dve.tensor_scalar(asc[:, g, 10:11], asc[:, g, 11:12], ATT_SCALE / 16384.0, None, ALU.mult))
                dve.tensor_scalar(asc[:, g, 8:10], asc[:, g, 6:8], 128.0, None, ALU.mult).then_inc(sm["q_scale"], 1)
                dve.wait_ge(sm["q_scale"], b * GROUPS + g + 1)

            def split_lo(b, m):
                k, w = SPLITS[m]
                dve.wait_ge(sm["split_hi"], 8 * b + m + 1)
                dve.scalar_tensor_tensor(parts[:, k, w, 1, :], qk[:, w, k, :], asc[:, k, 8 + w:9 + w],
                                         parts[:, k, w, 0, :], ALU.mult, ALU.subtract).then_inc(sm["split_lo"], 1)

            def core(b):
                n = {k: b * v for k, v in TOTAL.items()}
                ring = ring_steps(b)
                for e in ORDER:
                    kind, g = e[:2]
                    m = n[kind]
                    n[kind] += 1
                    if kind in ("row", "turn"):
                        bank, _ = next(ring)
                    if kind == "lo":
                        split_lo(b, g)
                    if kind == "row":
                        h, t, c = e[2:]
                        w = min(512, (t + 1) * P - 512 * c)
                        dve.wait_ge(sm["row_ps"], m + 1)
                        dve.tensor_reduce(mx[:, h, t, c:c + 1], rowP[bank][:, 0:w], AX.X, ALU.max)\
                            .then_inc(sm["row_max"], 1)
                    elif kind == "max":
                        dve.wait_ge(sm["row_max"], n["row"])
                        link(dve.tensor_reduce(mm_[:, :], mx[:, :, 4 * e[2]:4 * e[2] + 4, :], AX.X, ALU.max))
                        link(dve.tensor_scalar(mm_[:, :], mm_[:, :], -1.0 / MUNIT, None, ALU.mult))
                        if m:
                            dve.wait_ge(sm["mT_ps"], m)
                        mv = mm_[:, :].rearrange("p (h t) -> p t h", h=HG)
                        link(dve.tensor_copy(mrow[:, :, :, 0], mv))
                        dve.tensor_tensor(mrow[:, :, :, 1], mv, mrow[:, :, :, 0], ALU.subtract).then_inc(sm["m_set"], 1)
                    elif kind == "norm" and b == 0 and m == TOTAL["norm"] - 1:
                        for i in range(2):
                            normal_rows(1, i)
                    elif kind == "rec":
                        dve.wait_ge(sm["sum_out"], m // 4 + 1)
                        r = rec_of(m // 4 % TOTAL["norm"])[:, m % 4 * P:(m % 4 + 1) * P]
                        dve.reciprocal(r, r).then_inc(sm["rec_set"], 1)
                if b == 0:
                    for i in range(BT):
                        if i >= 2:
                            normal_rows(1, i)
                        x_att(b, i)

            def x_att(b, i):
                g = b * BT + i
                banks = out_banks(b)
                dve.wait_ge(sm["o_ps"], g + 1)
                dve.wait_ge(sm["bo_added"], g + 1)
                dve.tensor_tensor(x_sb[:, g, :], banks[i % len(banks)], x_sb[:, g, :], ALU.add)\
                    .then_inc(sm["x_att"], 1)

            scale_of(0, S1)
            dve.tensor_scalar(SC1, S1, 1.0 / XSCALE, None, ALU.mult).then_inc(sm["scales_set"], 1)
            for c in range(4):
                ternary(0, c)
            for f in range(NF):
                for s in slots:
                    if f == 0 and s == 1:
                        constants()
                    if f == 0 and 1 <= s < 5:
                        ternary(1, s - 1)
                    if FIRST_UPD <= s <= LAST_UPD:
                        update(f, s)
                    do(h_lo, f, s, S_OUT + 1, 3)
                    do(below, f, s, S_SEL)
                    do(h_lo, f, s, S_OUT, 0)
                    do(pick, f, s, S_SEL)
                    do(x_lo, f, s, 0)
                    do(h_lo, f, s, S_OUT, 1)
                    do(residual, f, s, S_FIN)
                    do(stats1, f, s, -1)
                    do(keep_top, f, s, S_SEL)
                    do(h_lo, f, s, S_OUT, 2)
                    do(normal, f, s, -1)
                    do(normal2, f, s, S_FIN)
                    for i in out_tiles(f, s):
                        x_att(1, i)
                if f == 0:
                    barrier(dve, 1)
                    for i in range(BT):
                        normal_rows(0, i)
                    link(dve.memset(mx[:, :, :, :], -BIG))
                    for b in range(2):
                        project(b)
                        core(b)
                        barrier(dve, 2 + b)


def kernel(**inputs):
    import numpy as np
    import concourse.bacc as bacc
    from concourse.bass_utils import run_bass_kernel_spmd

    nc = bacc.Bacc("TRN2", target_bir_lowering=False, num_devices=1)
    x = np.ascontiguousarray(inputs["L0_attn_x"]).reshape(TOKENS, D)
    arrays = {
        "x": x,
        "w_synT": np.ascontiguousarray(np.asarray(inputs["L0_ffn_W_syn"]).T),
        "b_syn": np.ascontiguousarray(inputs["L0_ffn_b_syn"]),
        "w_outT": np.ascontiguousarray(np.asarray(inputs["L0_ffn_W_out"]).T),
        "b_out": np.ascontiguousarray(inputs["L0_ffn_b_out"]),
        "gamma": np.ascontiguousarray(inputs["L0_ffn_gamma"]),
        "beta": np.ascontiguousarray(inputs["L0_ffn_beta"]),
    }
    for n in ("w_kv", "w_q", "w_kr", "w_ku", "w_qu", "w_qr", "w_vu", "w_o"):
        arrays[n] = np.ascontiguousarray(inputs["L0_attn_" + n])
    cols = [np.asarray(inputs["L0_attn_" + n]).reshape(-1, P) for n in ("b_kv", "b_q", "b_kr", "b_ku", "b_qu", "b_qr", "b_vu")]
    arrays["b_cols"] = np.ascontiguousarray(np.concatenate(cols).T)
    arrays["b_o"] = np.ascontiguousarray(inputs["L0_attn_b_o"])
    aps = [nc.dram_tensor("in_" + k, v.shape, F32, kind="ExternalInput").ap() for k, v in arrays.items()]
    o = nc.dram_tensor("out_dram", (TOKENS, D), F32, kind="ExternalOutput").ap()
    program(nc, *aps, o)
    r = run_bass_kernel_spmd(nc, [{"in_" + k: v for k, v in arrays.items()}], core_ids=[0])
    return r.results[0]["out_dram"].reshape(2, 1024, D)
```
